# Optimizing a Trainium2 kernel written in Bass

```python
import numpy as np
import jax
import jax.numpy as jnp

def _softmax(x, axis=-1):
    return jax.nn.softmax(x, axis=axis)

def _gelu(x):
    return jax.nn.gelu(x, approximate=True)

def _silu(x):
    return jax.nn.silu(x)

def _sigmoid(x):
    return jax.nn.sigmoid(x)

def _layernorm(x, axis=-1, eps=1e-05):
    m = jnp.mean(x, axis=axis, keepdims=True)
    v = jnp.var(x, axis=axis, keepdims=True)
    return (x - m) / jnp.sqrt(v + eps)

def _scatter_add(tgt, idx, src, axis=0):
    return tgt.at[idx].add(src)

def _segment_sum(src, seg, n):
    return jax.ops.segment_sum(src, seg, n)
kernel_name = 'mk_gnn_ffn_d2_gnn_r32_637e79'

def setup_inputs(seed: int=0):
    np.random.seed(seed)
    _w = jnp.asarray

    def _rec_inputs():
        import jax
        import jax.numpy as jnp
        _gk = jax.random.key(seed)
        x = -0.0003713 + 1 * jax.random.normal(jax.random.fold_in(_gk, 1), (3125, 256), jnp.float32)
        _s = jax.random.randint(jax.random.fold_in(_gk, 2), (25000,), 0, 3125, jnp.int32)
        _d = jax.random.randint(jax.random.fold_in(_gk, 3), (25000,), 0, 3125, jnp.int32)
        _loop = jnp.arange(3125, dtype=jnp.int32)
        src = jnp.concatenate([_s, _d, _loop])
        dst = jnp.concatenate([_d, _s, _loop])
        _o = jnp.argsort(dst, stable=True)
        src = src[_o]
        dst = dst[_o]
        return (x, src, dst)
    x, src, dst = _rec_inputs()

    def _L0_gnn_setup():
        import jax, jax.numpy as jnp
        import numpy as np
        N = 50000
        E = 25000
        HEADS = 4
        C = 64
        IN = 256
        NEG_SLOPE = 0.2

        def _gat_forward(x, edge_index, W, att_src, att_dst, bias):
            n = x.shape[0]
            h = (x @ W).reshape(n, HEADS, C)
            loop = jnp.arange(n, dtype=edge_index.dtype)
            src = jnp.concatenate([edge_index[0], loop])
            dst = jnp.concatenate([edge_index[1], loop])
            a_src = jnp.einsum('nhc,hc->nh', h, att_src)
            a_dst = jnp.einsum('nhc,hc->nh', h, att_dst)
            logits = a_src[src] + a_dst[dst]
            logits = jnp.where(logits >= 0, logits, NEG_SLOPE * logits)
            seg_max = jax.ops.segment_max(logits, dst, num_segments=n)
            seg_max = jnp.where(jnp.isfinite(seg_max), seg_max, 0.0)
            ex = jnp.exp(logits - seg_max[dst])
            denom = jax.ops.segment_sum(ex, dst, num_segments=n)
            alpha = ex / (denom[dst] + 1e-16)
            msgs = alpha[:, :, None] * h[src]
            out = jax.ops.segment_sum(msgs, dst, num_segments=n)
            out = out.reshape(n, HEADS * C) + bias
            return jax.nn.relu(out)
        key = jax.random.key(seed)
        k = jax.random.split(key, 6)
        x = jax.random.normal(k[0], (N, IN), dtype=jnp.float32)
        edge_index = jax.random.randint(k[1], (2, E), 0, N, dtype=jnp.int64)
        W = jax.random.normal(k[2], (IN, HEADS * C), dtype=jnp.float32) * (1.0 / np.sqrt(IN))
        att_src = jax.random.normal(k[3], (HEADS, C), dtype=jnp.float32) * (1.0 / np.sqrt(C))
        att_dst = jax.random.normal(k[4], (HEADS, C), dtype=jnp.float32) * (1.0 / np.sqrt(C))
        bias = jax.random.normal(k[5], (HEADS * C,), dtype=jnp.float32) * 0.02
        return {'x': x, 'edge_index': edge_index, 'W': W, 'att_src': att_src, 'att_dst': att_dst, 'bias': bias}
    _L0_gnn_all = _L0_gnn_setup()
    _L0_gnn_in = {k: v for k, v in _L0_gnn_all.items() if k in ('W', 'att_src', 'att_dst', 'bias')}
    del _L0_gnn_all

    def _L0_ffn_setup():
        import jax, jax.numpy as jnp
        import numpy as np
        B, N, D = (16, 128, 256)
        NUM_EXPERTS, TOP_K, HEADS = (4, 2, 4)
        N_EDGES = 32768
        LN_EPS = 1e-05

        def _layernorm(x, g, b):
            mu = x.mean(-1, keepdims=True)
            var = ((x - mu) ** 2).mean(-1, keepdims=True)
            return (x - mu) * jax.lax.rsqrt(var + LN_EPS) * g + b

        def _forward(x, edge_index, W_gat, att_src, att_dst, b_gat, ln_gamma, ln_beta, W1, b1, W2, b2):
            Bc, Nc, Dc = x.shape
            M = Bc * Nc
            x_flat = x.reshape(M, Dc)
            h = (x_flat @ W_gat).reshape(M, HEADS, NUM_EXPERTS)
            loops = jnp.arange(M, dtype=edge_index.dtype)
            src = jnp.concatenate([edge_index[0], loops])
            dst = jnp.concatenate([edge_index[1], loops])
            a_src = (h * att_src).sum(-1)
            a_dst = (h * att_dst).sum(-1)
            e = jax.nn.leaky_relu(a_src[src] + a_dst[dst], negative_slope=0.2)
            e_max = jax.ops.segment_max(e, dst, num_segments=M)
            ee = jnp.exp(e - e_max[dst])
            denom = jax.ops.segment_sum(ee, dst, num_segments=M)
            alpha = ee / (denom[dst] + 1e-16)
            msg = h[src] * alpha[:, :, None]
            agg = jax.ops.segment_sum(msg, dst, num_segments=M).reshape(M, HEADS * NUM_EXPERTS) + b_gat
            scores = _layernorm(agg, ln_gamma, ln_beta).reshape(M, HEADS, NUM_EXPERTS).mean(1)
            scores = scores.reshape(Bc, Nc, NUM_EXPERTS)
            topk_s, topk_i = jax.lax.top_k(scores, TOP_K)
            w = jax.nn.softmax(topk_s, axis=-1)
            out = jnp.zeros_like(x)
            for ei in range(NUM_EXPERTS):
                g = jnp.where(topk_i == ei, w, 0.0).sum(-1)
                hh = jax.nn.gelu(x @ W1[ei] + b1[ei], approximate=False)
                out = out + g[..., None] * (hh @ W2[ei] + b2[ei])
            return out
        key = jax.random.key(seed)
        ks = jax.random.split(key, 8)
        s = 0.05
        return {'x': jax.random.normal(ks[0], (B, N, D), jnp.float32), 'W_gat': jax.random.normal(ks[1], (D, HEADS * NUM_EXPERTS), jnp.float32) * s, 'att_src': jax.random.normal(ks[2], (HEADS, NUM_EXPERTS), jnp.float32) * s, 'att_dst': jax.random.normal(ks[3], (HEADS, NUM_EXPERTS), jnp.float32) * s, 'b_gat': jnp.zeros((HEADS * NUM_EXPERTS,), jnp.float32), 'ln_gamma': jnp.ones((HEADS * NUM_EXPERTS,), jnp.float32), 'ln_beta': jnp.zeros((HEADS * NUM_EXPERTS,), jnp.float32), 'W1': jax.random.normal(ks[4], (NUM_EXPERTS, D, 2 * D), jnp.float32) * s, 'b1': jnp.zeros((NUM_EXPERTS, 2 * D), jnp.float32), 'W2': jax.random.normal(ks[5], (NUM_EXPERTS, 2 * D, D), jnp.float32) * s, 'b2': jnp.zeros((NUM_EXPERTS, D), jnp.float32), 'edge_index': jax.random.randint(ks[6], (2, N_EDGES), 0, B * N, jnp.int32)}
    _L0_ffn_all = _L0_ffn_setup()
    _L0_ffn_in = {k: v for k, v in _L0_ffn_all.items() if k in ('W_gat', 'att_src', 'att_dst', 'b_gat', 'ln_gamma', 'ln_beta', 'W1', 'b1', 'W2', 'b2', 'edge_index')}
    del _L0_ffn_all

    def _L1_gnn_setup():
        import jax, jax.numpy as jnp
        import numpy as np
        N_NODES = 50000
        N_EDGES = 25000
        IN_CH = 256
        HID_CH = 256
        OUT_CH = 256
        N_LAYERS = 3
        key = jax.random.key(seed)
        ks = jax.random.split(key, 8)
        s_in = 1.0 / np.sqrt(IN_CH)
        s_h = 1.0 / np.sqrt(HID_CH)
        return {'x': jax.random.normal(ks[0], (N_NODES, IN_CH), dtype=jnp.float32), 'W_in': jax.random.normal(ks[1], (IN_CH, HID_CH), dtype=jnp.float32) * s_in, 'b_in': jnp.zeros((HID_CH,), dtype=jnp.float32), 'W_agg': jax.random.normal(ks[2], (N_LAYERS, HID_CH, HID_CH), dtype=jnp.float32) * s_h, 'W_self': jax.random.normal(ks[3], (N_LAYERS, HID_CH, HID_CH), dtype=jnp.float32) * s_h, 'b_hid': jnp.zeros((N_LAYERS, HID_CH), dtype=jnp.float32), 'W_out': jax.random.normal(ks[4], (HID_CH, OUT_CH), dtype=jnp.float32) * s_h, 'b_out': jnp.zeros((OUT_CH,), dtype=jnp.float32), 'edge_index': jax.random.randint(ks[5], (2, N_EDGES), 0, N_NODES, dtype=jnp.int64)}
    _L1_gnn_all = _L1_gnn_setup()
    _L1_gnn_in = {k: v for k, v in _L1_gnn_all.items() if k in ('W_in', 'b_in', 'W_agg', 'W_self', 'b_hid', 'W_out', 'b_out')}
    del _L1_gnn_all

    def _L1_ffn_setup():
        import jax, jax.numpy as jnp
        import numpy as np
        NUM_EXPERTS = 8
        TOP_K = 2
        B, S, D = (8, 256, 256)

        def _moe(tokens, router_w, w1, b1, w2, b2):
            N = tokens.shape[0]
            E = router_w.shape[0]
            logits = tokens.astype(jnp.float32) @ router_w.astype(jnp.float32).T
            probs = jax.nn.softmax(logits, axis=-1)
            rw, re = jax.lax.top_k(probs, TOP_K)
            if TOP_K > 1:
                rw = rw / jnp.maximum(rw.sum(-1, keepdims=True), 1e-12)
            rw = rw.astype(tokens.dtype)
            combine = jnp.zeros((N, E), tokens.dtype).at[jnp.arange(N)[:, None], re].set(rw)
            out = tokens
            for e in range(E):
                h = jax.nn.gelu(tokens @ w1[e] + b1[e], approximate=False)
                y = h @ w2[e] + b2[e]
                out = out + combine[:, e:e + 1] * y
            return out
        key = jax.random.key(seed)
        ks = jax.random.split(key, 4)
        scale = 1.0 / np.sqrt(D).astype(np.float32)
        return {'input_embeddings': jax.random.normal(ks[0], (B, S, D), jnp.float32), 'router_w': jax.random.normal(ks[1], (NUM_EXPERTS, D), jnp.float32) * scale, 'w1': jax.random.normal(ks[2], (NUM_EXPERTS, D, D), jnp.float32) * scale, 'b1': jnp.zeros((NUM_EXPERTS, D), jnp.float32), 'w2': jax.random.normal(ks[3], (NUM_EXPERTS, D, D), jnp.float32) * scale, 'b2': jnp.zeros((NUM_EXPERTS, D), jnp.float32)}
    _L1_ffn_all = _L1_ffn_setup()
    _L1_ffn_in = {k: v for k, v in _L1_ffn_all.items() if k in ('router_w', 'w1', 'b1', 'w2', 'b2')}
    del _L1_ffn_all
    return {'x': x, 'src': src, 'dst': dst, 'L0_gnn_W': _L0_gnn_in['W'], 'L0_gnn_att_src': _L0_gnn_in['att_src'], 'L0_gnn_att_dst': _L0_gnn_in['att_dst'], 'L0_gnn_bias': _L0_gnn_in['bias'], 'L0_ffn_W_gat': _L0_ffn_in['W_gat'], 'L0_ffn_att_src': _L0_ffn_in['att_src'], 'L0_ffn_att_dst': _L0_ffn_in['att_dst'], 'L0_ffn_b_gat': _L0_ffn_in['b_gat'], 'L0_ffn_ln_gamma': _L0_ffn_in['ln_gamma'], 'L0_ffn_ln_beta': _L0_ffn_in['ln_beta'], 'L0_ffn_W1': _L0_ffn_in['W1'], 'L0_ffn_b1': _L0_ffn_in['b1'], 'L0_ffn_W2': _L0_ffn_in['W2'], 'L0_ffn_b2': _L0_ffn_in['b2'], 'L0_ffn_edge_index': _L0_ffn_in['edge_index'], 'L1_gnn_W_in': _L1_gnn_in['W_in'], 'L1_gnn_b_in': _L1_gnn_in['b_in'], 'L1_gnn_W_agg': _L1_gnn_in['W_agg'], 'L1_gnn_W_self': _L1_gnn_in['W_self'], 'L1_gnn_b_hid': _L1_gnn_in['b_hid'], 'L1_gnn_W_out': _L1_gnn_in['W_out'], 'L1_gnn_b_out': _L1_gnn_in['b_out'], 'L1_ffn_router_w': _L1_ffn_in['router_w'], 'L1_ffn_w1': _L1_ffn_in['w1'], 'L1_ffn_b1': _L1_ffn_in['b1'], 'L1_ffn_w2': _L1_ffn_in['w2'], 'L1_ffn_b2': _L1_ffn_in['b2']}

def reference(x, src, dst, L0_gnn_W, L0_gnn_att_src, L0_gnn_att_dst, L0_gnn_bias, L0_ffn_W_gat, L0_ffn_att_src, L0_ffn_att_dst, L0_ffn_b_gat, L0_ffn_ln_gamma, L0_ffn_ln_beta, L0_ffn_W1, L0_ffn_b1, L0_ffn_W2, L0_ffn_b2, L0_ffn_edge_index, L1_gnn_W_in, L1_gnn_b_in, L1_gnn_W_agg, L1_gnn_W_self, L1_gnn_b_hid, L1_gnn_W_out, L1_gnn_b_out, L1_ffn_router_w, L1_ffn_w1, L1_ffn_b1, L1_ffn_w2, L1_ffn_b2):
    import jax
    import jax.numpy as jnp

    def _L0_gnn_ref(x, edge_index, W, att_src, att_dst, bias):
        import jax, jax.numpy as jnp
        import numpy as np
        N = 50000
        E = 25000
        HEADS = 4
        C = 64
        IN = 256
        NEG_SLOPE = 0.2

        def _gat_forward(x, edge_index, W, att_src, att_dst, bias):
            n = x.shape[0]
            h = (x @ W).reshape(n, HEADS, C)
            loop = jnp.arange(n, dtype=edge_index.dtype)
            src = jnp.concatenate([edge_index[0], loop])
            dst = jnp.concatenate([edge_index[1], loop])
            a_src = jnp.einsum('nhc,hc->nh', h, att_src)
            a_dst = jnp.einsum('nhc,hc->nh', h, att_dst)
            logits = a_src[src] + a_dst[dst]
            logits = jnp.where(logits >= 0, logits, NEG_SLOPE * logits)
            seg_max = jax.ops.segment_max(logits, dst, num_segments=n)
            seg_max = jnp.where(jnp.isfinite(seg_max), seg_max, 0.0)
            ex = jnp.exp(logits - seg_max[dst])
            denom = jax.ops.segment_sum(ex, dst, num_segments=n)
            alpha = ex / (denom[dst] + 1e-16)
            msgs = alpha[:, :, None] * h[src]
            out = jax.ops.segment_sum(msgs, dst, num_segments=n)
            out = out.reshape(n, HEADS * C) + bias
            return jax.nn.relu(out)
        return _gat_forward(x, edge_index, W, att_src, att_dst, bias)

    def _L0_ffn_ref(x, W_gat, att_src, att_dst, b_gat, ln_gamma, ln_beta, W1, b1, W2, b2, edge_index):
        import jax, jax.numpy as jnp
        import numpy as np
        B, N, D = (16, 128, 256)
        NUM_EXPERTS, TOP_K, HEADS = (4, 2, 4)
        N_EDGES = 32768
        LN_EPS = 1e-05

        def _layernorm(x, g, b):
            mu = x.mean(-1, keepdims=True)
            var = ((x - mu) ** 2).mean(-1, keepdims=True)
            return (x - mu) * jax.lax.rsqrt(var + LN_EPS) * g + b

        def _forward(x, edge_index, W_gat, att_src, att_dst, b_gat, ln_gamma, ln_beta, W1, b1, W2, b2):
            Bc, Nc, Dc = x.shape
            M = Bc * Nc
            x_flat = x.reshape(M, Dc)
            h = (x_flat @ W_gat).reshape(M, HEADS, NUM_EXPERTS)
            loops = jnp.arange(M, dtype=edge_index.dtype)
            src = jnp.concatenate([edge_index[0], loops])
            dst = jnp.concatenate([edge_index[1], loops])
            a_src = (h * att_src).sum(-1)
            a_dst = (h * att_dst).sum(-1)
            e = jax.nn.leaky_relu(a_src[src] + a_dst[dst], negative_slope=0.2)
            e_max = jax.ops.segment_max(e, dst, num_segments=M)
            ee = jnp.exp(e - e_max[dst])
            denom = jax.ops.segment_sum(ee, dst, num_segments=M)
            alpha = ee / (denom[dst] + 1e-16)
            msg = h[src] * alpha[:, :, None]
            agg = jax.ops.segment_sum(msg, dst, num_segments=M).reshape(M, HEADS * NUM_EXPERTS) + b_gat
            scores = _layernorm(agg, ln_gamma, ln_beta).reshape(M, HEADS, NUM_EXPERTS).mean(1)
            scores = scores.reshape(Bc, Nc, NUM_EXPERTS)
            topk_s, topk_i = jax.lax.top_k(scores, TOP_K)
            w = jax.nn.softmax(topk_s, axis=-1)
            out = jnp.zeros_like(x)
            for ei in range(NUM_EXPERTS):
                g = jnp.where(topk_i == ei, w, 0.0).sum(-1)
                hh = jax.nn.gelu(x @ W1[ei] + b1[ei], approximate=False)
                out = out + g[..., None] * (hh @ W2[ei] + b2[ei])
            return out
        return _forward(x, edge_index, W_gat, att_src, att_dst, b_gat, ln_gamma, ln_beta, W1, b1, W2, b2)

    def _L1_gnn_ref(x, W_in, b_in, W_agg, W_self, b_hid, W_out, b_out, edge_index):
        import jax, jax.numpy as jnp
        import numpy as np
        N_NODES = 50000
        N_EDGES = 25000
        IN_CH = 256
        HID_CH = 256
        OUT_CH = 256
        N_LAYERS = 3
        n = x.shape[0]
        dst = edge_index[0]
        src = edge_index[1]
        n_layers = W_agg.shape[0]
        h = x @ W_in + b_in
        deg = jax.ops.segment_sum(jnp.ones_like(dst, dtype=h.dtype), dst, num_segments=n)
        deg = jnp.maximum(deg, 1.0)[:, None]
        for l in range(n_layers):
            agg = jax.ops.segment_sum(h[src], dst, num_segments=n) / deg
            h = jax.nn.relu(agg @ W_agg[l] + h @ W_self[l] + b_hid[l])
        return h @ W_out + b_out

    def _L1_ffn_ref(input_embeddings, router_w, w1, b1, w2, b2):
        import jax, jax.numpy as jnp
        import numpy as np
        NUM_EXPERTS = 8
        TOP_K = 2
        B, S, D = (8, 256, 256)

        def _moe(tokens, router_w, w1, b1, w2, b2):
            N = tokens.shape[0]
            E = router_w.shape[0]
            logits = tokens.astype(jnp.float32) @ router_w.astype(jnp.float32).T
            probs = jax.nn.softmax(logits, axis=-1)
            rw, re = jax.lax.top_k(probs, TOP_K)
            if TOP_K > 1:
                rw = rw / jnp.maximum(rw.sum(-1, keepdims=True), 1e-12)
            rw = rw.astype(tokens.dtype)
            combine = jnp.zeros((N, E), tokens.dtype).at[jnp.arange(N)[:, None], re].set(rw)
            out = tokens
            for e in range(E):
                h = jax.nn.gelu(tokens @ w1[e] + b1[e], approximate=False)
                y = h @ w2[e] + b2[e]
                out = out + combine[:, e:e + 1] * y
            return out
        b, s, d = input_embeddings.shape
        tokens = input_embeddings.reshape(b * s, d)
        return _moe(tokens, router_w, w1, b1, w2, b2).reshape(b, s, d)
    edge_index = jnp.stack([src, dst])
    x = x + _L0_gnn_ref(_layernorm(x, axis=-1), edge_index, L0_gnn_W, L0_gnn_att_src, L0_gnn_att_dst, L0_gnn_bias)
    x = x + _L0_ffn_ref(_layernorm(x, axis=-1)[None], L0_ffn_W_gat, L0_ffn_att_src, L0_ffn_att_dst, L0_ffn_b_gat, L0_ffn_ln_gamma, L0_ffn_ln_beta, L0_ffn_W1, L0_ffn_b1, L0_ffn_W2, L0_ffn_b2, L0_ffn_edge_index)[0]
    x = x + _L1_gnn_ref(_layernorm(x, axis=-1), L1_gnn_W_in, L1_gnn_b_in, L1_gnn_W_agg, L1_gnn_W_self, L1_gnn_b_hid, L1_gnn_W_out, L1_gnn_b_out, edge_index)
    x = x + _L1_ffn_ref(_layernorm(x, axis=-1)[None], L1_ffn_router_w, L1_ffn_w1, L1_ffn_b1, L1_ffn_w2, L1_ffn_b2)[0]
    return x

_drawn_inputs = setup_inputs


def setup_inputs(seed=0):
    import zlib

    import numpy as np

    out = dict(_drawn_inputs(seed))
    spreads = {'L0_ffn_b_gat': (0.0, 0.1),
     'L0_ffn_ln_gamma': (1.0, 0.2),
     'L0_ffn_ln_beta': (0.0, 0.1),
     'L0_ffn_b1': (0.0, 0.1),
     'L0_ffn_b2': (0.0, 0.1),
     'L1_gnn_b_in': (0.0, 0.1),
     'L1_gnn_b_hid': (0.0, 0.1),
     'L1_gnn_b_out': (0.0, 0.1),
     'L1_ffn_b1': (0.0, 0.355),
     'L1_ffn_b2': (0.0, 0.1)}
    factors = {}
    for name, (base, spread) in spreads.items():
        noise = np.random.default_rng([zlib.crc32(name.encode()), seed]).standard_normal(out[name].shape)
        drawn = base * np.exp(spread * noise) if base else spread * noise
        out[name] = jnp.asarray(drawn.astype(out[name].dtype))
    for name, factor in factors.items():
        out[name] = (out[name] * factor).astype(out[name].dtype)
    return out
```

```python
import numpy as np
import concourse.bass as bass
from concourse import mybir
from contextlib import ExitStack, contextmanager

FP32 = mybir.dt.float32
I32 = mybir.dt.int32
ALU = mybir.AluOpType
ACT = mybir.ActivationFunctionType
AX = mybir.AxisListType.X
RMAX = bass.bass_isa.ReduceOp.max

N, D = 3125, 256
P, T = 125, 25
G, J = 5, 5
HEADS = 4
E1 = 53125
C1 = 416
Q = 4
B1 = C1 // Q
C1P = C1 + Q
E2 = 32768
C2 = E2 // 128
B2 = C2 // Q
C2P = C2 + Q
PAD = N
CW = 450
NG = 7
CC = CW * NG
CELLS = (N + 1) * CC
ROWS = N + 1
KQ = 5
MSG = 260
TAB = 264
TRASH_MARK = 1024.0


class Chain:

    def __init__(self, eng, sem):
        self.eng, self.sem, self.base, self.k = eng, sem, 0, 0

    def __call__(self, ins):
        ins.then_inc(self.sem, 1)
        self.k += 1
        self.eng.wait_ge(self.sem, self.base + self.k)

    @contextmanager
    def loop(self, turns, per):
        base, k = self.base, self.k
        with self.eng.Fori(0, turns) as i:
            self.base, self.k = base + (i * per + k), 0
            yield i
            assert self.k == per, (self.k, per)
        self.base, self.k = base, k + turns * per


def build_model(nc, x, src, dst, gat_W, gat_as, gat_ad, gat_b, rt_W, rt_as, rt_ad, rt_b, rt_gamma, rt_beta,
                f0_W1, f0_b1, f0_W2, f0_b2, rt_edges, gn_Win, gn_bin, gn_Wagg, gn_Wself, gn_bhid, gn_Wout,
                gn_bout, f1_router, f1_W1, f1_b1, f1_W2, f1_b2, out):
    ctx = ExitStack()
    with ctx:
        def sb(name, shape, dt=FP32):
            return ctx.enter_context(nc.sbuf_tensor(name, shape, dt))

        def sem(name):
            return ctx.enter_context(nc.semaphore(name))

        counts = nc.dram_tensor("counts", [CELLS + 128, 1], FP32).ap()
        sums = nc.dram_tensor("sums", [ROWS + 128, MSG], FP32).ap()
        tab_src = nc.dram_tensor("tab_src", [ROWS, TAB], FP32).ap()
        tab_dst = nc.dram_tensor("tab_dst", [ROWS, 8], FP32).ap()
        rt_src = nc.dram_tensor("rt_src", [N, 24], FP32).ap()
        rt_dst = nc.dram_tensor("rt_dst", [N, 8], FP32).ap()

        X = sb("X", [P, T, D])
        BIG1 = sb("BIG1", [128, T * TAB])
        BIG2 = sb("BIG2", [128, KQ * KQ * CW])
        XT = sb("XT", [128, 2, CC])
        FW = sb("FW", [128, 8192])
        RD = sb("RD", [128, CC])
        xn_s = sb("xn_s", [P, J, D])
        xT_s = sb("xT_s", [128, 2, 2, P])
        Wg = sb("Wg", [128, 2, D])
        W16 = sb("W16", [128, 2, 16])
        Wr = sb("Wr", [128, 2, 8])
        Win = FW[:, 0:512].rearrange("p (k n) -> p k n", k=2)
        Wout = FW[:, 512:1024].rearrange("p (k n) -> p k n", k=2)
        Wagg = FW[:, 1024:2560].rearrange("p (l k n) -> p l k n", l=3, k=2)
        Wself = FW[:, 2560:4096].rearrange("p (l k n) -> p l k n", l=3, k=2)
        scr_g = sb("scr_g", [128, 2, CW])
        Wcur = sb("Wcur", [128, 2, D])
        row_as = sb("row_as", [P, D])
        row_ad = sb("row_ad", [P, D])
        row_b = sb("row_b", [P, D])
        row16 = sb("row16", [P, 5, 16])
        b2_bc = BIG1[0:P, 4500:4500 + 8 * D].rearrange("p (e n) -> p e n", e=8)
        b1_T = sb("b1_T", [128, 16])
        bin_T = sb("bin_T", [128, 2])
        bhid_T = sb("bhid_T", [128, 3, 2])
        ident = sb("ident", [128, 128])
        ones = sb("ones", [128, 128])
        lower = sb("lower", [128, 128])
        dupw = sb("dupw", [128, 128])
        tie = sb("tie", [128, 8, 8])
        iota_i = sb("iota_i", [128, P], I32)
        iota_f = sb("iota_f", [128, P])
        pidx_i = sb("pidx_i", [128, 2], I32)
        pidx_f = sb("pidx_f", [128, 2])
        stats = sb("stats", [P, T, 6])
        ln = sb("ln", [P, 8, T])
        small = sb("small", [P, 10, T, HEADS])
        amax = sb("amax", [P, 2, HEADS])
        s16 = sb("s16", [P, 3, T, 16])
        tab2 = sb("tab2", [P, T, 24])
        uv = sb("uv", [P, T, 8])
        gates = sb("gates", [P, T, 8])
        e_src2 = sb("e_src2", [128, C2P], I32)
        e_dst2 = sb("e_dst2", [128, C2P], I32)
        xt_flat = XT[:, :, :].rearrange("p k n -> p (k n)")

        def column(k, dt=FP32):
            part = xt_flat[:, k * C1P:(k + 1) * C1P]
            return part if dt == FP32 else part.bitcast(dt)

        e_src, e_dst = column(0, I32), column(1, I32)
        src_f, dst_f, key_f, off_row, off_cell = (column(k) for k in range(2, 7))
        tab = BIG1[0:P, 0:T * TAB].rearrange("p (t c) -> p t c", c=TAB)
        tab_h = tab[:, :, 0:MSG].rearrange("p t (h c) -> p t h c", c=65)
        hid1 = BIG1[0:P, 0:T * D].rearrange("p (t c) -> p t c", c=D)
        hrow = BIG1[0:P, 0:T * D].rearrange("p (t h c) -> p t h c", h=HEADS, c=64)

        def carve(big, at, shape):
            size = int(np.prod(shape))
            names = "abcd"[:len(shape)]
            view = big[:, at:at + size].rearrange(
                f"p ({' '.join(names)}) -> p {' '.join(names)}", **dict(zip(names, shape)))
            return view, at + size

        at = 0
        gath, at = carve(BIG2, at, [2, Q, TAB])
        gathd, at = carve(BIG2, at, [2, Q, 8])
        same, at = carve(BIG2, at, [2, Q, 128])
        msg, at = carve(BIG2, at, [2, Q, MSG])
        msum, at = carve(BIG2, at, [2, Q, MSG])
        samek, at = carve(BIG2, at, [Q, 128])
        scr, at = carve(BIG2, at, [Q, 128])
        diag, at = carve(BIG2, at, [2, Q, 128])
        assert at <= KQ * KQ * CW
        slot_i = sb("slot_i", [128, 2, 4, Q], I32)
        slot_f = sb("slot_f", [128, 2, 6, Q])
        wgt = sb("wgt", [128, 2, Q, HEADS])
        sums_sb = BIG2[0:P, 0:T * MSG].rearrange("p (t h c) -> p t h c", h=HEADS, c=65)
        at = 0
        gath2, at = carve(BIG1, at, [2, Q, 24])
        gathd2, at = carve(BIG1, at, [2, Q, 8])
        onep, at = carve(BIG1, at, [2, Q, P])
        onet, at = carve(BIG1, at, [Q, T])
        msg2, at = carve(BIG1, at, [Q, 20])
        spread, at = carve(BIG1, at, [2, Q, T, 20])
        pd, at = carve(BIG1, at, [C2P])
        td, at = carve(BIG1, at, [C2P])
        dd, at = carve(BIG1, at, [C2P])
        halves, at = carve(BIG1, at, [C2P])
        e_half = halves.bitcast(I32)
        assert at <= T * TAB
        rank_a = BIG1[0:P, 0:T * 64]
        rank_b = BIG1[0:P, T * 64:2 * T * 64]
        piece = [BIG2[0:P, k * KQ * CW:(k + 1) * KQ * CW].rearrange("p (k n) -> p k n", n=CW) for k in range(KQ)]
        hh, _ = carve(BIG2, 0, [2, 4, J * P])
        zrow = RD[:, :]

        bank = [ctx.enter_context(nc.psum_tensor(f"bank{k}", [128, 512], FP32)) for k in range(8)]

        ld_x = sem("ld_x")
        ld_gat = sem("ld_gat")
        ld_edges = sem("ld_edges")
        ld_rt = sem("ld_rt")
        ld_gn = sem("ld_gn")
        ld_f0 = sem("ld_f0")
        ld_f1 = sem("ld_f1")
        ld_f1b = sem("ld_f1b")
        ld_b2 = sem("ld_b2")
        z_mem = sem("z_mem")
        z_done = sem("z_done")
        consts = sem("consts")
        consts2 = sem("consts2")
        idx_mem = sem("idx_mem")
        idx_dve = sem("idx_dve")
        dve_chain = sem("dve_chain")
        act_chain = sem("act_chain")
        ln_var = sem("ln_var")
        ln_std = sem("ln_std")
        S = [{k: sem(f"{k}_{i}") for k in ("xn", "tr", "xT", "h", "hev")} for i in range(4)]
        mx = sem("mx")
        mxr = sem("mxr")
        f_in = sem("f_in")
        f_out = sem("f_out")
        tab_rdy = sem("tab_rdy")
        tab_st = sem("tab_st")
        gidx = sem("gidx")
        gat_s = [sem(f"gathered{s}") for s in range(2)]
        diag_rdy = sem("diag_rdy")
        bc_rdy = sem("bc_rdy")
        prep = sem("prep")
        msg_rdy = sem("msg_rdy")
        agg_rdy = sem("agg_rdy")
        msum_rdy = sem("msum_rdy")
        row_sc = sem("row_sc")
        cell_sc = sem("cell_sc")
        sc_done = sem("sc_done")
        ld_sums = sem("ld_sums")
        sums_free = sem("sums_free")
        rt_tab_rdy = sem("rt_tab_rdy")
        rt_tab_st = sem("rt_tab_st")
        gidx2 = sem("gidx2")
        gat2_s = [sem(f"gathered2_{s}") for s in range(2)]
        spread_rdy = sem("spread_rdy")
        spread_used = sem("spread_used")
        rt_agg = sem("rt_agg")
        pc_ld = [sem(f"pc_ld{k}") for k in range(KQ)]
        pc_free = sem("pc_free")
        deg_ev = sem("deg_ev")
        rd_done = sem("rd_done")
        EX = [{k: sem(f"{k}_e{i}") for k in ("up", "act", "dn", "acc")} for i in range(2)]
        gate_rdy = sem("gate_rdy")
        gate1_rdy = sem("gate1_rdy")
        f0_done = sem("f0_done")
        in_mm = sem("in_mm")
        in_ev = sem("in_ev")
        z_mm = sem("z_mm")
        z_ev = sem("z_ev")
        wcur = sem("wcur")
        gn_mm = sem("gn_mm")
        gn_sum = sem("gn_sum")
        gn_rel = sem("gn_rel")
        o_mm = sem("o_mm")
        o_acc = sem("o_acc")
        all_done = sem("all_done")
        stored = sem("stored")
        pool_steps = sem("pool_steps")
        pe_steps = sem("pe_steps")

        LD_GN = 16 * (2 + 6 + 3)
        LD_F1 = 16 * (8 + 2)
        LD_F0 = 16 * 10

        block = ctx.enter_context(nc.Block())

        def free(n, j):
            return n + (2 if j == 0 else 1)

        @block.sync
        def _(sp):
            sp.dma_start(X[:, :, :], x.rearrange("(p t) d -> p t d", t=T)).then_inc(ld_x, 16)
            sp.wait_ge(idx_mem, 2)
            for e, a in ((e_src, src), (e_dst, dst)):
                sp.dma_start(e[0:127, 0:C1], a[0:127 * C1].rearrange("(p c) -> p c", c=C1)).then_inc(ld_edges, 16)
                sp.dma_start(e[127:128, 0:E1 - 127 * C1], a[127 * C1:E1].rearrange("(o c) -> o c", o=1)).then_inc(ld_edges, 16)
            wk = "(k p) n -> p k n"
            sp.dma_start(Wg[:, :, :], gat_W.rearrange(wk, p=128)).then_inc(ld_gat, 16)
            sp.dma_start(row_as[:, :], gat_as.rearrange("h c -> (h c)").partition_broadcast(P)).then_inc(ld_gat, 16)
            sp.dma_start(row_ad[:, :], gat_ad.rearrange("h c -> (h c)").partition_broadcast(P)).then_inc(ld_gat, 16)
            sp.dma_start(row_b[:, :], gat_b.partition_broadcast(P)).then_inc(ld_gat, 16)
            sp.wait_ge(z_mem, 1)
            cv = counts[0:N * CC, 0].rearrange("(p t n) -> p t n", t=T, n=CC)
            for t in range(T):
                sp.dma_start(cv[:, t, :], zrow[0:P, :]).then_inc(z_done, 16)
            sp.dma_start(counts[N * CC:N * CC + CC + 128, 0].rearrange("(o n) -> o n", n=149), zrow[0:22, 0:149]).then_inc(z_done, 16)
            sv = sums[0:N, :].rearrange("(p t) c -> p (t c)", t=T)
            for a in range(0, T * MSG, CC):
                b = min(a + CC, T * MSG)
                sp.dma_start(sv[:, a:b], zrow[0:P, 0:b - a]).then_inc(z_done, 16)
            sp.dma_start(sums[N:N + 129, :].rearrange("(a b) c -> a (b c)", b=3), zrow[0:43, 0:3 * MSG]).then_inc(z_done, 16)
            sp.dma_start(tab_src[N:N + 1, :], zrow[0:1, 0:TAB]).then_inc(z_done, 16)
            sp.dma_start(tab_dst[N:N + 1, :], zrow[0:1, 0:8]).then_inc(z_done, 16)
            sp.dma_start(e_src2[:, 0:C2], rt_edges[0, :].rearrange("(p c) -> p c", c=C2)).then_inc(ld_rt, 16)
            sp.dma_start(e_dst2[:, 0:C2], rt_edges[1, :].rearrange("(p c) -> p c", c=C2)).then_inc(ld_rt, 16)
            sp.dma_start(W16[:, :, :], rt_W.rearrange(wk, p=128)).then_inc(ld_rt, 16)
            for k, a in enumerate((rt_as, rt_ad)):
                sp.dma_start(row16[:, k, :], a.rearrange("h c -> (h c)").partition_broadcast(P)).then_inc(ld_rt, 16)
            for k, a in enumerate((rt_b, rt_gamma, rt_beta)):
                sp.dma_start(row16[:, 2 + k, :], a.partition_broadcast(P)).then_inc(ld_rt, 16)
            f0w1 = FW[:, 0:4096].rearrange("p (e k n) -> p e k n", e=4, k=2)
            f0w2 = FW[:, 4096:8192].rearrange("p (e k n) -> p e k n", e=4, k=4)
            for e in range(4):
                sp.dma_start(f0w1[:, e, :, :], f0_W1[e, :, :].rearrange(wk, p=128)).then_inc(ld_f0, 16)
                sp.dma_start(f0w2[:, e, :, :], f0_W2[e, :, :].rearrange(wk, p=128)).then_inc(ld_f0, 16)
            sp.dma_start(Wr[:, :, :], f1_router.rearrange(wk, p=128)).then_inc(ld_gn, 16)
            with nc.allow_non_contiguous_dma(reason="biases, a few hundred elements"):
                sp.dma_start(b1_T[:, :].unsqueeze(2), f0_b1.rearrange("e (m p) -> p (e m)", p=128).unsqueeze(2)).then_inc(ld_f0, 16)
                sp.dma_start(bin_T[:, :].unsqueeze(2), gn_bin.rearrange("(m p) -> p m", p=128).unsqueeze(2)).then_inc(ld_gn, 16)
                sp.dma_start(bhid_T[:, :, :].rearrange("p l m -> p (l m)").unsqueeze(2), gn_bhid.rearrange("l (m p) -> p (l m)", p=128).unsqueeze(2)).then_inc(ld_gn, 16)
            sp.wait_ge(tab_rdy, 1)
            sp.dma_start(tab_src[0:N, :].rearrange("(p t) c -> p t c", t=T), tab).then_inc(tab_st, 16)
            sp.dma_start(tab_dst[0:N, :].rearrange("(p t) c -> p t c", t=T), uv[:, :, :]).then_inc(tab_st, 16)
            sp.wait_ge(sc_done, B1 + 1)
            sp.wait_ge(gat_s[0], 128 * (B1 // 2 + 1))
            sp.wait_ge(prep, B1 + 1)
            sp.dma_start(BIG2[0:P, 0:T * MSG].rearrange("p (t c) -> p t c", c=MSG), sums[0:N, :].rearrange("(p t) c -> p t c", t=T)).then_inc(ld_sums, 16)
            sp.wait_ge(rt_tab_rdy, 1)
            sp.dma_start(rt_src.rearrange("(p t) c -> p t c", t=T), tab2[:, :, :]).then_inc(rt_tab_st, 16)
            sp.dma_start(rt_dst.rearrange("(p t) c -> p t c", t=T), uv[:, :, :]).then_inc(rt_tab_st, 16)
            cells = counts[0:N * CC, 0].rearrange("(p k n) -> p k n", k=T, n=CC)

            def stream(q0, g):
                for k in range(KQ):
                    sp.wait_ge(pc_free, q0 + k + 1)
                    sp.dma_start(piece[k], cells[:, KQ * k:KQ * k + KQ, bass.ds(g * CW, CW)]).then_inc(pc_ld[k], 16)

            sp.wait_ge(sums_free, 1)
            with sp.Fori(0, NG) as g:
                stream(g * KQ, g)
            sp.wait_ge(rt_agg, 2)
            sp.dma_start(b2_bc[:, 0:4, :].rearrange("p e n -> p (e n)"), f0_b2.rearrange("e n -> (e n)").partition_broadcast(P)).then_inc(ld_f0, 16)
            sp.wait_ge(f0_done, 1)
            f1w1 = FW[:, 0:4096].rearrange("p (e k n) -> p e k n", e=8, k=2)
            f1w2 = FW[:, 4096:8192].rearrange("p (e k n) -> p e k n", e=8, k=2)
            sp.dma_start(Win[:, :, :], gn_Win.rearrange(wk, p=128)).then_inc(ld_gn, 16)
            sp.dma_start(Wout[:, :, :], gn_Wout.rearrange(wk, p=128)).then_inc(ld_gn, 16)
            for l in range(3):
                sp.dma_start(Wagg[:, l, :, :], gn_Wagg[l, :, :].rearrange(wk, p=128)).then_inc(ld_gn, 16)
                sp.dma_start(Wself[:, l, :, :], gn_Wself[l, :, :].rearrange(wk, p=128)).then_inc(ld_gn, 16)
            for e in range(8):
                sp.dma_start(f1w2[:, e, :, :], f1_W2[e, :, :].rearrange(wk, p=128)).then_inc(ld_f1, 16)
            sp.dma_start(row_b[:, :], gn_bout.partition_broadcast(P)).then_inc(ld_f1, 16)
            with nc.allow_non_contiguous_dma(reason="biases, a few hundred elements"):
                sp.dma_start(b1_T[:, :].unsqueeze(2), f1_b1.rearrange("e (m p) -> p (e m)", p=128).unsqueeze(2)).then_inc(ld_f1, 16)
            with sp.Fori(0, 3) as l:
                with sp.Fori(0, NG) as g:
                    stream(l * (NG * KQ) + g * KQ + NG * KQ, g)
            sp.wait_ge(o_mm, T)
            for e in range(8):
                sp.dma_start(f1w1[:, e, :, :], f1_W1[e, :, :].rearrange(wk, p=128)).then_inc(ld_f1b, 16)
            sp.wait_ge(gate1_rdy, 1)
            sp.dma_start(b2_bc[:, :, :].rearrange("p e n -> p (e n)"), f1_b2.rearrange("e n -> (e n)").partition_broadcast(P)).then_inc(ld_b2, 16)
            sp.wait_ge(all_done, 1)
            sp.dma_start(out.rearrange("(p t) d -> p t d", t=T), X[:, :, :]).then_inc(stored, 16)
            sp.wait_ge(stored, 16)

        @block.gpsimd
        def _(pool):
            pool.memset(e_src, PAD).then_inc(idx_mem, 1)
            pool.memset(e_dst, PAD).then_inc(idx_mem, 1)
            pool.memset(zrow, 0.0).then_inc(z_mem, 1)
            pool.memset(ident[:, :], 0.0).then_inc(consts, 1)
            pool.memset(ones[:, :], 1.0).then_inc(consts, 1)
            pool.memset(tie[:, :, :], 1.0).then_inc(consts, 1)
            pool.memset(e_src2[:, C2:C2P], 0).then_inc(consts, 1)
            pool.memset(e_dst2[:, C2:C2P], 0).then_inc(consts, 1)
            pool.memset(XT[:, :, N:CC], 0.0).then_inc(consts, 1)
            pool.wait_ge(consts, 6)
            pool.affine_select(out=ident[:, :], in_=ident[:, :], compare_op=ALU.not_equal, fill=1.0, base=0,
                               pattern=[[-1, 128]], channel_multiplier=1).then_inc(consts, 1)
            pool.affine_select(out=lower[:, :], in_=ones[:, :], compare_op=ALU.is_gt, fill=0.0, base=0,
                               pattern=[[-1, 128]], channel_multiplier=1).then_inc(consts, 1)
            pool.affine_select(out=tie[:, :, :], in_=tie[:, :, :], compare_op=ALU.is_gt, fill=0.0, base=0,
                               pattern=[[1, 8], [-1, 8]], channel_multiplier=0).then_inc(consts, 1)
            pool.iota(iota_i[:, :], pattern=[[1, P]], base=0, channel_multiplier=0).then_inc(consts, 1)
            pool.iota(pidx_i[:, 0:1], pattern=[[0, 1]], base=ROWS, channel_multiplier=1).then_inc(consts, 1)
            pool.iota(pidx_i[:, 1:2], pattern=[[0, 1]], base=CELLS, channel_multiplier=1).then_inc(consts, 1)

            pool.wait_ge(mx, 1)
            pool.partition_all_reduce(amax[:, 1, :], amax[:, 0, :], P, RMAX).then_inc(mxr, 1)

            pool.sem_inc(sc_done, 1)

            def gather(s, j, tabs, slots, bufs, done):
                for k in range(2):
                    pool.indirect_dma_start(
                        out=bufs[k][:, s, j, :], out_offset=None, in_=tabs[k],
                        in_offset=bass.IndirectOffsetOnAxis(ap=slots[:, s, k, j:j + 1], axis=0)).then_inc(done[s], 16)

            first = ([tab_src, tab_dst], slot_i, [gath, gathd], gat_s)
            pool.wait_ge(tab_st, 32)
            pool.wait_ge(z_done, 16 * (T + 1 + 3 + 3))
            pool.wait_ge(gidx, 1)
            for j in range(Q):
                gather(0, j, *first)
            with pool.Fori(0, B1 // 2) as it:
                for s in range(2):
                    b = it * 2 + s
                    pool.wait_ge(gidx, b + 2)
                    pool.wait_ge(prep, b + 1)
                    pool.wait_ge(msum_rdy, b + 2)
                    pool.sem_inc(pool_steps, 1)
                    for j in range(Q):
                        pool.indirect_dma_start(
                            out=sums, out_offset=bass.IndirectOffsetOnAxis(ap=slot_i[:, s, 2, j:j + 1], axis=0),
                            in_=msum[:, s, j, :], in_offset=None, compute_op=ALU.add).then_inc(row_sc, 16)
                        pool.indirect_dma_start(
                            out=counts, out_offset=bass.IndirectOffsetOnAxis(ap=slot_i[:, s, 3, j:j + 1], axis=0),
                            in_=slot_f[:, s, 0, j:j + 1], in_offset=None, compute_op=ALU.add).then_inc(cell_sc, 16)
                        gather(1 - s, j, *first)
                        pool.wait_ge(row_sc, b * (16 * Q) + 16 * (j + 1))
                        pool.wait_ge(cell_sc, b * (16 * Q) + 16 * (j + 1))
                        pool.sem_inc(pool_steps, 1)
                    pool.sem_inc(sc_done, 1)
            pool.wait_ge(gat_s[0], 128 * (B1 // 2 + 1))

            pool.wait_ge(mx, 2)
            pool.partition_all_reduce(amax[:, 1, :], amax[:, 0, :], P, RMAX).then_inc(mxr, 1)
            second = ([rt_src, rt_dst], slot_i, [gath2, gathd2], gat2_s)
            pool.wait_ge(rt_tab_st, 32)
            pool.wait_ge(gidx2, 1)
            for j in range(Q):
                gather(0, j, *second)
            with pool.Fori(0, B2 // 2) as it:
                for s in range(2):
                    pool.wait_ge(gidx2, it * 2 + s + 2)
                    pool.sem_inc(pool_steps, 1)
                    for j in range(Q):
                        gather(1 - s, j, *second)
            pool.wait_ge(gat2_s[0], 128 * (B2 // 2 + 1))

        @block.tensor
        def _(pe):
            mm = pe.matmul
            pe.wait_ge(consts, 12)

            def tiles(i, product=None, done=None):
                s = S[i]
                pe.sem_inc(s["tr"], 5)
                if product:
                    pe.sem_inc(s["h"], 2)
                with pe.Fori(0, G) as g:
                    def turn(j):
                        n = g * J + j
                        pe.wait_ge(s["xn"], n + 1)
                        pe.wait_ge(s["xT"], free(n, j))
                        for k in range(2):
                            last = pe.transpose(bank[j % 2][:, k * P:(k + 1) * P], xn_s[:, j, k * 128:(k + 1) * 128], ident[0:P, 0:P])
                        last.then_inc(s["tr"], 1)

                    def multiply(j):
                        n = g * J + j
                        pe.wait_ge(s["xT"], n + 3)
                        pe.wait_ge(s["hev"], free(n, j))
                        product(j).then_inc(s["h"], 1)

                    for j in range(J):
                        turn(j)
                        if product and j:
                            multiply(j - 1)
                    if product:
                        multiply(J - 1)

            def with_weights(w, width):
                def product(j):
                    for k in range(2):
                        last = mm(bank[2 + j % 2][0:P, 0:width], xT_s[:, j % 2, k, :], w[:, k, :], start=k == 0, stop=k == 1)
                    return last
                return product

            pe.wait_ge(ld_gat, 64)
            tiles(0, with_weights(Wg, D))

            def spread_numbers():
                for k in range(2):
                    last = mm(bank[k][:, :], ones[:, :], diag[:, k, :, :].rearrange("p q n -> p (q n)"), start=True, stop=True)
                return last

            pe.wait_ge(diag_rdy, 1)
            spread_numbers().then_inc(bc_rdy, 1)
            with pe.Fori(0, B1 // 2) as it:
                for s in range(2):
                    b = it * 2 + s
                    pe.wait_ge(diag_rdy, b + 2)
                    pe.wait_ge(prep, b + 1)
                    spread_numbers().then_inc(bc_rdy, 1)
                    pe.wait_ge(msg_rdy, b + 1)
                    pe.wait_ge(msum_rdy, b + 1)
                    for j in range(Q):
                        last = mm(bank[2 + j][:, 0:MSG], same[:, s, j, :], msg[:, s, j, :], start=True, stop=True)
                    last.then_inc(agg_rdy, 1)

            pe.wait_ge(ld_rt, 128)
            tiles(1, with_weights(W16, 16))

            for_router = bank[0]
            zero_l, zero_r = RD[:, 0:P], RD[:, 0:T * 20]
            pe.sem_inc(spread_used, 2)
            pe.sem_inc(pc_free, KQ)
            pe.wait_ge(rt_tab_rdy, 1)
            mm(for_router[0:P, 0:T * 20], zero_l, zero_r, start=True, stop=False, skip_group_check=True).then_inc(rt_agg, 1)
            with pe.Fori(0, B2 // 2) as it:
                for s in range(2):
                    pe.wait_ge(spread_rdy, it * 2 + s + 1)
                    for j in range(Q):
                        last = mm(for_router[0:P, 0:T * 20], onep[:, s, j, :],
                                  spread[:, s, j, :, :].rearrange("p t c -> p (t c)"), start=False, stop=False, skip_group_check=True)
                    last.then_inc(spread_used, 1)
            mm(for_router[0:P, 0:T * 20], zero_l, zero_r, start=False, stop=True, skip_group_check=True).then_inc(rt_agg, 1)
            with pe.Fori(0, NG) as g:
                pe.wait_ge(deg_ev, g + 1)
                for k in range(KQ):
                    pe.wait_ge(pc_ld[k], g * 16 + 16)
                    for r in range(KQ):
                        last = mm(bank[1][:, 0:CW], ones[0:P, :], piece[k][:, r, :], start=k + r == 0, stop=k + r == 2 * (KQ - 1))
                    last.then_inc(pc_free, 1)

            def experts(i, n_e, n_m, w1, w2):
                s = EX[i]
                with pe.Fori(0, G) as g:
                    def up(e):
                        for m in range(n_m):
                            c = e * n_m + m
                            a = 2 * (c % 2)
                            pe.wait_ge(s["act"], g * (n_e * n_m) + (c + 1))
                            for lo, width, bk in ((0, 3 * P, a), (3 * P, 2 * P, a + 1)):
                                for k in range(2):
                                    last = mm(bank[bk][:, 0:width], w1[:, e, k, m * 128:(m + 1) * 128],
                                              XT[:, k, bass.ds(g * (J * P) + lo, width)], start=k == 0, stop=k == 1)
                            last.then_inc(s["up"], 1)

                    def down(e):
                        pe.wait_ge(s["act"], g * (n_e * n_m) + ((e + 1) * n_m + 2))
                        for j in range(J):
                            c = e * J + j
                            pe.wait_ge(s["acc"], g * (n_e * J) + (c + 1))
                            for m in range(n_m):
                                last = mm(bank[4 + c % 2][0:P, 0:D], hh[:, e % 2, m, j * P:(j + 1) * P], w2[:, e, m, :],
                                          start=m == 0, stop=m == n_m - 1)
                            last.then_inc(s["dn"], 1)

                    up(0)
                    for e in range(n_e):
                        if e + 1 < n_e:
                            up(e + 1)
                        down(e)

            pe.wait_ge(ld_f0, LD_F0)
            pe.wait_ge(gate_rdy, 1)
            experts(0, 4, 4, FW[:, 0:4096].rearrange("p (e k n) -> p e k n", e=4, k=2),
                    FW[:, 4096:8192].rearrange("p (e k n) -> p e k n", e=4, k=4))

            pe.wait_ge(ld_gn, LD_GN)
            tiles(2)
            pe.wait_ge(S[2]["xT"], T + 2)
            with pe.Fori(0, NG) as g:
                pe.wait_ge(in_ev, g + 1)
                for f in range(2):
                    for k in range(2):
                        last = mm(bank[2 + f][:, 0:CW], Win[:, k, f * 128:(f + 1) * 128], XT[:, k, bass.ds(g * CW, CW)], start=k == 0, stop=k == 1)
                last.then_inc(in_mm, 1)
            pe.wait_ge(in_ev, NG + 1)

            def tile_cols(k, t):
                return XT[:, k, 0:N].rearrange("p (a t) -> p t a", t=T)[:, t, :]

            with pe.Fori(0, 3) as l:
                pe.wait_ge(gn_rel, l * NG + 1)
                for t in range(T):
                    pe.wait_ge(z_ev, l * T + free(t, t))
                    for k in range(2):
                        last = mm(bank[t % 2][0:P, 0:D], tile_cols(k, t), Wagg[:, bass.ds(l, 1), k, :].rearrange("p o n -> p (o n)"), start=k == 0, stop=k == 1)
                    last.then_inc(z_mm, 1)
                pe.wait_ge(wcur, l + 1)
                pe.wait_ge(z_ev, l * T + (T + 2))
                pe.sem_inc(pe_steps, 1)
                with pe.Fori(0, NG) as g:
                    q = l * NG + g
                    pe.wait_ge(gn_sum, q + 1)
                    for k in range(KQ):
                        pe.wait_ge(pc_ld[k], q * 16 + 16 * (NG + 1))
                        for r in range(KQ):
                            t = KQ * k + r
                            for f in range(2):
                                last = mm(bank[4 + f][:, 0:CW], hid1[:, t, f * 128:(f + 1) * 128], piece[k][:, r, :], start=t == 0, stop=t == T - 1)
                        last.then_inc(pc_free, 1)
                    for f in range(2):
                        for k in range(2):
                            last = mm(bank[6 + f][:, 0:CW], Wcur[:, k, f * 128:(f + 1) * 128], XT[:, k, bass.ds(g * CW, CW)], start=k == 0, stop=k == 1)
                    last.then_inc(gn_mm, 1)
            pe.wait_ge(gn_rel, 3 * NG + 1)
            for t in range(T):
                pe.wait_ge(o_acc, free(t, t))
                for k in range(2):
                    last = mm(bank[t % 2][0:P, 0:D], tile_cols(k, t), Wout[:, k, :], start=k == 0, stop=k == 1)
                last.then_inc(o_mm, 1)

            tiles(3, with_weights(Wr, 8))
            pe.wait_ge(ld_f1, LD_F1)
            pe.wait_ge(ld_f1b, 16 * 8)
            pe.wait_ge(gate1_rdy, 1)
            experts(1, 8, 2, FW[:, 0:4096].rearrange("p (e k n) -> p e k n", e=8, k=2),
                    FW[:, 4096:8192].rearrange("p (e k n) -> p e k n", e=8, k=2))

        @block.scalar
        def _(act):
            step = Chain(act, act_chain)
            fn = act.activation

            def root(i):
                act.wait_ge(ln_var, i + 1)
                fn(ln[:, 3, :], ln[:, 2, :], ACT.Sqrt).then_inc(ln_std, 1)

            def tiles(i, wide=None, store=None):
                s = S[i]
                act.sem_inc(s["xT"], 2)
                if store:
                    act.sem_inc(s["hev"], 2)
                with act.Fori(0, G) as g:
                    def copy(j):
                        n = g * J + j
                        act.wait_ge(s["tr"], n + 6)
                        if store:
                            act.wait_ge(s["h"], free(n, j))
                        got = bank[j % 2][:, 0:2 * P].rearrange("p (k n) -> p k n", k=2)
                        if wide:
                            last = fn(wide(n), got, ACT.Copy)
                        if store:
                            last = fn(xT_s[:, j % 2, :, :], got, ACT.Copy)
                        last.then_inc(s["xT"], 1)

                    def take(j):
                        n = g * J + j
                        act.wait_ge(s["h"], n + 3)
                        store(j, n).then_inc(s["hev"], 1)

                    for j in range(J):
                        copy(j)
                        if store and j:
                            take(j - 1)
                    if store:
                        take(J - 1)

            root(0)
            tiles(0, store=lambda j, n: fn(tab_h[:, n, :, 0:64], bank[2 + j % 2][0:P, 0:D].rearrange("p (h c) -> p h c", h=HEADS), ACT.Copy))

            def factors():
                for k, scale in ((4, 0.8), (5, 0.2), (6, 0.8), (7, -0.8)):
                    source = small[:, 2 if k < 6 else 3 if k == 6 else 8, :, :]
                    last = fn(small[:, k, :, :], source, ACT.Exp, scale=scale)
                last.then_inc(f_out, 1)

            act.wait_ge(f_in, 1)
            factors()

            act.sem_inc(msum_rdy, 1)

            def diagonals(b):
                for k, a in ((0, dst_f), (1, key_f)):
                    for j in range(Q):
                        last = fn(diag[:, k, j, :], ident[:, :], ACT.Copy, scale=a[:, bass.ds(b * Q + j, 1)] if not isinstance(b, int) else a[:, b * Q + j:b * Q + j + 1])
                last.then_inc(diag_rdy, 1)

            act.wait_ge(idx_dve, 1)
            act.wait_ge(consts, 12)
            diagonals(0)
            with act.Fori(0, B1 // 2) as it:
                for s in range(2):
                    b = it * 2 + s
                    act.wait_ge(bc_rdy, b + 1)
                    diagonals(b + 1)
                    act.wait_ge(agg_rdy, b + 1)
                    for j in range(Q):
                        last = fn(msum[:, s, j, :], bank[2 + j][:, 0:MSG], ACT.Copy)
                    last.then_inc(msum_rdy, 1)

            root(1)
            tmajor = XT[:, :, 0:N].rearrange("p k (t n) -> p k t n", n=P)
            tiles(1, wide=lambda n: tmajor[:, :, n, :],
                  store=lambda j, n: fn(s16[:, 0, n, :], bank[2 + j % 2][0:P, 0:16], ACT.Copy))
            act.wait_ge(f_in, 2)
            factors()
            act.sem_inc(deg_ev, 1)
            act.wait_ge(z_done, 16 * (T + 1 + 3 + 3))
            act.wait_ge(rt_agg, 2)
            with act.Fori(0, NG) as g:
                act.wait_ge(pc_free, g * KQ + 2 * KQ)
                fn(RD[:, bass.ds(g * CW, CW)], bank[1][:, 0:CW], ACT.Copy).then_inc(deg_ev, 1)
            act.wait_ge(ln_var, 3)
            fn(ln[:, 3, :], ln[:, 2, :], ACT.Sqrt).then_inc(ln_std, 1)
            act.wait_ge(f_in, 3)
            fn(small[:, 1, :, :], small[:, 1, :, :], ACT.Exp).then_inc(f_out, 1)

            def experts(i, n_e, n_m):
                s = EX[i]
                act.sem_inc(s["act"], 2)
                with act.Fori(0, G) as g:
                    for e in range(n_e):
                        u = e % 2
                        for m in range(n_m):
                            c = e * n_m + m
                            a = 2 * (c % 2)
                            act.wait_ge(s["up"], g * (n_e * n_m) + (c + 1))
                            for lo, width, bk in ((0, 3 * P, a), (3 * P, 2 * P, a + 1)):
                                last = fn(hh[:, u, m, lo:lo + width], bank[bk][:, 0:width], ACT.Gelu, bias=b1_T[:, c:c + 1])
                            last.then_inc(s["act"], 1)

            act.wait_ge(rd_done, 1)
            act.wait_ge(ld_f0, LD_F0)
            experts(0, 4, 4)

            root(3)
            natural = XT[:, :, 0:N].rearrange("p k (n t) -> p k t n", t=T)
            act.wait_ge(EX[0]["dn"], G * 4 * J)
            tiles(2, wide=lambda n: natural[:, :, n, :])
            act.wait_ge(ld_gn, LD_GN)
            act.sem_inc(in_ev, 1)
            with act.Fori(0, NG) as g:
                act.wait_ge(in_mm, g + 1)
                for f in range(2):
                    last = fn(XT[:, f, bass.ds(g * CW, CW)], bank[2 + f][:, 0:CW], ACT.Identity, bias=bin_T[:, f:f + 1])
                last.then_inc(in_ev, 1)
            act.sem_inc(z_ev, 2)
            act.sem_inc(gn_rel, 1)
            with act.Fori(0, 3) as l:
                act.wait_ge(gn_rel, l * NG + 1)
                fn(Wcur[:, :, :], Wself[:, bass.ds(l, 1), :, :].rearrange("p o k n -> p (o k) n"), ACT.Copy).then_inc(wcur, 1)
                for t in range(T):
                    act.wait_ge(z_mm, l * T + (t + 1))
                    fn(hid1[:, t, :], bank[t % 2][0:P, 0:D], ACT.Copy).then_inc(z_ev, 1)
                with act.Fori(0, NG) as g:
                    act.wait_ge(gn_sum, l * NG + g + 2)
                    for f in range(2):
                        last = fn(XT[:, f, bass.ds(g * CW, CW)], XT[:, f, bass.ds(g * CW, CW)], ACT.Relu, bias=bhid_T[:, bass.ds(l, 1), f])
                    last.then_inc(gn_rel, 1)

            root(4)
            tiles(3, wide=lambda n: tmajor[:, :, n, :],
                  store=lambda j, n: fn(gates[:, n, :], bank[2 + j % 2][0:P, 0:8], ACT.Copy))
            act.wait_ge(f_in, 4)
            fn(gates[:, :, :], gates[:, :, :], ACT.Exp).then_inc(f_out, 1)
            act.wait_ge(ld_f1, LD_F1)
            experts(1, 8, 2)

        @block.vector
        def _(dve):
            step = Chain(dve, dve_chain)
            tt, ts, stt = dve.tensor_tensor, dve.tensor_scalar, dve.scalar_tensor_tensor

            def cast(shape, a, axis):
                return a.unsqueeze(axis).to_broadcast(shape)

            dve.wait_ge(consts, 12)
            dve.tensor_copy(iota_f[:, :], iota_i[:, :])
            step(dve.tensor_copy(pidx_f[:, :], pidx_i[:, :]))
            ts(dupw[:, :], lower[:, :], TRASH_MARK, 1.0, ALU.mult, ALU.add).then_inc(consts2, 1)
            dve.wait_ge(ld_edges, 64)
            dve.tensor_copy(src_f, e_src)
            step(dve.tensor_copy(dst_f, e_dst))
            step(stt(key_f, dst_f, float(CC), src_f, ALU.mult, ALU.add))
            ts(off_row, dst_f, -1.0, pidx_f[:, 0:1], ALU.mult, ALU.add)
            step(ts(off_cell, key_f, -1.0, pidx_f[:, 1:2], ALU.mult, ALU.add))
            dve.sem_inc(idx_dve, 1)

            def norm_stats(i):
                with step.loop(G, 1) as g:
                    for j in range(J):
                        last = dve.bn_stats(stats[:, bass.ds(g * J + j, 1), :].rearrange("p o c -> p (o c)"), X[:, bass.ds(g * J + j, 1), :].rearrange("p o c -> p (o c)"))
                    step(last)
                me, ve, mo, vo = stats[:, :, 1], stats[:, :, 2], stats[:, :, 4], stats[:, :, 5]
                tt(ln[:, 0, :], me, mo, ALU.add)
                tt(ln[:, 1, :], me, mo, ALU.subtract)
                step(tt(ln[:, 2, :], ve, vo, ALU.add))
                step(tt(ln[:, 1, :], ln[:, 1, :], ln[:, 1, :], ALU.mult))
                ts(ln[:, 0, :], ln[:, 0, :], 0.5, None, ALU.mult)
                ts(ln[:, 1, :], ln[:, 1, :], 0.25, 1e-5, ALU.mult, ALU.add)
                step(ts(ln[:, 2, :], ln[:, 2, :], 1.0 / D, None, ALU.mult))
                tt(ln[:, 2, :], ln[:, 2, :], ln[:, 1, :], ALU.add).then_inc(ln_var, 1)
                rsqrt(i)

            def rsqrt(i):
                dve.wait_ge(ln_std, i + 1)
                step(dve.reciprocal(ln[:, 4, :], ln[:, 3, :]))
                step(tt(ln[:, 4, :], ln[:, 4, :], ln[:, 2, :], ALU.mult))
                step(tt(ln[:, 4, :], ln[:, 4, :], ln[:, 3, :], ALU.add))
                step(dve.reciprocal(ln[:, 4, :], ln[:, 4, :]))
                step(ts(ln[:, 5, :], ln[:, 4, :], 2.0, None, ALU.mult))

            def normalised(i, g):
                for j in range(J):
                    n = g * J + j
                    dve.wait_ge(S[i]["tr"], n + 1)
                    ts(xn_s[:, j, :], X[:, n, :], ln[:, 0, bass.ds(n, 1)], ln[:, 5, bass.ds(n, 1)],
                       ALU.subtract, ALU.mult).then_inc(S[i]["xn"], 1)

            def heads(k):
                return small[:, k, :, :]

            def factors(turn):
                dve.tensor_reduce(amax[:, 0, :], heads(0).rearrange("p t h -> p h t"), AX, ALU.max).then_inc(mx, 1)
                dve.wait_ge(mxr, turn)
                top = cast([P, T, HEADS], amax[:, 1, :], 1)
                tt(heads(2), heads(0), top, ALU.subtract)
                step(tt(heads(3), heads(1), top, ALU.add))
                step(ts(heads(8), heads(3), 0.0, None, ALU.max))
                ts(heads(3), heads(3), 0.0, None, ALU.min).then_inc(f_in, 1)
                dve.wait_ge(f_out, turn)
                dve.tensor_copy(uv[:, :, 0:4], heads(6))
                dve.tensor_copy(uv[:, :, 4:8], heads(7))
                step(tt(heads(9), heads(4), heads(6), ALU.mult))
                step(tt(heads(9), heads(9), heads(7), ALU.max))

            dve.wait_ge(ld_x, 16)
            norm_stats(0)
            dve.wait_ge(ld_gat, 64)
            att_scr = BIG2[0:P, 0:2 * D].rearrange("p (k n) -> p k n", k=2)
            with step.loop(G, 2 * J) as g:
                normalised(0, g)
                for j in range(J):
                    n = g * J + j
                    dve.wait_ge(S[0]["hev"], n + 3)
                    for k, row in enumerate((row_as, row_ad)):
                        last = tt(att_scr[:, k, :].rearrange("p (h c) -> p h c", h=HEADS), tab_h[:, n, :, 0:64],
                                  row[:, :].rearrange("p (h c) -> p h c", h=HEADS), ALU.mult)
                    step(last)
                    step(dve.tensor_reduce(small[:, 0:2, n, :], att_scr.rearrange("p k (h c) -> p k h c", c=64), AX, ALU.add))
            factors(1)
            dve.wait_ge(S[0]["hev"], T + 2)
            dve.tensor_copy(tab[:, :, MSG:TAB], heads(4))
            dve.tensor_copy(tab_h[:, :, :, 64], heads(5))
            with step.loop(G, 1) as g:
                for j in range(J):
                    n = g * J + j
                    part = tab_h[:, n, :, 0:64]
                    last = tt(part, part, cast([P, HEADS, 64], small[:, 5, n, :], 2), ALU.mult)
                step(last)
            dve.sem_inc(tab_rdy, 1)

            def numbers(s, b):
                cols = bass.ds(b * Q, Q) if not isinstance(b, int) else slice(b * Q, b * Q + Q)
                dve.tensor_copy(slot_i[:, s, 0, :], e_src[:, cols])
                dve.tensor_copy(slot_i[:, s, 1, :], e_dst[:, cols]).then_inc(gidx, 1)

            def prepare(s, b):
                cols = bass.ds(b * Q, Q) if not isinstance(b, int) else slice(b * Q, b * Q + Q)
                shape = [128, Q, 128]
                f = lambda k: slot_f[:, s, k, :]
                tt(same[:, s, :, :], bank[0][:, :].rearrange("p (q n) -> p q n", q=Q), cast(shape, dst_f[:, cols], 2), ALU.is_equal)
                step(tt(samek, bank[1][:, :].rearrange("p (q n) -> p q n", q=Q), cast(shape, key_f[:, cols], 2), ALU.is_equal))
                tt(scr, same[:, s, :, :], cast(shape, lower[:, :], 1), ALU.mult)
                step(tt(samek, samek, cast(shape, dupw[:, :], 1), ALU.mult))
                dve.tensor_reduce(f(1), scr, AX, ALU.add)
                step(dve.tensor_reduce(f(0), samek, AX, ALU.add))
                stt(f(2), f(1), 0.0, off_row[:, cols], ALU.is_gt, ALU.mult)
                step(stt(f(3), f(0), TRASH_MARK, off_cell[:, cols], ALU.is_ge, ALU.mult))
                tt(slot_i[:, s, 2, :], f(2), dst_f[:, cols], ALU.add)
                tt(slot_i[:, s, 3, :], f(3), key_f[:, cols], ALU.add).then_inc(prep, 1)

            numbers(0, 0)
            dve.wait_ge(bc_rdy, 1)
            dve.wait_ge(consts2, 1)
            prepare(0, 0)
            with step.loop(B1 // 2, 12) as it:
                for s in range(2):
                    b = it * 2 + s
                    numbers(1 - s, b + 1)
                    dve.wait_ge(gat_s[s], it * 128 + 128)
                    step(tt(wgt[:, s, :, :], gath[:, s, :, MSG:TAB], gathd[:, s, :, 0:4], ALU.mult))
                    step(tt(wgt[:, s, :, :], wgt[:, s, :, :], gathd[:, s, :, 4:8], ALU.max))
                    dve.wait_ge(msum_rdy, b + 1)
                    tt(msg[:, s, :, :].rearrange("p q (h c) -> p q h c", c=65),
                       gath[:, s, :, 0:MSG].rearrange("p q (h c) -> p q h c", c=65),
                       cast([128, Q, HEADS, 65], wgt[:, s, :, :], 3), ALU.mult).then_inc(msg_rdy, 1)
                    dve.wait_ge(bc_rdy, b + 2)
                    dve.wait_ge(sc_done, b + 1)
                    prepare(1 - s, b + 1)
            dve.wait_ge(ld_sums, 16)
            dve.wait_ge(tab_st, 32)
            with step.loop(G, 3 * J) as g:
                for j in range(J):
                    n = g * J + j
                    own = tab_h[:, n, :, :]
                    tot = sums_sb[:, n, :, :]
                    step(tt(own, own, cast([P, HEADS, 65], small[:, 9, n, :], 2), ALU.mult))
                    step(tt(tot, tot, own, ALU.add))
                    step(ts(small[:, 4, n, :], tot[:, :, 64], 1e-30, None, ALU.max))
            step(dve.reciprocal(heads(5), heads(4)))
            with step.loop(G, 2 * J) as g:
                for j in range(J):
                    n = g * J + j
                    o = hrow[:, n, :, :]
                    flat = hid1[:, n, :]
                    step(tt(o, sums_sb[:, n, :, 0:64], cast([P, HEADS, 64], small[:, 5, n, :], 2), ALU.mult))
                    step(tt(flat, flat, row_b[:, :], ALU.add))
                    last = stt(X[:, n, :], flat, 0.0, X[:, n, :], ALU.max, ALU.add)
            step(dve.tensor_copy(small[:, 4, :, :], small[:, 5, :, :]))
            dve.sem_inc(sums_free, 1)

            norm_stats(1)
            with step.loop(G, 0) as g:
                normalised(1, g)
            dve.wait_ge(S[1]["hev"], T + 2)
            dve.wait_ge(ld_rt, 128)
            for k in range(2):
                step(tt(s16[:, 1, :, :], s16[:, 0, :, :], cast([P, T, 16], row16[:, k, :], 1), ALU.mult))
                step(dve.tensor_reduce(heads(k), s16[:, 1, :, :].rearrange("p t (h c) -> p t h c", c=4), AX, ALU.add))
            factors(2)
            own2 = tab2[:, :, 0:20].rearrange("p t (h c) -> p t h c", c=5)
            dve.tensor_copy(tab2[:, :, 20:24], heads(4))
            dve.tensor_copy(own2[:, :, :, 4], heads(5))
            step(tt(own2[:, :, :, 0:4], s16[:, 0, :, :].rearrange("p t (h c) -> p t h c", c=4), cast([P, T, HEADS, 4], heads(5), 3), ALU.mult))
            step(dve.tensor_copy(dd, e_dst2[:, :]))
            step(ts(td, dd, 0.5, 1.0 / T, ALU.add, ALU.mult))
            step(ts(td, td, -0.5, None, ALU.add))
            step(dve.tensor_copy(e_half, td))
            step(dve.tensor_copy(pd, e_half))
            step(stt(td, pd, -float(T), dd, ALU.mult, ALU.add))
            step(ts(dd, td, float(T), None, ALU.is_ge))
            step(tt(pd, pd, dd, ALU.add))
            step(stt(td, dd, -float(T), td, ALU.mult, ALU.add))
            dve.sem_inc(rt_tab_rdy, 1)

            def numbers2(s, b):
                cols = bass.ds(b * Q, Q) if not isinstance(b, int) else slice(b * Q, b * Q + Q)
                dve.tensor_copy(slot_i[:, s, 0, :], e_src2[:, cols])
                dve.tensor_copy(slot_i[:, s, 1, :], e_dst2[:, cols]).then_inc(gidx2, 1)

            numbers2(0, 0)
            with step.loop(B2 // 2, 6) as it:
                for s in range(2):
                    b = it * 2 + s
                    numbers2(1 - s, b + 1)
                    cols = bass.ds(b * Q, Q)
                    dve.wait_ge(gat2_s[s], it * 128 + 128)
                    step(tt(wgt[:, s, :, :], gath2[:, s, :, 20:24], gathd2[:, s, :, 0:4], ALU.mult))
                    step(tt(wgt[:, s, :, :], wgt[:, s, :, :], gathd2[:, s, :, 4:8], ALU.max))
                    dve.wait_ge(spread_used, b + 1)
                    tt(msg2.rearrange("p q (h c) -> p q h c", c=5), gath2[:, s, :, 0:20].rearrange("p q (h c) -> p q h c", c=5),
                       cast([128, Q, HEADS, 5], wgt[:, s, :, :], 3), ALU.mult)
                    tt(onet, cast([128, Q, T], iota_f[:, 0:T], 1), cast([128, Q, T], td[:, cols], 2), ALU.is_equal)
                    step(tt(onep[:, s, :, :], cast([128, Q, P], iota_f[:, :], 1), cast([128, Q, P], pd[:, cols], 2), ALU.is_equal))
                    for j in range(Q):
                        last = tt(spread[:, s, j, :, :], cast([128, T, 20], onet[:, j, :], 2), cast([128, T, 20], msg2[:, j, :], 1), ALU.mult)
                    last.then_inc(spread_rdy, 1)
            dve.wait_ge(rt_agg, 2)
            dve.wait_ge(gat2_s[0], 128 * (B2 // 2 + 1))
            got = bank[0][0:P, 0:T * 20].rearrange("p (t h c) -> p t h c", h=HEADS, c=5)
            step(tt(own2, own2, cast([P, T, HEADS, 5], heads(9), 3), ALU.mult))
            step(tt(own2, own2, got, ALU.add))
            step(ts(heads(4), own2[:, :, :, 4], 1e-30, None, ALU.max))
            step(dve.reciprocal(heads(5), heads(4)))
            agg, dev, sq = (s16[:, k, :, :] for k in range(3))
            step(tt(agg.rearrange("p t (h c) -> p t h c", c=4), own2[:, :, :, 0:4], cast([P, T, HEADS, 4], heads(5), 3), ALU.mult))
            step(tt(agg, agg, cast([P, T, 16], row16[:, 2, :], 1), ALU.add))
            step(dve.tensor_reduce(ln[:, 0, :], agg, AX, ALU.add))
            step(ts(ln[:, 0, :], ln[:, 0, :], 1.0 / 16, None, ALU.mult))
            step(tt(dev, agg, cast([P, T, 16], ln[:, 0, :], 2), ALU.subtract))
            step(tt(sq, dev, dev, ALU.mult))
            step(dve.tensor_reduce(ln[:, 1, :], sq, AX, ALU.add))
            ts(ln[:, 2, :], ln[:, 1, :], 1.0 / 16, 1e-5, ALU.mult, ALU.add).then_inc(ln_var, 1)
            rsqrt(2)
            step(tt(dev, dev, cast([P, T, 16], ln[:, 5, :], 2), ALU.mult))
            step(tt(dev, dev, cast([P, T, 16], row16[:, 3, :], 1), ALU.mult))
            step(tt(dev, dev, cast([P, T, 16], row16[:, 4, :], 1), ALU.add))
            step(dve.tensor_reduce(heads(0), dev.rearrange("p t (h e) -> p t e h", h=HEADS), AX, ALU.add))
            step(ts(heads(0), heads(0), 1.0 / HEADS, None, ALU.mult))

            def top_two(scores, n_e, sel):
                shape = [P, T, n_e, n_e]
                a = rank_a[:, 0:T * n_e * n_e].rearrange("p (t e f) -> p t e f", e=n_e, f=n_e)
                b = rank_b[:, 0:T * n_e * n_e].rearrange("p (t e f) -> p t e f", e=n_e, f=n_e)
                mine, other = cast(shape, scores, 3), cast(shape, scores, 2)
                tt(a, other, mine, ALU.is_gt)
                step(tt(b, other, mine, ALU.is_equal))
                for e in range(n_e):
                    last = tt(b[:, :, e, :], b[:, :, e, :], cast([P, T, n_e], tie[0:P, e, 0:n_e], 1), ALU.mult)
                step(last)
                step(tt(a, a, b, ALU.add))
                step(dve.tensor_reduce(sel, a, AX, ALU.add))
                step(ts(sel, sel, 2.0, None, ALU.is_lt))

            top_two(heads(0), 4, heads(2))
            step(dve.tensor_reduce(ln[:, 0, :], heads(0), AX, ALU.max))
            tt(heads(1), heads(0), cast([P, T, 4], ln[:, 0, :], 2), ALU.subtract).then_inc(f_in, 1)
            dve.wait_ge(f_out, 3)
            step(tt(heads(1), heads(1), heads(2), ALU.mult))
            step(dve.tensor_reduce(ln[:, 0, :], heads(1), AX, ALU.add))
            step(dve.reciprocal(ln[:, 0, :], ln[:, 0, :]))
            step(tt(gates[:, :, 0:4], heads(1), cast([P, T, 4], ln[:, 0, :], 2), ALU.mult))
            dve.wait_ge(deg_ev, NG + 1)
            step(ts(RD[:, :], RD[:, :], 1.0, None, ALU.max))
            step(dve.reciprocal(RD[:, :], RD[:, :]))
            dve.sem_inc(rd_done, 1)
            dve.sem_inc(gate_rdy, 1)

            def experts(i, n_e):
                s = EX[i]
                dve.sem_inc(s["acc"], 2)
                with step.loop(T, n_e) as t:
                    for e in range(n_e):
                        step(stt(X[:, t, :], b2_bc[:, e, :], gates[:, t, e:e + 1], X[:, t, :], ALU.mult, ALU.add))
                with dve.Fori(0, G) as g:
                    for e in range(n_e):
                        for j in range(J):
                            c = e * J + j
                            n = g * J + j
                            dve.wait_ge(s["dn"], g * (n_e * J) + (c + 1))
                            if e:
                                dve.wait_ge(s["acc"], g * (n_e * J) + (c - J + 3))
                            stt(X[:, n, :], bank[4 + c % 2][0:P, 0:D], gates[:, n, e:e + 1], X[:, n, :], ALU.mult, ALU.add).then_inc(s["acc"], 1)
                dve.wait_ge(s["acc"], G * n_e * J + 2)

            dve.wait_ge(ld_f0, LD_F0)
            experts(0, 4)
            dve.sem_inc(f0_done, 1)

            norm_stats(3)
            with step.loop(G, 0) as g:
                normalised(2, g)
            dve.sem_inc(gn_sum, 1)
            dve.wait_ge(rd_done, 1)
            with step.loop(3, NG) as l:
                with step.loop(NG, 1) as g:
                    q = l * NG + g
                    cols = bass.ds(g * CW, CW)
                    dve.wait_ge(gn_mm, q + 1)
                    for f in range(2):
                        last = tt(scr_g[:, f, :], bank[4 + f][:, 0:CW], RD[:, cols], ALU.mult)
                    step(last)
                    for f in range(2):
                        last = tt(XT[:, f, cols], scr_g[:, f, :], bank[6 + f][:, 0:CW], ALU.add)
                    last.then_inc(gn_sum, 1)
            dve.sem_inc(o_acc, 2)
            dve.wait_ge(ld_f1, LD_F1)
            with step.loop(T, 1) as t:
                step(tt(X[:, t, :], X[:, t, :], row_b[:, :], ALU.add))
            for t in range(T):
                dve.wait_ge(o_mm, t + 1)
                tt(X[:, t, :], bank[t % 2][0:P, 0:D], X[:, t, :], ALU.add).then_inc(o_acc, 1)
            dve.wait_ge(o_acc, T + 2)

            norm_stats(4)
            with step.loop(G, 1) as g:
                normalised(3, g)
                dve.wait_ge(S[3]["xn"], g * J + J)
                for j in range(J):
                    n = g * J + j
                    last = tt(X[:, n, :], X[:, n, :], xn_s[:, j, :], ALU.add)
                step(last)
            dve.wait_ge(S[3]["hev"], T + 2)
            g8 = gates[:, :, :]
            step(dve.tensor_reduce(ln[:, 0, :], g8, AX, ALU.max))
            tt(g8, g8, cast([P, T, 8], ln[:, 0, :], 2), ALU.subtract).then_inc(f_in, 1)
            dve.wait_ge(f_out, 4)
            step(dve.tensor_reduce(ln[:, 0, :], g8, AX, ALU.add))
            step(dve.reciprocal(ln[:, 0, :], ln[:, 0, :]))
            step(tt(g8, g8, cast([P, T, 8], ln[:, 0, :], 2), ALU.mult))
            top_two(g8, 8, uv[:, :, :])
            step(tt(g8, g8, uv[:, :, :], ALU.mult))
            step(dve.tensor_reduce(ln[:, 0, :], g8, AX, ALU.add))
            step(ts(ln[:, 0, :], ln[:, 0, :], 1e-12, None, ALU.max))
            step(dve.reciprocal(ln[:, 0, :], ln[:, 0, :]))
            step(tt(g8, g8, cast([P, T, 8], ln[:, 0, :], 2), ALU.mult))
            dve.sem_inc(gate1_rdy, 1)
            dve.wait_ge(ld_b2, 16)
            experts(1, 8)
            dve.sem_inc(all_done, 1)


_INS = ["x", "src", "dst", "L0_gnn_W", "L0_gnn_att_src", "L0_gnn_att_dst", "L0_gnn_bias", "L0_ffn_W_gat",
        "L0_ffn_att_src", "L0_ffn_att_dst", "L0_ffn_b_gat", "L0_ffn_ln_gamma", "L0_ffn_ln_beta", "L0_ffn_W1",
        "L0_ffn_b1", "L0_ffn_W2", "L0_ffn_b2", "L0_ffn_edge_index", "L1_gnn_W_in", "L1_gnn_b_in", "L1_gnn_W_agg",
        "L1_gnn_W_self", "L1_gnn_b_hid", "L1_gnn_W_out", "L1_gnn_b_out", "L1_ffn_router_w", "L1_ffn_w1",
        "L1_ffn_b1", "L1_ffn_w2", "L1_ffn_b2"]


def kernel(**inputs):
    import numpy as _np
    import concourse.bacc as _bacc
    from concourse import mybir as _mybir
    from concourse.bass_utils import run_bass_kernel_spmd as _run

    nc = _bacc.Bacc("TRN2", target_bir_lowering=False, num_devices=1)
    arrays, args = {}, []
    for name in _INS:
        a = _np.asarray(inputs[name])
        if name == "L1_ffn_router_w":
            a = a.T
        a = _np.ascontiguousarray(a)
        arrays[f"in_{name}"] = a
        args.append(nc.dram_tensor(f"in_{name}", a.shape, _mybir.dt.from_np(a.dtype), kind="ExternalInput").ap())
    out = nc.dram_tensor("out_0", (N, D), _mybir.dt.float32, kind="ExternalOutput").ap()
    build_model(nc, *args, out)
    r = _run(nc, [arrays], core_ids=[0])
    return r.results[0]["out_0"]
```

```python
import numpy as np
import concourse.bass as bass
from concourse import mybir
from contextlib import ExitStack, contextmanager

FP32 = mybir.dt.float32
F32R = mybir.dt.float32r
I32 = mybir.dt.int32
ALU = mybir.AluOpType
ACT = mybir.ActivationFunctionType
AX = mybir.AxisListType.X
RMAX = bass.bass_isa.ReduceOp.max

N, D = 3125, 256
P, T = 125, 25
G, J = 5, 5
HEADS = 4
E1 = 53125
C1 = 416
Q = 4
B1 = C1 // Q
C1P = C1 + 2 * Q
E2 = 32768
C2 = E2 // 128
B2 = C2 // Q
C2P = C2 + 2 * Q
PAD = N
CW = 450
NG = 7
CC = CW * NG
CELLS = (N + 1) * CC
ROWS = N + 1
KQ = 5
MSG = 260
TAB = 264
TRASH_MARK = 1024.0
EXACT = 4096
HALF = CC // 2
MERGES = 2 * T


class Chain:

    def __init__(self, eng, sem):
        self.eng, self.sem, self.base, self.k = eng, sem, 0, 0

    def __call__(self, ins):
        ins.then_inc(self.sem, 1)
        self.k += 1
        self.eng.wait_ge(self.sem, self.base + self.k)

    @contextmanager
    def loop(self, turns, per):
        base, k = self.base, self.k
        with self.eng.Fori(0, turns) as i:
            self.base, self.k = base + (i * per + k), 0
            yield i
            assert self.k == per, (self.k, per)
        self.base, self.k = base, k + turns * per


def build_model(nc, x, src, dst, gat_W, gat_as, gat_ad, gat_b, rt_W, rt_as, rt_ad, rt_b, rt_gamma, rt_beta,
                f0_W1, f0_b1, f0_W2, f0_b2, rt_edges, gn_Win, gn_bin, gn_Wagg, gn_Wself, gn_bhid, gn_Wout,
                gn_bout, f1_router, f1_W1, f1_b1, f1_W2, f1_b2, out):
    ctx = ExitStack()
    with ctx:
        def sb(name, shape, dt=FP32):
            return ctx.enter_context(nc.sbuf_tensor(name, shape, dt))

        def shared(name, shape, later):
            def aligned(n):
                return -(-n // 32) * 32

            sizes = [aligned(4 * int(np.prod(sh[1:]))) for _, sh, _ in later]
            size = max(aligned(4 * int(np.prod(shape[1:]))), sum(sizes))
            with nc.sbuf_tensor(name, [shape[0], size // 4], FP32) as first:
                pass
            views = [sb(n, sh, dt) for n, sh, dt in later]
            if size > sum(sizes):
                sb(name + "_rest", [shape[0], (size - sum(sizes)) // 4])
            return [first] + views

        def sem(name):
            return ctx.enter_context(nc.semaphore(name))

        counts = [nc.dram_tensor(f"counts{k}", [CELLS + 128, 1], FP32).ap() for k in range(2)]
        sums = [nc.dram_tensor(f"sums{k}", [ROWS + 128, MSG], FP32).ap() for k in range(2)]
        tab_src = nc.dram_tensor("tab_src", [ROWS, TAB], FP32).ap()
        rt_src = nc.dram_tensor("rt_src", [N, 24], FP32).ap()

        X = sb("X", [P, T, D])
        BIG1, Z_hi = shared("BIG1", [128, T * TAB], [("Z_hi", [P, T, D], F32R)])
        BIG2, *piece = shared("BIG2", [128, KQ * KQ * CW], [(f"piece{k}", [P, KQ, CW], F32R) for k in range(KQ)])
        XT = sb("XT", [128, 2, CC])
        FW, Z_lo, Wagg = shared("FW", [128, 8192], [("Z_lo", [P, T, D], F32R), ("Wagg", [128, 3, 2, D], FP32)])
        RD = sb("RD", [128, CC])
        xn_s = sb("xn_s", [P, J, D])
        xT_s = sb("xT_s", [128, 2, 2, P])
        Wg = sb("Wg", [128, 2, D])
        W16 = sb("W16", [128, 2, 16])
        Wr = sb("Wr", [128, 2, 8])
        Win = Wout = Wg
        scr_g = sb("scr_g", [128, 2, CW])
        Wself = sb("Wself", [128, 2, D])
        row_as = sb("row_as", [P, D])
        row_ad = sb("row_ad", [P, D])
        row_b = sb("row_b", [P, D])
        row16 = sb("row16", [P, 5, 16])
        b2_bc = BIG1[0:P, 4500:4500 + 8 * D].rearrange("p (e n) -> p e n", e=8)
        b1_T = sb("b1_T", [128, 16])
        bin_T = sb("bin_T", [128, 2])
        bhid_T = sb("bhid_T", [128, 3, 2])
        ident = sb("ident", [128, 128])
        ones = sb("ones", [128, 128])
        lower = sb("lower", [128, 128])
        dupw = sb("dupw", [128, 128])
        tie = sb("tie", [128, 8, 8])
        iota_i = sb("iota_i", [128, P], I32)
        iota_f = sb("iota_f", [128, P])
        pidx_i = sb("pidx_i", [128, 3], I32)
        pidx_f = sb("pidx_f", [128, 3])
        lane = pidx_f[:, 2:3]
        flag = sb("flag", [128, 8], I32)
        stats = sb("stats", [P, T, 6])
        ln = sb("ln", [P, 8, T])
        small = sb("small", [P, 10, T, HEADS])
        amax = sb("amax", [P, 2, HEADS])
        s16 = sb("s16", [P, 3, T, 16])
        tab2 = sb("tab2", [P, T, 24])
        uv = sb("uv", [P, T, 8])
        gates = sb("gates", [P, T, 8])
        e_src2 = sb("e_src2", [128, C2P], I32)
        e_dst2 = sb("e_dst2", [128, C2P], I32)
        xt_flat = XT[:, :, :].rearrange("p k n -> p (k n)")

        def column(k, dt=FP32):
            first = k * C1P if k < 7 else CC + (k - 7) * C1P
            part = xt_flat[:, first:first + C1P]
            return part if dt == FP32 else part.bitcast(dt)

        e_src, e_dst = column(0, I32), column(1, I32)
        src_f, dst_f, key_f, off_row, off_cell, dst_p, dst_t, div_f = (column(k) for k in range(2, 10))
        div_i = column(10, I32)
        tab = BIG1[0:P, 0:T * TAB].rearrange("p (t c) -> p t c", c=TAB)
        tab_h = tab[:, :, 0:MSG].rearrange("p t (h c) -> p t h c", c=65)
        hid1 = BIG1[0:P, 0:T * D].rearrange("p (t c) -> p t c", c=D)
        hrow = BIG1[0:P, 0:T * D].rearrange("p (t h c) -> p t h c", h=HEADS, c=64)

        def carve(big, at, shape):
            size = int(np.prod(shape))
            names = "abcd"[:len(shape)]
            view = big[:, at:at + size].rearrange(
                f"p ({' '.join(names)}) -> p {' '.join(names)}", **dict(zip(names, shape)))
            return view, at + size

        at = 0
        gath, at = carve(BIG2, at, [2, Q, TAB])
        same, at = carve(BIG2, at, [2, Q, 128])
        msg, at = carve(BIG2, at, [2, Q, MSG])
        msum, at = carve(BIG2, at, [2, Q, MSG])
        samek, at = carve(BIG2, at, [Q, 128])
        diag, at = carve(BIG2, at, [3, Q, 128])
        owner, at = carve(BIG2, at, [Q, 128])
        picked, at = carve(BIG2, at, [Q, T, 8])
        onet, at = carve(BIG2, at, [2, Q, T])
        scr = picked.rearrange("p q t c -> p (q t c)")[:, 0:Q * 128].rearrange("p (q n) -> p q n", q=Q)
        assert at <= KQ * KQ * CW
        slot_i = sb("slot_i", [128, 2, 3, Q], I32)
        slot_f = sb("slot_f", [128, 2, 6, Q])
        wgt = sb("wgt", [128, 2, Q, HEADS])
        uve = sb("uve", [128, Q, 8])
        sums_sb = BIG2[0:P, 0:T * MSG].rearrange("p (t h c) -> p t h c", h=HEADS, c=65)
        sums1_sb = FW[0:P, 0:T * MSG]
        at = 0
        gath2, at = carve(BIG1, at, [2, Q, 24])
        onep, at = carve(BIG1, at, [2, Q, P])
        msg2, at = carve(BIG1, at, [Q, 20])
        spread, at = carve(BIG1, at, [2, Q, T, 20])
        pd, at = carve(BIG1, at, [C2P])
        td, at = carve(BIG1, at, [C2P])
        dd, at = carve(BIG1, at, [C2P])
        halves, at = carve(BIG1, at, [C2P])
        e_half = halves.bitcast(I32)
        assert at <= T * TAB
        rank_a = BIG1[0:P, 0:T * 64]
        rank_b = BIG1[0:P, T * 64:2 * T * 64]
        hh, at = carve(BIG2, 0, [2, 4, J * P])
        merge_b = [BIG2[0:P, at + k * HALF:at + (k + 1) * HALF] for k in range(2)]
        merge_a = [BIG1[0:P, k * HALF:(k + 1) * HALF] for k in range(2)]
        assert at + 2 * HALF <= KQ * KQ * CW and 2 * HALF <= 4500
        zrow = RD[:, :]

        bank = [ctx.enter_context(nc.psum_tensor(f"bank{k}", [128, 512], FP32)) for k in range(8)]

        ld_x = sem("ld_x")
        ld_gat = sem("ld_gat")
        ld_edges = sem("ld_edges")
        ld_rt = sem("ld_rt")
        ld_gn = sem("ld_gn")
        ld_f0 = sem("ld_f0")
        ld_f1 = sem("ld_f1")
        ld_b2 = sem("ld_b2")
        z_mem = sem("z_mem")
        z_sums = sem("z_sums")
        z_counts = sem("z_counts")
        consts = sem("consts")
        consts2 = sem("consts2")
        idx_mem = sem("idx_mem")
        idx_dve = sem("idx_dve")
        dve_chain = sem("dve_chain")
        act_chain = sem("act_chain")
        ln_var = sem("ln_var")
        ln_std = sem("ln_std")
        S = [{k: sem(f"{k}_{i}") for k in ("xn", "tr", "xT", "h", "hev")} for i in range(4)]
        mx = sem("mx")
        mxr = sem("mxr")
        f_in = sem("f_in")
        f_out = sem("f_out")
        tab_rdy = sem("tab_rdy")
        tab_st = sem("tab_st")
        gidx = sem("gidx")
        gat_s = [sem(f"gathered{s}") for s in range(2)]
        diag_rdy = sem("diag_rdy")
        bc_rdy = sem("bc_rdy")
        prep = sem("prep")
        msg_rdy = sem("msg_rdy")
        agg_rdy = sem("agg_rdy")
        msum_rdy = sem("msum_rdy")
        row_sc = [sem(f"row_sc{k}") for k in range(2)]
        cell_sc = [sem(f"cell_sc{k}") for k in range(2)]
        own_rdy = sem("own_rdy")
        pick_mm = sem("pick_mm")
        pick_done = sem("pick_done")
        diag2_rdy = sem("diag2_rdy")
        bc2_rdy = sem("bc2_rdy")
        own2_rdy = sem("own2_rdy")
        pick2_mm = sem("pick2_mm")
        pick2_done = sem("pick2_done")
        mg_ld = [sem(f"mg_ld{k}") for k in range(2)]
        mg_st = [sem(f"mg_st{k}") for k in range(2)]
        mg_sum = sem("mg_sum")
        sc_done = sem("sc_done")
        ld_sums = sem("ld_sums")
        sums_free = sem("sums_free")
        rt_tab_rdy = sem("rt_tab_rdy")
        rt_tab_st = sem("rt_tab_st")
        gidx2 = sem("gidx2")
        gat2_s = [sem(f"gathered2_{s}") for s in range(2)]
        spread_rdy = sem("spread_rdy")
        spread_used = sem("spread_used")
        rt_agg = sem("rt_agg")
        pc_ld = [sem(f"pc_ld{k}") for k in range(KQ)]
        pc_free = sem("pc_free")
        deg_mm = sem("deg_mm")
        deg_ev = sem("deg_ev")
        rd_done = sem("rd_done")
        EX = [{k: sem(f"{k}_e{i}") for k in ("up", "act", "dn", "acc")} for i in range(2)]
        gate_rdy = sem("gate_rdy")
        gate1_rdy = sem("gate1_rdy")
        f0_done = sem("f0_done")
        in_mm = sem("in_mm")
        in_ev = sem("in_ev")
        z_mm = sem("z_mm")
        z_ev = sem("z_ev")
        ld_win = sem("ld_win")
        ld_wout = sem("ld_wout")
        ld_wself = sem("ld_wself")
        z_hi = sem("z_hi")
        ag_mm = sem("ag_mm")
        ag_read = sem("ag_read")
        gn_mm = sem("gn_mm")
        gn_sum = sem("gn_sum")
        gn_rel = sem("gn_rel")
        o_mm = sem("o_mm")
        o_acc = sem("o_acc")
        all_done = sem("all_done")
        stored = sem("stored")
        pool_steps = sem("pool_steps")
        pe_steps = sem("pe_steps")

        LD_GN = 16 * (3 + 3)
        LD_F1 = 16 * (16 + 2)
        LD_F0 = 16 * 10

        block = ctx.enter_context(nc.Block())

        def free(n, j):
            return n + (2 if j == 0 else 1)

        @block.sync
        def _(sp):
            sp.dma_start(X[:, :, :], x.rearrange("(p t) d -> p t d", t=T)).then_inc(ld_x, 16)
            sp.wait_ge(idx_mem, 2)
            for e, a in ((e_src, src), (e_dst, dst)):
                sp.dma_start(e[0:127, 0:C1], a[0:127 * C1].rearrange("(p c) -> p c", c=C1)).then_inc(ld_edges, 16)
                sp.dma_start(e[127:128, 0:E1 - 127 * C1], a[127 * C1:E1].rearrange("(o c) -> o c", o=1)).then_inc(ld_edges, 16)
            wk = "(k p) n -> p k n"
            sp.dma_start(Wg[:, :, :], gat_W.rearrange(wk, p=128)).then_inc(ld_gat, 16)
            sp.dma_start(row_as[:, :], gat_as.rearrange("h c -> (h c)").partition_broadcast(P)).then_inc(ld_gat, 16)
            sp.dma_start(row_ad[:, :], gat_ad.rearrange("h c -> (h c)").partition_broadcast(P)).then_inc(ld_gat, 16)
            sp.dma_start(row_b[:, :], gat_b.partition_broadcast(P)).then_inc(ld_gat, 16)
            sp.wait_ge(z_mem, 1)
            for k in range(2):
                sv = sums[k][0:N, :].rearrange("(p t) c -> p (t c)", t=T)
                for a in range(0, T * MSG, CC):
                    b = min(a + CC, T * MSG)
                    sp.dma_start(sv[:, a:b], zrow[0:P, 0:b - a]).then_inc(z_sums, 16)
                sp.dma_start(sums[k][N:N + 129, :].rearrange("(a b) c -> a (b c)", b=3), zrow[0:43, 0:3 * MSG]).then_inc(z_sums, 16)
            sp.dma_start(tab_src[N:N + 1, :], zrow[0:1, 0:TAB]).then_inc(z_sums, 16)
            for k in range(2):
                cv = counts[k][0:N * CC, 0].rearrange("(p t n) -> p t n", t=T, n=CC)
                for t in range(T):
                    sp.dma_start(cv[:, t, :], zrow[0:P, :]).then_inc(z_counts, 16)
                sp.dma_start(counts[k][N * CC:N * CC + CC + 128, 0].rearrange("(o n) -> o n", n=149), zrow[0:22, 0:149]).then_inc(z_counts, 16)
            sp.dma_start(e_src2[:, 0:C2], rt_edges[0, :].rearrange("(p c) -> p c", c=C2)).then_inc(ld_rt, 16)
            sp.dma_start(e_dst2[:, 0:C2], rt_edges[1, :].rearrange("(p c) -> p c", c=C2)).then_inc(ld_rt, 16)
            sp.dma_start(W16[:, :, :], rt_W.rearrange(wk, p=128)).then_inc(ld_rt, 16)
            for k, a in enumerate((rt_as, rt_ad)):
                sp.dma_start(row16[:, k, :], a.rearrange("h c -> (h c)").partition_broadcast(P)).then_inc(ld_rt, 16)
            for k, a in enumerate((rt_b, rt_gamma, rt_beta)):
                sp.dma_start(row16[:, 2 + k, :], a.partition_broadcast(P)).then_inc(ld_rt, 16)
            f0w1 = FW[:, 0:4096].rearrange("p (e k n) -> p e k n", e=4, k=2)
            f0w2 = FW[:, 4096:8192].rearrange("p (e k n) -> p e k n", e=4, k=4)
            sp.dma_start(Wr[:, :, :], f1_router.rearrange(wk, p=128)).then_inc(ld_gn, 16)
            with nc.allow_non_contiguous_dma(reason="biases, a few hundred elements"):
                sp.dma_start(b1_T[:, :].unsqueeze(2), f0_b1.rearrange("e (m p) -> p (e m)", p=128).unsqueeze(2)).then_inc(ld_f0, 16)
                sp.dma_start(bin_T[:, :].unsqueeze(2), gn_bin.rearrange("(m p) -> p m", p=128).unsqueeze(2)).then_inc(ld_gn, 16)
                sp.dma_start(bhid_T[:, :, :].rearrange("p l m -> p (l m)").unsqueeze(2), gn_bhid.rearrange("l (m p) -> p (l m)", p=128).unsqueeze(2)).then_inc(ld_gn, 16)
            sp.wait_ge(tab_rdy, 1)
            sp.dma_start(tab_src[0:N, :].rearrange("(p t) c -> p t c", t=T), tab).then_inc(tab_st, 16)
            for k in range(2):
                sp.wait_ge(row_sc[k], 16 * (2 * B1 + k))
            for s in range(2):
                sp.wait_ge(gat_s[s], 64 * (B1 // 2 + 1))
            sp.wait_ge(prep, B1 + 1)
            sp.wait_ge(pick_mm, B1 + 1)
            for k, to in enumerate((BIG2[0:P, 0:T * MSG], sums1_sb)):
                sp.dma_start(to.rearrange("p (t c) -> p t c", c=MSG), sums[k][0:N, :].rearrange("(p t) c -> p t c", t=T)).then_inc(ld_sums, 16)
            sp.wait_ge(sums_free, 1)
            for e in range(4):
                sp.dma_start(f0w1[:, e, :, :], f0_W1[e, :, :].rearrange(wk, p=128)).then_inc(ld_f0, 16)
                sp.dma_start(f0w2[:, e, :, :], f0_W2[e, :, :].rearrange(wk, p=128)).then_inc(ld_f0, 16)
            sp.wait_ge(rt_tab_rdy, 1)
            sp.dma_start(rt_src.rearrange("(p t) c -> p t c", t=T), tab2[:, :, :]).then_inc(rt_tab_st, 16)
            cells = counts[0][0:N * CC, 0].rearrange("(p k n) -> p k n", k=T, n=CC)

            def stream(q, g):
                for k in range(KQ):
                    if k < KQ - 1:
                        sp.wait_ge(pc_free, q * (KQ - 1) + (k + 1))
                    else:
                        sp.wait_ge(ag_mm, q + 1)
                    sp.dma_start(piece[k][:, :, :].bitcast(FP32), cells[:, KQ * k:KQ * k + KQ, bass.ds(g * CW, CW)]).then_inc(pc_ld[k], 16)

            sp.wait_ge(rt_agg, 2)
            sp.dma_start(b2_bc[:, 0:4, :].rearrange("p e n -> p (e n)"), f0_b2.rearrange("e n -> (e n)").partition_broadcast(P)).then_inc(ld_f0, 16)
            for s in range(2):
                sp.wait_ge(gat2_s[s], 64 * (B2 // 2 + 1))
            sp.wait_ge(gate_rdy, 1)
            for k in range(2):
                sp.wait_ge(cell_sc[k], 16 * (2 * B1 + k))
                sp.sem_inc(mg_st[k], 16)
            parts = [c[0:N * CC, 0].rearrange("(p m n) -> p m n", m=MERGES, n=HALF) for c in counts]
            per = MERGES // G
            with sp.Fori(0, G) as g:
                def fetch(i):
                    sp.wait_ge(mg_st[i % 2], g * (8 * per) + 16 * (i // 2 + 1))
                    for a, c in ((merge_a, 0), (merge_b, 1)):
                        sp.dma_start(a[i % 2], parts[c][:, bass.ds(g * per + i, 1), :].rearrange("p o n -> p (o n)")).then_inc(mg_ld[i % 2], 16)

                def put(i):
                    sp.wait_ge(mg_sum, g * per + (i + 1))
                    sp.dma_start(parts[0][:, bass.ds(g * per + i, 1), :].rearrange("p o n -> p (o n)"), merge_a[i % 2]).then_inc(mg_st[i % 2], 16)

                fetch(0)
                for i in range(1, per):
                    fetch(i)
                    put(i - 1)
                put(per - 1)
            sp.wait_ge(f0_done, 1)
            f1w1 = FW[:, 0:4096].rearrange("p (e k n) -> p e k n", e=8, k=2)
            f1w2 = FW[:, 4096:8192].rearrange("p (e k n) -> p e k n", e=8, k=2)
            sp.dma_start(Win[:, :, :], gn_Win.rearrange(wk, p=128)).then_inc(ld_win, 16)
            for l in range(3):
                sp.dma_start(Wagg[:, l, :, :], gn_Wagg[l, :, :].rearrange(wk, p=128)).then_inc(ld_gn, 16)
            sp.dma_start(row_b[:, :], gn_bout.partition_broadcast(P)).then_inc(ld_f1, 16)
            with nc.allow_non_contiguous_dma(reason="biases, a few hundred elements"):
                sp.dma_start(b1_T[:, :].unsqueeze(2), f1_b1.rearrange("e (m p) -> p (e m)", p=128).unsqueeze(2)).then_inc(ld_f1, 16)
            for k in range(2):
                sp.wait_ge(mg_st[k], 16 * (T + 1))
            sp.sem_inc(gn_mm, 1)
            with sp.Fori(0, 3) as l:
                sp.wait_ge(gn_mm, l * NG + 1)
                sp.dma_start(Wself[:, :, :], gn_Wself[bass.ds(l, 1), :, :].rearrange("o (k p) n -> p (o k) n", p=128)).then_inc(ld_wself, 16)
                with sp.Fori(0, NG) as g:
                    stream(l * NG + g, g)
            sp.dma_start(Wout[:, :, :], gn_Wout.rearrange(wk, p=128)).then_inc(ld_wout, 16)
            sp.wait_ge(gn_mm, 3 * NG + 1)
            for e in range(8):
                sp.dma_start(f1w1[:, e, :, :], f1_W1[e, :, :].rearrange(wk, p=128)).then_inc(ld_f1, 16)
                sp.dma_start(f1w2[:, e, :, :], f1_W2[e, :, :].rearrange(wk, p=128)).then_inc(ld_f1, 16)
            sp.wait_ge(gate1_rdy, 1)
            sp.dma_start(b2_bc[:, :, :].rearrange("p e n -> p (e n)"), f1_b2.rearrange("e n -> (e n)").partition_broadcast(P)).then_inc(ld_b2, 16)
            sp.wait_ge(all_done, 1)
            sp.dma_start(out.rearrange("(p t) d -> p t d", t=T), X[:, :, :]).then_inc(stored, 16)
            sp.wait_ge(stored, 16)

        @block.gpsimd
        def _(pool):
            pool.memset(e_src, PAD).then_inc(idx_mem, 1)
            pool.memset(e_dst, PAD).then_inc(idx_mem, 1)
            pool.memset(zrow, 0.0).then_inc(z_mem, 1)
            pool.memset(ident[:, :], 0.0).then_inc(consts, 1)
            pool.memset(ones[:, :], 1.0).then_inc(consts, 1)
            pool.memset(tie[:, :, :], 1.0).then_inc(consts, 1)
            pool.memset(e_src2[:, C2:C2P], 0).then_inc(consts, 1)
            pool.memset(e_dst2[:, C2:C2P], 0).then_inc(consts, 1)
            pool.memset(XT[:, :, N:CC], 0.0).then_inc(consts, 1)
            pool.wait_ge(consts, 6)
            pool.affine_select(out=ident[:, :], in_=ident[:, :], compare_op=ALU.not_equal, fill=1.0, base=0,
                               pattern=[[-1, 128]], channel_multiplier=1).then_inc(consts, 1)
            pool.affine_select(out=lower[:, :], in_=ones[:, :], compare_op=ALU.is_gt, fill=0.0, base=0,
                               pattern=[[-1, 128]], channel_multiplier=1).then_inc(consts, 1)
            pool.affine_select(out=tie[:, :, :], in_=tie[:, :, :], compare_op=ALU.is_gt, fill=0.0, base=0,
                               pattern=[[1, 8], [-1, 8]], channel_multiplier=0).then_inc(consts, 1)
            pool.iota(iota_i[:, :], pattern=[[1, P]], base=0, channel_multiplier=0).then_inc(consts, 1)
            pool.iota(pidx_i[:, 0:1], pattern=[[0, 1]], base=ROWS, channel_multiplier=1).then_inc(consts, 1)
            pool.iota(pidx_i[:, 1:2], pattern=[[0, 1]], base=CELLS, channel_multiplier=1).then_inc(consts, 1)

            pool.iota(pidx_i[:, 2:3], pattern=[[0, 1]], base=0, channel_multiplier=1).then_inc(consts, 1)

            pool.wait_ge(mx, 1)
            pool.partition_all_reduce(amax[:, 1, :], amax[:, 0, :], P, RMAX).then_inc(mxr, 1)

            def gather(s, j, table, buf, done):
                pool.indirect_dma_start(
                    out=buf[:, s, j, :], out_offset=None, in_=table,
                    in_offset=bass.IndirectOffsetOnAxis(ap=slot_i[:, s, 0, j:j + 1], axis=0)).then_inc(done[s], 16)

            first = (tab_src, gath, gat_s)
            pool.wait_ge(tab_st, 16)
            pool.wait_ge(z_sums, 16 * 9)
            for s in range(2):
                pool.wait_ge(gidx, s + 1)
                for j in range(Q):
                    gather(s, j, *first)
            pool.wait_ge(z_counts, 16 * 2 * (T + 1))
            pool.dma_start(sums[1][ROWS:ROWS + 1, :], zrow[0:1, 0:MSG]).then_inc(row_sc[1], 16)
            pool.dma_start(counts[1][CELLS:CELLS + 128, 0].rearrange("(o n) -> o n", o=1), zrow[0:1, 0:128]).then_inc(cell_sc[1], 16)
            with pool.Fori(0, B1 // 2) as it:
                for s in range(2):
                    b = it * 2 + s
                    pool.wait_ge(gidx, b + 3)
                    pool.wait_ge(prep, b + 1)
                    pool.wait_ge(msum_rdy, b + 2)
                    pool.sem_inc(pool_steps, 1)
                    for j in range(Q):
                        pool.indirect_dma_start(
                            out=sums[j % 2], out_offset=bass.IndirectOffsetOnAxis(ap=slot_i[:, s, 1, j:j + 1], axis=0),
                            in_=msum[:, s, j, :], in_offset=None, compute_op=ALU.add).then_inc(row_sc[j % 2], 16)
                        pool.indirect_dma_start(
                            out=counts[j % 2], out_offset=bass.IndirectOffsetOnAxis(ap=slot_i[:, s, 2, j:j + 1], axis=0),
                            in_=slot_f[:, s, 0, j:j + 1], in_offset=None, compute_op=ALU.add).then_inc(cell_sc[j % 2], 16)
                        gather(s, j, *first)
                        pool.wait_ge(row_sc[(j + 1) % 2], b * 32 + 16 * (j // 2 + 1))
                        pool.wait_ge(cell_sc[(j + 1) % 2], b * 32 + 16 * (j // 2 + 1))
                        pool.sem_inc(pool_steps, 1)
                        if j == 0:
                            pool.sem_inc(sc_done, 1)
            for s in range(2):
                pool.wait_ge(gat_s[s], 64 * (B1 // 2 + 1))

            pool.wait_ge(mx, 2)
            pool.partition_all_reduce(amax[:, 1, :], amax[:, 0, :], P, RMAX).then_inc(mxr, 1)
            second = (rt_src, gath2, gat2_s)
            pool.wait_ge(rt_tab_st, 16)
            for s in range(2):
                pool.wait_ge(gidx2, s + 1)
                for j in range(Q):
                    gather(s, j, *second)
            with pool.Fori(0, B2 // 2) as it:
                for s in range(2):
                    pool.wait_ge(gidx2, it * 2 + s + 3)
                    pool.sem_inc(pool_steps, 1)
                    for j in range(Q):
                        gather(s, j, *second)
            for s in range(2):
                pool.wait_ge(gat2_s[s], 64 * (B2 // 2 + 1))

        @block.tensor
        def _(pe):
            mm = pe.matmul
            pe.wait_ge(consts, 13)

            def tiles(i, product=None, done=None):
                s = S[i]
                pe.sem_inc(s["tr"], 5)
                if product:
                    pe.sem_inc(s["h"], 2)
                with pe.Fori(0, G) as g:
                    def turn(j):
                        n = g * J + j
                        pe.wait_ge(s["xn"], n + 1)
                        pe.wait_ge(s["xT"], free(n, j))
                        for k in range(2):
                            last = pe.transpose(bank[j % 2][:, k * P:(k + 1) * P], xn_s[:, j, k * 128:(k + 1) * 128], ident[0:P, 0:P])
                        last.then_inc(s["tr"], 1)

                    def multiply(j):
                        n = g * J + j
                        pe.wait_ge(s["xT"], n + 3)
                        pe.wait_ge(s["hev"], free(n, j))
                        product(j).then_inc(s["h"], 1)

                    for j in range(J):
                        turn(j)
                        if product and j:
                            multiply(j - 1)
                    if product:
                        multiply(J - 1)

            def with_weights(w, width):
                def product(j):
                    for k in range(2):
                        last = mm(bank[2 + j % 2][0:P, 0:width], xT_s[:, j % 2, k, :], w[:, k, :], start=k == 0, stop=k == 1)
                    return last
                return product

            pe.wait_ge(ld_gat, 64)
            tiles(0, with_weights(Wg, D))

            def spread_numbers(banks):
                for k, bk in banks:
                    last = mm(bank[bk][:, :], ones[:, :], diag[:, k, :, :].rearrange("p q n -> p (q n)"), start=True, stop=True)
                return last

            def pick(b0):
                for j in range(Q):
                    last = mm(bank[b0 + j // 2][:, (j % 2) * T * 8:(j % 2 + 1) * T * 8], owner[0:P, j, :],
                              uv[:, :, :].rearrange("p t c -> p (t c)"), start=True, stop=True)
                return last

            rows = ((0, 0), (1, 1), (2, 6))
            pe.wait_ge(diag_rdy, 1)
            spread_numbers(rows).then_inc(bc_rdy, 1)
            pe.wait_ge(own_rdy, 1)
            pe.wait_ge(prep, 1)
            pick(6).then_inc(pick_mm, 1)
            with pe.Fori(0, B1 // 2) as it:
                for s in range(2):
                    b = it * 2 + s
                    pe.wait_ge(diag_rdy, b + 2)
                    pe.wait_ge(prep, b + 1)
                    pe.wait_ge(pick_done, b + 1)
                    spread_numbers(rows).then_inc(bc_rdy, 1)
                    pe.wait_ge(msg_rdy, b + 1)
                    pe.wait_ge(msum_rdy, b + 1)
                    for j in range(Q):
                        last = mm(bank[2 + j][:, 0:MSG], same[:, s, j, :], msg[:, s, j, :], start=True, stop=True)
                    last.then_inc(agg_rdy, 1)
                    pe.wait_ge(own_rdy, b + 2)
                    pick(6).then_inc(pick_mm, 1)

            pe.wait_ge(ld_rt, 128)
            tiles(1, with_weights(W16, 16))

            for_router = bank[0]
            zero_l, zero_r = RD[:, 0:P], RD[:, 0:T * 20]
            pe.sem_inc(spread_used, 2)
            pe.wait_ge(rt_tab_rdy, 1)
            mm(for_router[0:P, 0:T * 20], zero_l, zero_r, start=True, stop=False, skip_group_check=True).then_inc(rt_agg, 1)
            rows2 = ((0, 1),)
            pe.wait_ge(diag2_rdy, 1)
            spread_numbers(rows2).then_inc(bc2_rdy, 1)
            pe.wait_ge(own2_rdy, 1)
            pick(2).then_inc(pick2_mm, 1)
            pe.wait_ge(diag2_rdy, 2)
            spread_numbers(rows2).then_inc(bc2_rdy, 1)
            with pe.Fori(0, B2 // 2) as it:
                for s in range(2):
                    b = it * 2 + s
                    pe.wait_ge(diag2_rdy, b + 3)
                    pe.wait_ge(own2_rdy, b + 2)
                    spread_numbers(rows2).then_inc(bc2_rdy, 1)
                    pe.wait_ge(pick2_done, b + 1)
                    pick(2).then_inc(pick2_mm, 1)
                    pe.wait_ge(spread_rdy, b + 1)
                    for j in range(Q):
                        last = mm(for_router[0:P, 0:T * 20], onep[:, s, j, :],
                                  spread[:, s, j, :, :].rearrange("p t c -> p (t c)"), start=False, stop=False, skip_group_check=True)
                    last.then_inc(spread_used, 1)
            mm(for_router[0:P, 0:T * 20], zero_l, zero_r, start=False, stop=True, skip_group_check=True).then_inc(rt_agg, 1)

            def experts(i, n_e, n_m, w1, w2):
                s = EX[i]
                with pe.Fori(0, G) as g:
                    def up(e):
                        for m in range(n_m):
                            c = e * n_m + m
                            a = 2 * (c % 2)
                            pe.wait_ge(s["act"], g * (n_e * n_m) + (c + 1))
                            for lo, width, bk in ((0, 3 * P, a), (3 * P, 2 * P, a + 1)):
                                for k in range(2):
                                    last = mm(bank[bk][:, 0:width], w1[:, e, k, m * 128:(m + 1) * 128],
                                              XT[:, k, bass.ds(g * (J * P) + lo, width)], start=k == 0, stop=k == 1)
                            last.then_inc(s["up"], 1)

                    def down(e):
                        pe.wait_ge(s["act"], g * (n_e * n_m) + ((e + 1) * n_m + 2))
                        for j in range(J):
                            c = e * J + j
                            pe.wait_ge(s["acc"], g * (n_e * J) + (c + 1))
                            for m in range(n_m):
                                last = mm(bank[4 + c % 2][0:P, 0:D], hh[:, e % 2, m, j * P:(j + 1) * P], w2[:, e, m, :],
                                          start=m == 0, stop=m == n_m - 1)
                            last.then_inc(s["dn"], 1)

                    up(0)
                    for e in range(n_e):
                        if e + 1 < n_e:
                            up(e + 1)
                        down(e)

            pe.wait_ge(ld_f0, LD_F0)
            pe.wait_ge(gate_rdy, 1)
            experts(0, 4, 4, FW[:, 0:4096].rearrange("p (e k n) -> p e k n", e=4, k=2),
                    FW[:, 4096:8192].rearrange("p (e k n) -> p e k n", e=4, k=4))

            pe.sem_inc(pc_free, KQ - 1)
            pe.sem_inc(ag_mm, 1)
            pe.wait_ge(mg_sum, MERGES)
            with pe.Fori(0, NG) as g:
                pe.wait_ge(deg_ev, g + 1)
                mm(bank[7][:, 0:CW], ones[0:P, :], RD[0:P, bass.ds(g * CW, CW)], start=True, stop=True).then_inc(deg_mm, 1)

            pe.wait_ge(ld_gn, LD_GN)
            pe.wait_ge(ld_win, 16)
            tiles(2)
            pe.wait_ge(S[2]["xT"], T + 2)
            with pe.Fori(0, NG) as g:
                pe.wait_ge(in_ev, g + 1)
                for f in range(2):
                    for k in range(2):
                        last = mm(bank[2 + f][:, 0:CW], Win[:, k, f * 128:(f + 1) * 128], XT[:, k, bass.ds(g * CW, CW)], start=k == 0, stop=k == 1)
                last.then_inc(in_mm, 1)
            pe.wait_ge(in_ev, NG + 1)

            def tile_cols(k, t):
                return XT[:, k, 0:N].rearrange("p (a t) -> p t a", t=T)[:, t, :]

            pe.wait_ge(rd_done, 1)
            largest = pe.value_load(flag[0:1, 0:1])
            with pe.Fori(0, 3) as l:
                pe.wait_ge(gn_rel, l * NG + 1)
                for t in range(T):
                    pe.wait_ge(z_ev, l * T + free(t, t))
                    for k in range(2):
                        last = mm(bank[t % 2][0:P, 0:D], tile_cols(k, t), Wagg[:, bass.ds(l, 1), k, :].rearrange("p o n -> p (o n)"), start=k == 0, stop=k == 1)
                    last.then_inc(z_mm, 1)
                pe.wait_ge(z_ev, l * T + (T + 2))
                pe.wait_ge(ld_wself, l * 16 + 16)
                pe.sem_inc(pe_steps, 1)
                with pe.Fori(0, NG) as g:
                    q = l * NG + g

                    def aggregate(dt):
                        for k in range(KQ):
                            pe.wait_ge(pc_ld[k], q * 16 + 16)
                            for r in range(KQ):
                                t = KQ * k + r
                                for f in range(2):
                                    for z in (Z_hi, Z_lo):
                                        last = mm(bank[4 + f][:, 0:CW], z[:, t, f * 128:(f + 1) * 128].bitcast(dt), piece[k][:, r, :].bitcast(dt),
                                                  start=t == 0 and z is Z_hi, stop=t == T - 1 and z is Z_lo)
                            last.then_inc(pc_free if k < KQ - 1 else ag_mm, 1)

                    pe.wait_ge(ag_read, q + 1)
                    pe.sem_inc(pe_steps, 1)
                    with pe.If(largest < EXACT):
                        aggregate(F32R)
                    with pe.If(largest >= EXACT):
                        aggregate(FP32)
                    pe.wait_ge(gn_sum, q + 1)
                    for f in range(2):
                        for k in range(2):
                            last = mm(bank[6 + f][:, 0:CW], Wself[:, k, f * 128:(f + 1) * 128], XT[:, k, bass.ds(g * CW, CW)], start=k == 0, stop=k == 1)
                    last.then_inc(gn_mm, 1)
            pe.wait_ge(gn_rel, 3 * NG + 1)
            pe.wait_ge(ld_wout, 16)
            for t in range(T):
                pe.wait_ge(o_acc, free(t, t))
                for k in range(2):
                    last = mm(bank[t % 2][0:P, 0:D], tile_cols(k, t), Wout[:, k, :], start=k == 0, stop=k == 1)
                last.then_inc(o_mm, 1)

            tiles(3, with_weights(Wr, 8))
            pe.wait_ge(ld_f1, LD_F1)
            pe.wait_ge(gate1_rdy, 1)
            experts(1, 8, 2, FW[:, 0:4096].rearrange("p (e k n) -> p e k n", e=8, k=2),
                    FW[:, 4096:8192].rearrange("p (e k n) -> p e k n", e=8, k=2))

        @block.scalar
        def _(act):
            step = Chain(act, act_chain)
            fn = act.activation

            def root(i):
                act.wait_ge(ln_var, i + 1)
                fn(ln[:, 3, :], ln[:, 2, :], ACT.Sqrt).then_inc(ln_std, 1)

            def tiles(i, wide=None, store=None):
                s = S[i]
                act.sem_inc(s["xT"], 2)
                if store:
                    act.sem_inc(s["hev"], 2)
                with act.Fori(0, G) as g:
                    def copy(j):
                        n = g * J + j
                        act.wait_ge(s["tr"], n + 6)
                        if store:
                            act.wait_ge(s["h"], free(n, j))
                        got = bank[j % 2][:, 0:2 * P].rearrange("p (k n) -> p k n", k=2)
                        if wide:
                            last = fn(wide(n), got, ACT.Copy)
                        if store:
                            last = fn(xT_s[:, j % 2, :, :], got, ACT.Copy)
                        last.then_inc(s["xT"], 1)

                    def take(j):
                        n = g * J + j
                        act.wait_ge(s["h"], n + 3)
                        store(j, n).then_inc(s["hev"], 1)

                    for j in range(J):
                        copy(j)
                        if store and j:
                            take(j - 1)
                    if store:
                        take(J - 1)

            root(0)
            tiles(0, store=lambda j, n: fn(tab_h[:, n, :, 0:64], bank[2 + j % 2][0:P, 0:D].rearrange("p (h c) -> p h c", h=HEADS), ACT.Copy))

            def factors():
                for k, scale in ((4, 0.8), (5, 0.2), (6, 0.8), (7, -0.8)):
                    source = small[:, 2 if k < 6 else 3 if k == 6 else 8, :, :]
                    last = fn(small[:, k, :, :], source, ACT.Exp, scale=scale)
                last.then_inc(f_out, 1)

            act.wait_ge(f_in, 1)
            factors()

            act.sem_inc(msum_rdy, 1)

            def diagonals(b, numbers, ready):
                for k, a in enumerate(numbers):
                    for j in range(Q):
                        last = fn(diag[:, k, j, :], ident[:, :], ACT.Copy, scale=a[:, bass.ds(b * Q + j, 1)] if not isinstance(b, int) else a[:, b * Q + j:b * Q + j + 1])
                last.then_inc(ready, 1)

            act.wait_ge(idx_dve, 1)
            act.wait_ge(consts, 13)
            numbers1 = (dst_f, key_f, dst_p)
            diagonals(0, numbers1, diag_rdy)
            with act.Fori(0, B1 // 2) as it:
                for s in range(2):
                    b = it * 2 + s
                    act.wait_ge(bc_rdy, b + 1)
                    diagonals(b + 1, numbers1, diag_rdy)
                    act.wait_ge(agg_rdy, b + 1)
                    for j in range(Q):
                        last = fn(msum[:, s, j, :], bank[2 + j][:, 0:MSG], ACT.Copy)
                    last.then_inc(msum_rdy, 1)

            root(1)
            tmajor = XT[:, :, 0:N].rearrange("p k (t n) -> p k t n", n=P)
            tiles(1, wide=lambda n: tmajor[:, :, n, :],
                  store=lambda j, n: fn(s16[:, 0, n, :], bank[2 + j % 2][0:P, 0:16], ACT.Copy))
            act.wait_ge(f_in, 2)
            factors()
            act.wait_ge(rt_tab_rdy, 1)
            diagonals(0, (pd,), diag2_rdy)
            act.wait_ge(bc2_rdy, 1)
            diagonals(1, (pd,), diag2_rdy)
            with act.Fori(0, B2 // 2) as it:
                for s in range(2):
                    act.wait_ge(bc2_rdy, it * 2 + s + 2)
                    diagonals(it * 2 + s + 2, (pd,), diag2_rdy)
            act.wait_ge(ln_var, 3)
            fn(ln[:, 3, :], ln[:, 2, :], ACT.Sqrt).then_inc(ln_std, 1)
            act.wait_ge(f_in, 3)
            fn(small[:, 1, :, :], small[:, 1, :, :], ACT.Exp).then_inc(f_out, 1)

            def experts(i, n_e, n_m):
                s = EX[i]
                act.sem_inc(s["act"], 2)
                with act.Fori(0, G) as g:
                    for e in range(n_e):
                        u = e % 2
                        for m in range(n_m):
                            c = e * n_m + m
                            a = 2 * (c % 2)
                            act.wait_ge(s["up"], g * (n_e * n_m) + (c + 1))
                            for lo, width, bk in ((0, 3 * P, a), (3 * P, 2 * P, a + 1)):
                                last = fn(hh[:, u, m, lo:lo + width], bank[bk][:, 0:width], ACT.Gelu, bias=b1_T[:, c:c + 1])
                            last.then_inc(s["act"], 1)

            act.wait_ge(gate_rdy, 1)
            act.wait_ge(ld_f0, LD_F0)
            experts(0, 4, 4)

            root(3)
            natural = XT[:, :, 0:N].rearrange("p k (n t) -> p k t n", t=T)
            act.wait_ge(EX[0]["dn"], G * 4 * J)
            tiles(2, wide=lambda n: natural[:, :, n, :])
            act.wait_ge(ld_gn, LD_GN)
            act.sem_inc(in_ev, 1)
            with act.Fori(0, NG) as g:
                act.wait_ge(in_mm, g + 1)
                for f in range(2):
                    last = fn(XT[:, f, bass.ds(g * CW, CW)], bank[2 + f][:, 0:CW], ACT.Identity, bias=bin_T[:, f:f + 1])
                last.then_inc(in_ev, 1)
            act.sem_inc(gn_rel, 1)
            for k in range(2):
                act.wait_ge(mg_st[k], 16 * (T + 1))
            with act.Fori(0, 3) as l:
                for t in range(T):
                    act.wait_ge(z_mm, l * T + (t + 1))
                    fn(Z_hi[:, t, :], bank[t % 2][0:P, 0:D], ACT.Copy).then_inc(z_hi, 1)
                with act.Fori(0, NG) as g:
                    act.wait_ge(gn_sum, l * NG + g + 2)
                    for f in range(2):
                        last = fn(XT[:, f, bass.ds(g * CW, CW)], XT[:, f, bass.ds(g * CW, CW)], ACT.Relu, bias=bhid_T[:, bass.ds(l, 1), f])
                    last.then_inc(gn_rel, 1)

            root(4)
            tiles(3, wide=lambda n: tmajor[:, :, n, :],
                  store=lambda j, n: fn(gates[:, n, :], bank[2 + j % 2][0:P, 0:8], ACT.Copy))
            act.wait_ge(f_in, 4)
            fn(gates[:, :, :], gates[:, :, :], ACT.Exp).then_inc(f_out, 1)
            act.wait_ge(ld_f1, LD_F1)
            experts(1, 8, 2)

        @block.vector
        def _(dve):
            step = Chain(dve, dve_chain)
            tt, ts, stt = dve.tensor_tensor, dve.tensor_scalar, dve.scalar_tensor_tensor

            def cast(shape, a, axis):
                return a.unsqueeze(axis).to_broadcast(shape)

            dve.wait_ge(consts, 13)
            dve.tensor_copy(iota_f[:, :], iota_i[:, :])
            step(dve.tensor_copy(pidx_f[:, :], pidx_i[:, :]))
            ts(dupw[:, :], lower[:, :], TRASH_MARK, 1.0, ALU.mult, ALU.add).then_inc(consts2, 1)
            dve.wait_ge(ld_edges, 64)
            dve.tensor_copy(src_f, e_src)
            step(dve.tensor_copy(dst_f, e_dst))
            step(stt(key_f, dst_f, float(CC), src_f, ALU.mult, ALU.add))
            ts(off_row, dst_f, -1.0, pidx_f[:, 0:1], ALU.mult, ALU.add)
            step(ts(off_cell, key_f, -1.0, pidx_f[:, 1:2], ALU.mult, ALU.add))
            def divide(n, p, t, tmp, whole):
                step(ts(tmp, n, 0.5, 1.0 / T, ALU.add, ALU.mult))
                step(ts(tmp, tmp, -0.5, None, ALU.add))
                step(dve.tensor_copy(whole, tmp))
                step(dve.tensor_copy(p, whole))
                step(stt(t, p, -float(T), n, ALU.mult, ALU.add))
                step(ts(tmp, t, float(T), None, ALU.is_ge))
                step(tt(p, p, tmp, ALU.add))
                step(stt(t, tmp, -float(T), t, ALU.mult, ALU.add))

            divide(dst_f, dst_p, dst_t, div_f, div_i)
            dve.sem_inc(idx_dve, 1)

            def norm_stats(i):
                with step.loop(G, 1) as g:
                    for j in range(J):
                        last = dve.bn_stats(stats[:, bass.ds(g * J + j, 1), :].rearrange("p o c -> p (o c)"), X[:, bass.ds(g * J + j, 1), :].rearrange("p o c -> p (o c)"))
                    step(last)
                me, ve, mo, vo = stats[:, :, 1], stats[:, :, 2], stats[:, :, 4], stats[:, :, 5]
                tt(ln[:, 0, :], me, mo, ALU.add)
                tt(ln[:, 1, :], me, mo, ALU.subtract)
                step(tt(ln[:, 2, :], ve, vo, ALU.add))
                step(tt(ln[:, 1, :], ln[:, 1, :], ln[:, 1, :], ALU.mult))
                ts(ln[:, 0, :], ln[:, 0, :], 0.5, None, ALU.mult)
                ts(ln[:, 1, :], ln[:, 1, :], 0.25, 1e-5, ALU.mult, ALU.add)
                step(ts(ln[:, 2, :], ln[:, 2, :], 1.0 / D, None, ALU.mult))
                tt(ln[:, 2, :], ln[:, 2, :], ln[:, 1, :], ALU.add).then_inc(ln_var, 1)
                rsqrt(i)

            def rsqrt(i):
                dve.wait_ge(ln_std, i + 1)
                step(dve.reciprocal(ln[:, 4, :], ln[:, 3, :]))
                step(tt(ln[:, 4, :], ln[:, 4, :], ln[:, 2, :], ALU.mult))
                step(tt(ln[:, 4, :], ln[:, 4, :], ln[:, 3, :], ALU.add))
                step(dve.reciprocal(ln[:, 4, :], ln[:, 4, :]))
                step(ts(ln[:, 5, :], ln[:, 4, :], 2.0, None, ALU.mult))

            def normalised(i, g):
                for j in range(J):
                    n = g * J + j
                    dve.wait_ge(S[i]["tr"], n + 1)
                    ts(xn_s[:, j, :], X[:, n, :], ln[:, 0, bass.ds(n, 1)], ln[:, 5, bass.ds(n, 1)],
                       ALU.subtract, ALU.mult).then_inc(S[i]["xn"], 1)

            def heads(k):
                return small[:, k, :, :]

            def factors(turn):
                dve.tensor_reduce(amax[:, 0, :], heads(0).rearrange("p t h -> p h t"), AX, ALU.max).then_inc(mx, 1)
                dve.wait_ge(mxr, turn)
                top = cast([P, T, HEADS], amax[:, 1, :], 1)
                tt(heads(2), heads(0), top, ALU.subtract)
                step(tt(heads(3), heads(1), top, ALU.add))
                step(ts(heads(8), heads(3), 0.0, None, ALU.max))
                ts(heads(3), heads(3), 0.0, None, ALU.min).then_inc(f_in, 1)
                dve.wait_ge(f_out, turn)
                dve.tensor_copy(uv[:, :, 0:4], heads(6))
                dve.tensor_copy(uv[:, :, 4:8], heads(7))
                step(tt(heads(9), heads(4), heads(6), ALU.mult))
                step(tt(heads(9), heads(9), heads(7), ALU.max))

            dve.wait_ge(ld_x, 16)
            norm_stats(0)
            dve.wait_ge(ld_gat, 64)
            att_scr = BIG2[0:P, 0:2 * D].rearrange("p (k n) -> p k n", k=2)
            with step.loop(G, 2 * J) as g:
                normalised(0, g)
                for j in range(J):
                    n = g * J + j
                    dve.wait_ge(S[0]["hev"], n + 3)
                    for k, row in enumerate((row_as, row_ad)):
                        last = tt(att_scr[:, k, :].rearrange("p (h c) -> p h c", h=HEADS), tab_h[:, n, :, 0:64],
                                  row[:, :].rearrange("p (h c) -> p h c", h=HEADS), ALU.mult)
                    step(last)
                    step(dve.tensor_reduce(small[:, 0:2, n, :], att_scr.rearrange("p k (h c) -> p k h c", c=64), AX, ALU.add))
            factors(1)
            dve.wait_ge(S[0]["hev"], T + 2)
            dve.tensor_copy(tab[:, :, MSG:TAB], heads(4))
            dve.tensor_copy(tab_h[:, :, :, 64], heads(5))
            part = tab_h[:, :, :, 0:64]
            step(tt(part, part, cast([P, T, HEADS, 64], heads(5), 3), ALU.mult))
            dve.sem_inc(tab_rdy, 1)

            def numbers(s, b, e, ready):
                cols = bass.ds(b * Q, Q) if not isinstance(b, int) else slice(b * Q, b * Q + Q)
                dve.tensor_copy(slot_i[:, s, 0, :], e[:, cols]).then_inc(ready, 1)

            def owners(b, bk, t, ready, s):
                cols = bass.ds(b * Q, Q) if not isinstance(b, int) else slice(b * Q, b * Q + Q)
                ts(owner[0:P, :, :], bank[bk][0:P, :].rearrange("p (q n) -> p q n", q=Q), lane[0:P, 0:1], None, ALU.is_equal).then_inc(ready, 1)
                return tt(onet[:, s, :, :], cast([128, Q, T], iota_f[:, 0:T], 1), cast([128, Q, T], t[:, cols], 2), ALU.is_equal)

            def pick(b0, done, s):
                for h in range(2):
                    last = tt(picked[:, 2 * h:2 * h + 2, :, :], bank[b0 + h][:, 0:2 * T * 8].rearrange("p (q t c) -> p q t c", q=2, t=T),
                              cast([128, 2, T, 8], onet[:, s, 2 * h:2 * h + 2, :], 3), ALU.mult)
                step(last)
                dve.sem_inc(done, 1)
                step(dve.tensor_reduce(uve[:, :, :], picked.rearrange("p q t c -> p q c t"), AX, ALU.add))

            def weights(s, factors):
                step(tt(wgt[:, s, :, :], factors, uve[:, :, 0:4], ALU.mult))
                step(tt(wgt[:, s, :, :], wgt[:, s, :, :], uve[:, :, 4:8], ALU.max))

            def prepare(s, b, scattered):
                cols = bass.ds(b * Q, Q) if not isinstance(b, int) else slice(b * Q, b * Q + Q)
                shape = [128, Q, 128]
                f = lambda k: slot_f[:, s, k, :]
                owners(b, 6, dst_t, own_rdy, s)
                tt(same[:, s, :, :], bank[0][:, :].rearrange("p (q n) -> p q n", q=Q), cast(shape, dst_f[:, cols], 2), ALU.is_equal)
                step(tt(samek, bank[1][:, :].rearrange("p (q n) -> p q n", q=Q), cast(shape, key_f[:, cols], 2), ALU.is_equal))
                tt(scr, same[:, s, :, :], cast(shape, lower[:, :], 1), ALU.mult)
                step(tt(samek, samek, cast(shape, dupw[:, :], 1), ALU.mult))
                dve.tensor_reduce(f(1), scr, AX, ALU.add)
                step(dve.tensor_reduce(f(4), samek, AX, ALU.add))
                stt(f(2), f(1), 0.0, off_row[:, cols], ALU.is_gt, ALU.mult)
                step(stt(f(3), f(4), TRASH_MARK, off_cell[:, cols], ALU.is_ge, ALU.mult))
                if scattered is not None:
                    dve.wait_ge(sc_done, scattered)
                dve.tensor_copy(f(0), f(4))
                tt(slot_i[:, s, 1, :], f(2), dst_f[:, cols], ALU.add)
                tt(slot_i[:, s, 2, :], f(3), key_f[:, cols], ALU.add).then_inc(prep, 1)

            numbers(0, 0, e_src, gidx)
            numbers(1, 1, e_src, gidx)
            dve.wait_ge(bc_rdy, 1)
            dve.wait_ge(consts2, 1)
            prepare(0, 0, None)
            with step.loop(B1 // 2, 16) as it:
                for s in range(2):
                    b = it * 2 + s
                    dve.wait_ge(pick_mm, b + 1)
                    pick(6, pick_done, s)
                    dve.wait_ge(gat_s[s], it * 64 + 64)
                    numbers(s, b + 2, e_src, gidx)
                    weights(s, gath[:, s, :, MSG:TAB])
                    dve.wait_ge(msum_rdy, b + 1)
                    tt(msg[:, s, :, :].rearrange("p q (h c) -> p q h c", c=65),
                       gath[:, s, :, 0:MSG].rearrange("p q (h c) -> p q h c", c=65),
                       cast([128, Q, HEADS, 65], wgt[:, s, :, :], 3), ALU.mult).then_inc(msg_rdy, 1)
                    dve.wait_ge(bc_rdy, b + 2)
                    prepare(1 - s, b + 1, b + 1)
            dve.wait_ge(ld_sums, 32)
            dve.wait_ge(tab_st, 16)
            tot = BIG2[0:P, 0:T * MSG]
            step(tt(tab_h, tab_h, cast([P, T, HEADS, 65], heads(9), 3), ALU.mult))
            step(tt(tot, tot, sums1_sb, ALU.add))
            step(tt(sums_sb, sums_sb, tab_h, ALU.add))
            step(ts(heads(4), sums_sb[:, :, :, 64], 1e-30, None, ALU.max))
            step(dve.reciprocal(heads(5), heads(4)))
            step(tt(hrow, sums_sb[:, :, :, 0:64], cast([P, T, HEADS, 64], heads(5), 3), ALU.mult))
            step(tt(hid1, hid1, cast([P, T, D], row_b[:, :], 1), ALU.add))
            flat = lambda a: a.rearrange("p t c -> p (t c)")
            step(stt(flat(X[:, :, :]), flat(hid1), 0.0, flat(X[:, :, :]), ALU.max, ALU.add))
            dve.sem_inc(sums_free, 1)

            norm_stats(1)
            with step.loop(G, 0) as g:
                normalised(1, g)
            dve.wait_ge(S[1]["hev"], T + 2)
            dve.wait_ge(ld_rt, 128)
            for k in range(2):
                step(tt(s16[:, 1, :, :], s16[:, 0, :, :], cast([P, T, 16], row16[:, k, :], 1), ALU.mult))
                step(dve.tensor_reduce(heads(k), s16[:, 1, :, :].rearrange("p t (h c) -> p t h c", c=4), AX, ALU.add))
            factors(2)
            own2 = tab2[:, :, 0:20].rearrange("p t (h c) -> p t h c", c=5)
            dve.tensor_copy(tab2[:, :, 20:24], heads(4))
            dve.tensor_copy(own2[:, :, :, 4], heads(5))
            step(tt(own2[:, :, :, 0:4], s16[:, 0, :, :].rearrange("p t (h c) -> p t h c", c=4), cast([P, T, HEADS, 4], heads(5), 3), ALU.mult))
            step(dve.tensor_copy(dd, e_dst2[:, :]))
            divide(dd, pd, td, halves, e_half)
            dve.sem_inc(rt_tab_rdy, 1)

            numbers(0, 0, e_src2, gidx2)
            numbers(1, 1, e_src2, gidx2)
            dve.wait_ge(bc2_rdy, 1)
            step(owners(0, 1, td, own2_rdy, 0))
            with step.loop(B2 // 2, 12) as it:
                for s in range(2):
                    b = it * 2 + s
                    cols = bass.ds(b * Q, Q)
                    dve.wait_ge(pick2_mm, b + 1)
                    pick(2, pick2_done, s)
                    dve.wait_ge(bc2_rdy, b + 2)
                    owners(b + 1, 1, td, own2_rdy, 1 - s)
                    dve.wait_ge(gat2_s[s], it * 64 + 64)
                    weights(s, gath2[:, s, :, 20:24])
                    tt(msg2.rearrange("p q (h c) -> p q h c", c=5), gath2[:, s, :, 0:20].rearrange("p q (h c) -> p q h c", c=5),
                       cast([128, Q, HEADS, 5], wgt[:, s, :, :], 3), ALU.mult)
                    dve.wait_ge(spread_used, b + 1)
                    step(tt(onep[:, s, :, :], cast([128, Q, P], iota_f[:, :], 1), cast([128, Q, P], pd[:, cols], 2), ALU.is_equal))
                    numbers(s, b + 2, e_src2, gidx2)
                    for j in range(Q):
                        last = tt(spread[:, s, j, :, :], cast([128, T, 20], onet[:, s, j, :], 2), cast([128, T, 20], msg2[:, j, :], 1), ALU.mult)
                    step(last)
                    dve.sem_inc(spread_rdy, 1)
            dve.wait_ge(pick2_mm, B2 + 1)
            dve.wait_ge(rt_agg, 2)
            for s in range(2):
                dve.wait_ge(gat2_s[s], 64 * (B2 // 2 + 1))
            got = bank[0][0:P, 0:T * 20].rearrange("p (t h c) -> p t h c", h=HEADS, c=5)
            step(tt(own2, own2, cast([P, T, HEADS, 5], heads(9), 3), ALU.mult))
            step(tt(own2, own2, got, ALU.add))
            step(ts(heads(4), own2[:, :, :, 4], 1e-30, None, ALU.max))
            step(dve.reciprocal(heads(5), heads(4)))
            agg, dev, sq = (s16[:, k, :, :] for k in range(3))
            step(tt(agg.rearrange("p t (h c) -> p t h c", c=4), own2[:, :, :, 0:4], cast([P, T, HEADS, 4], heads(5), 3), ALU.mult))
            step(tt(agg, agg, cast([P, T, 16], row16[:, 2, :], 1), ALU.add))
            step(dve.tensor_reduce(ln[:, 0, :], agg, AX, ALU.add))
            step(ts(ln[:, 0, :], ln[:, 0, :], 1.0 / 16, None, ALU.mult))
            step(tt(dev, agg, cast([P, T, 16], ln[:, 0, :], 2), ALU.subtract))
            step(tt(sq, dev, dev, ALU.mult))
            step(dve.tensor_reduce(ln[:, 1, :], sq, AX, ALU.add))
            ts(ln[:, 2, :], ln[:, 1, :], 1.0 / 16, 1e-5, ALU.mult, ALU.add).then_inc(ln_var, 1)
            rsqrt(2)
            step(tt(dev, dev, cast([P, T, 16], ln[:, 5, :], 2), ALU.mult))
            step(tt(dev, dev, cast([P, T, 16], row16[:, 3, :], 1), ALU.mult))
            step(tt(dev, dev, cast([P, T, 16], row16[:, 4, :], 1), ALU.add))
            step(dve.tensor_reduce(heads(0), dev.rearrange("p t (h e) -> p t e h", h=HEADS), AX, ALU.add))
            step(ts(heads(0), heads(0), 1.0 / HEADS, None, ALU.mult))

            def top_two(scores, n_e, sel):
                shape = [P, T, n_e, n_e]
                a = rank_a[:, 0:T * n_e * n_e].rearrange("p (t e f) -> p t e f", e=n_e, f=n_e)
                b = rank_b[:, 0:T * n_e * n_e].rearrange("p (t e f) -> p t e f", e=n_e, f=n_e)
                mine, other = cast(shape, scores, 3), cast(shape, scores, 2)
                tt(a, other, mine, ALU.is_gt)
                step(tt(b, other, mine, ALU.is_equal))
                for e in range(n_e):
                    last = tt(b[:, :, e, :], b[:, :, e, :], cast([P, T, n_e], tie[0:P, e, 0:n_e], 1), ALU.mult)
                step(last)
                step(tt(a, a, b, ALU.add))
                step(dve.tensor_reduce(sel, a, AX, ALU.add))
                step(ts(sel, sel, 2.0, None, ALU.is_lt))

            top_two(heads(0), 4, heads(2))
            step(dve.tensor_reduce(ln[:, 0, :], heads(0), AX, ALU.max))
            tt(heads(1), heads(0), cast([P, T, 4], ln[:, 0, :], 2), ALU.subtract).then_inc(f_in, 1)
            dve.wait_ge(f_out, 3)
            step(tt(heads(1), heads(1), heads(2), ALU.mult))
            step(dve.tensor_reduce(ln[:, 0, :], heads(1), AX, ALU.add))
            step(dve.reciprocal(ln[:, 0, :], ln[:, 0, :]))
            step(tt(gates[:, :, 0:4], heads(1), cast([P, T, 4], ln[:, 0, :], 2), ALU.mult))
            dve.sem_inc(gate_rdy, 1)

            def merge(g, i):
                dve.wait_ge(mg_ld[i % 2], g * (16 * MERGES // G) + 32 * (i // 2 + 1))
                part = RD[0:P, (i % 2) * HALF:(i % 2 + 1) * HALF]
                step(tt(merge_a[i % 2], merge_a[i % 2], merge_b[i % 2], ALU.add))
                step(tt(part, part, merge_a[i % 2], ALU.add))
                dve.sem_inc(mg_sum, 1)

            def experts(i, n_e, beside=None, per=0):
                s = EX[i]
                dve.sem_inc(s["acc"], 2)
                with step.loop(T, n_e) as t:
                    for e in range(n_e):
                        step(stt(X[:, t, :], b2_bc[:, e, :], gates[:, t, e:e + 1], X[:, t, :], ALU.mult, ALU.add))
                with step.loop(G, per) as g:
                    for e in range(n_e):
                        for j in range(J):
                            c = e * J + j
                            if beside and c % 2:
                                beside(g, c // 2)
                            n = g * J + j
                            dve.wait_ge(s["dn"], g * (n_e * J) + (c + 1))
                            if e:
                                dve.wait_ge(s["acc"], g * (n_e * J) + (c - J + 3))
                            stt(X[:, n, :], bank[4 + c % 2][0:P, 0:D], gates[:, n, e:e + 1], X[:, n, :], ALU.mult, ALU.add).then_inc(s["acc"], 1)
                dve.wait_ge(s["acc"], G * n_e * J + 2)

            dve.wait_ge(ld_f0, LD_F0)
            experts(0, 4, merge, 4 * MERGES // G // 2)
            dve.sem_inc(f0_done, 1)
            dve.sem_inc(deg_ev, 1)
            with step.loop(NG, 1) as g:
                cols = RD[:, bass.ds(g * CW, CW)]
                dve.wait_ge(deg_mm, g + 1)
                step(ts(cols, bank[7][:, 0:CW], 1.0, None, ALU.max))
                dve.sem_inc(deg_ev, 1)
            step(dve.tensor_reduce(flag[:, 0:1], RD[:, :], AX, ALU.max))
            step(dve.reciprocal(RD[:, :], RD[:, :]))
            dve.sem_inc(rd_done, 1)

            norm_stats(3)
            with step.loop(G, 0) as g:
                normalised(2, g)
            dve.sem_inc(gn_sum, 1)
            dve.sem_inc(ag_read, 1)
            dve.sem_inc(z_ev, 2)
            with step.loop(3, NG) as l:
                for t in range(T):
                    dve.wait_ge(z_hi, l * T + (t + 1))
                    tt(Z_lo[:, t, :], bank[t % 2][0:P, 0:D], Z_hi[:, t, :].bitcast(FP32), ALU.subtract).then_inc(z_ev, 1)
                with step.loop(NG, 1) as g:
                    q = l * NG + g
                    cols = bass.ds(g * CW, CW)
                    dve.wait_ge(ag_mm, q + 2)
                    dve.wait_ge(gn_sum, q + 1)
                    for f in range(2):
                        last = tt(scr_g[:, f, :], bank[4 + f][:, 0:CW], RD[:, cols], ALU.mult)
                    step(last)
                    dve.sem_inc(ag_read, 1)
                    dve.wait_ge(gn_mm, q + 2)
                    for f in range(2):
                        last = tt(XT[:, f, cols], scr_g[:, f, :], bank[6 + f][:, 0:CW], ALU.add)
                    last.then_inc(gn_sum, 1)
            dve.sem_inc(o_acc, 2)
            dve.wait_ge(ld_f1, LD_F1)
            with step.loop(T, 1) as t:
                step(tt(X[:, t, :], X[:, t, :], row_b[:, :], ALU.add))
            for t in range(T):
                dve.wait_ge(o_mm, t + 1)
                tt(X[:, t, :], bank[t % 2][0:P, 0:D], X[:, t, :], ALU.add).then_inc(o_acc, 1)
            dve.wait_ge(o_acc, T + 2)

            norm_stats(4)
            with step.loop(G, 1) as g:
                normalised(3, g)
                dve.wait_ge(S[3]["xn"], g * J + J)
                for j in range(J):
                    n = g * J + j
                    last = tt(X[:, n, :], X[:, n, :], xn_s[:, j, :], ALU.add)
                step(last)
            dve.wait_ge(S[3]["hev"], T + 2)
            g8 = gates[:, :, :]
            step(dve.tensor_reduce(ln[:, 0, :], g8, AX, ALU.max))
            tt(g8, g8, cast([P, T, 8], ln[:, 0, :], 2), ALU.subtract).then_inc(f_in, 1)
            dve.wait_ge(f_out, 4)
            step(dve.tensor_reduce(ln[:, 0, :], g8, AX, ALU.add))
            step(dve.reciprocal(ln[:, 0, :], ln[:, 0, :]))
            step(tt(g8, g8, cast([P, T, 8], ln[:, 0, :], 2), ALU.mult))
            top_two(g8, 8, uv[:, :, :])
            step(tt(g8, g8, uv[:, :, :], ALU.mult))
            step(dve.tensor_reduce(ln[:, 0, :], g8, AX, ALU.add))
            step(ts(ln[:, 0, :], ln[:, 0, :], 1e-12, None, ALU.max))
            step(dve.reciprocal(ln[:, 0, :], ln[:, 0, :]))
            step(tt(g8, g8, cast([P, T, 8], ln[:, 0, :], 2), ALU.mult))
            dve.sem_inc(gate1_rdy, 1)
            dve.wait_ge(ld_b2, 16)
            experts(1, 8)
            dve.sem_inc(all_done, 1)


_INS = ["x", "src", "dst", "L0_gnn_W", "L0_gnn_att_src", "L0_gnn_att_dst", "L0_gnn_bias", "L0_ffn_W_gat",
        "L0_ffn_att_src", "L0_ffn_att_dst", "L0_ffn_b_gat", "L0_ffn_ln_gamma", "L0_ffn_ln_beta", "L0_ffn_W1",
        "L0_ffn_b1", "L0_ffn_W2", "L0_ffn_b2", "L0_ffn_edge_index", "L1_gnn_W_in", "L1_gnn_b_in", "L1_gnn_W_agg",
        "L1_gnn_W_self", "L1_gnn_b_hid", "L1_gnn_W_out", "L1_gnn_b_out", "L1_ffn_router_w", "L1_ffn_w1",
        "L1_ffn_b1", "L1_ffn_w2", "L1_ffn_b2"]


def kernel(**inputs):
    import numpy as _np
    import concourse.bacc as _bacc
    from concourse import mybir as _mybir
    from concourse.bass_utils import run_bass_kernel_spmd as _run

    nc = _bacc.Bacc("TRN2", target_bir_lowering=False, num_devices=1)
    arrays, args = {}, []
    for name in _INS:
        a = _np.asarray(inputs[name])
        if name == "L1_ffn_router_w":
            a = a.T
        a = _np.ascontiguousarray(a)
        arrays[f"in_{name}"] = a
        args.append(nc.dram_tensor(f"in_{name}", a.shape, _mybir.dt.from_np(a.dtype), kind="ExternalInput").ap())
    out = nc.dram_tensor("out_0", (N, D), _mybir.dt.float32, kind="ExternalOutput").ap()
    build_model(nc, *args, out)
    r = _run(nc, [arrays], core_ids=[0])
    return r.results[0]["out_0"]
```

```python
import numpy as np
import concourse.bass as bass
from concourse import mybir
from contextlib import ExitStack, contextmanager

FP32 = mybir.dt.float32
F32R = mybir.dt.float32r
I32 = mybir.dt.int32
ALU = mybir.AluOpType
ACT = mybir.ActivationFunctionType
AX = mybir.AxisListType.X
RMAX = bass.bass_isa.ReduceOp.max

N, D = 3125, 256
P, T = 125, 25
G, J = 5, 5
HEADS = 4
E1 = 53125
C1 = 416
Q = 4
B1 = C1 // Q
C1P = C1 + 2 * Q
E2 = 32768
C2 = E2 // 128
B2 = C2 // Q
C2P = C2 + 3 * Q
PAD = N
CW = 450
NG = 7
CC = CW * NG
CELLS = (N + 1) * CC
ROWS = N + 1
KQ = 5
MSG = 260
TAB = 264
TRASH_MARK = 1024.0
NOW = 2
LATER = (Q - NOW) * B1
BESIDE = 2
BEFORE = 52
AFTER = LATER - BEFORE - BESIDE * B2
assert BEFORE % 4 == 0 and AFTER % 4 == 0 and BESIDE == 2
EXACT = 4096
HALF = CC // 2
MERGES = 2 * T


class Chain:

    def __init__(self, eng, sem):
        self.eng, self.sem, self.base, self.k = eng, sem, 0, 0

    def __call__(self, ins):
        self.need(self.mark(ins))

    def mark(self, ins):
        ins.then_inc(self.sem, 1)
        self.k += 1
        return self.k

    def need(self, k):
        self.eng.wait_ge(self.sem, self.base + k)

    @contextmanager
    def loop(self, turns, per):
        base, k = self.base, self.k
        with self.eng.Fori(0, turns) as i:
            self.base, self.k = base + (i * per + k), 0
            yield i
            assert self.k == per, (self.k, per)
        self.base, self.k = base, k + turns * per


def build_model(nc, x, src, dst, gat_W, gat_as, gat_ad, gat_b, rt_W, rt_as, rt_ad, rt_b, rt_gamma, rt_beta,
                f0_W1, f0_b1, f0_W2, f0_b2, rt_edges, gn_Win, gn_bin, gn_Wagg, gn_Wself, gn_bhid, gn_Wout,
                gn_bout, f1_router, f1_W1, f1_b1, f1_W2, f1_b2, out):
    ctx = ExitStack()
    with ctx:
        def sb(name, shape, dt=FP32):
            return ctx.enter_context(nc.sbuf_tensor(name, shape, dt))

        def shared(name, shape, *later):
            def aligned(n):
                return -(-n // 32) * 32

            def bytes_of(sh):
                return aligned(4 * int(np.prod(sh[1:])))

            size = max([bytes_of(shape)] + [sum(bytes_of(sh) for _, sh, _ in group) for group in later])
            with nc.sbuf_tensor(name, [shape[0], size // 4], FP32) as first:
                pass
            groups = []
            for n, group in enumerate(later):
                stack = ctx if n == len(later) - 1 else ExitStack()
                groups.append([stack.enter_context(nc.sbuf_tensor(k, sh, dt)) for k, sh, dt in group])
                rest = size - sum(bytes_of(sh) for _, sh, _ in group)
                if rest:
                    stack.enter_context(nc.sbuf_tensor(f"{name}_rest{n}", [shape[0], rest // 4], FP32))
                if stack is not ctx:
                    stack.close()
            return [first] + groups

        def sem(name):
            return ctx.enter_context(nc.semaphore(name))

        counts = [nc.dram_tensor(f"counts{k}", [CELLS + 128, 1], FP32).ap() for k in range(2)]
        sums = [nc.dram_tensor(f"sums{k}", [ROWS + 128, MSG], FP32).ap() for k in range(2)]
        tab_src = nc.dram_tensor("tab_src", [ROWS, TAB], FP32).ap()
        rt_src = nc.dram_tensor("rt_src", [N, 24], FP32).ap()

        X = sb("X", [P, T, D])
        BIG1, (Z_hi,), (XT_lo,) = shared("BIG1", [128, T * TAB], [("Z_hi", [P, T, D], F32R)], [("XT_lo", [128, 2, CC], F32R)])
        BIG2, piece, (hh1_all, W1_hi, W1_lo) = shared(
            "BIG2", [128, KQ * KQ * CW], [(f"piece{k}", [P, KQ, CW], F32R) for k in range(KQ)],
            [("hh1_all", [128, 4 * J * P], FP32), ("W1_hi", [128, 8 * 2 * D], F32R), ("W1_lo", [128, 8 * 2 * D], F32R)])
        XT_flat, (XT_hi,) = shared("XT", [128, 2 * CC], [("XT_hi", [128, 2, CC], F32R)])
        XT = XT_flat[:, 0:2 * CC].rearrange("p (k n) -> p k n", k=2)
        FW, (Z_lo, Wagg) = shared("FW", [128, 8192], [("Z_lo", [P, T, D], F32R), ("Wagg", [128, 3, 2, D], FP32)])
        RD = sb("RD", [128, CC])
        xn_s = sb("xn_s", [P, J, D])
        xT_s = sb("xT_s", [128, 2, 2, P])
        Wg = sb("Wg", [128, 2, D])
        W16 = sb("W16", [128, 2, 16])
        Wr = sb("Wr", [128, 2, 8])
        Win = Wout = Wg
        scaled = sb("scaled", [128, 2, CW])
        Wself = sb("Wself", [128, 2, D])
        row_as = sb("row_as", [P, D])
        row_ad = sb("row_ad", [P, D])
        row_b = sb("row_b", [P, D])
        row16 = sb("row16", [P, 5, 16])
        b2_rows = BIG1[0:8, 2 * CC:2 * CC + D]
        b1_T = sb("b1_T", [128, 16])
        bin_T = sb("bin_T", [128, 2])
        bhid_T = sb("bhid_T", [128, 3, 2])
        ident = sb("ident", [128, 128])
        ones = sb("ones", [128, 128])
        lower = sb("lower", [128, 128])
        dupw = sb("dupw", [128, 128])
        tie = sb("tie", [128, 8, 8])
        iota_i = sb("iota_i", [128, P], I32)
        iota_f = sb("iota_f", [128, P])
        middle = sb("middle", [128, 8])
        pidx_i = sb("pidx_i", [128, 3], I32)
        pidx_f = sb("pidx_f", [128, 3])
        lane = pidx_f[:, 2:3]
        flag = sb("flag", [128, 8], I32)
        stats = sb("stats", [P, T, 6])
        ln = sb("ln", [P, 8, T])
        small = sb("small", [P, 10, T, HEADS])
        amax = sb("amax", [P, 2, HEADS])
        s16 = sb("s16", [P, 3, T, 16])
        tab2 = sb("tab2", [P, T, 24])
        uv = sb("uv", [P, T, 8])
        gates = sb("gates", [P, T, 8])
        e_src2 = sb("e_src2", [128, C2P], I32)
        e_dst2 = sb("e_dst2", [128, C2P], I32)
        xt_flat = XT[:, :, :].rearrange("p k n -> p (k n)")

        def column(k, dt=FP32):
            first = k * C1P if k < 7 else CC + (k - 7) * C1P
            part = xt_flat[:, first:first + C1P]
            return part if dt == FP32 else part.bitcast(dt)

        e_src, e_dst = column(0, I32), column(1, I32)
        src_f, dst_f, key_f, off_row, off_cell, dst_p, dst_t, div_f = (column(k) for k in range(2, 10))
        div_i = column(10, I32)
        tab = BIG1[0:P, 0:T * TAB].rearrange("p (t c) -> p t c", c=TAB)
        tab_h = tab[:, :, 0:MSG].rearrange("p t (h c) -> p t h c", c=65)

        def carve(big, at, shape):
            size = int(np.prod(shape))
            names = "abcd"[:len(shape)]
            view = big[:, at:at + size].rearrange(
                f"p ({' '.join(names)}) -> p {' '.join(names)}", **dict(zip(names, shape)))
            return view, at + size

        at = 0
        gath, at = carve(BIG2, at, [2, Q, TAB])
        same, at = carve(BIG2, at, [2, Q, 128])
        msg, at = carve(BIG2, at, [2, Q, MSG])
        msum, at = carve(BIG2, at, [2, Q, MSG])
        same_cell, at = carve(BIG2, at, [Q, 128])
        diag, at = carve(BIG2, at, [2, Q, 128])
        owner, at = carve(BIG2, at, [Q, 128])
        picked, at = carve(BIG2, at, [Q, T, 8])
        onet, at = carve(BIG2, at, [2, Q, T])
        earlier, _ = carve(FW, 0, [Q, 128])
        far, _ = carve(FW, Q * 128, [Q, 128])
        assert at <= KQ * KQ * CW
        slot_i = sb("slot_i", [128, 2, 3, Q], I32)
        slot_f = sb("slot_f", [128, 2, 6, Q])
        kept = sb("kept", [128, 2, (Q - NOW) * B1])
        late_i = sb("late_i", [128, 2, BESIDE], I32)
        late_f = sb("late_f", [128, 2, BESIDE])
        wgt = sb("wgt", [128, 2, Q, HEADS])
        uve = sb("uve", [128, Q, 8])
        sums_sb = BIG2[0:P, 0:T * MSG].rearrange("p (t h c) -> p t h c", h=HEADS, c=65)
        sums1_sb = FW[0:P, 0:T * MSG]
        at = 0
        gath2, at = carve(BIG1, at, [2, Q, 24])
        onep, at = carve(BIG1, at, [2, Q, P])
        msg2, at = carve(BIG1, at, [2, Q, 20])
        spread, at = carve(BIG1, at, [2, Q, T, 20])
        pd, at = carve(BIG1, at, [C2P])
        td, at = carve(BIG1, at, [C2P])
        dd, at = carve(BIG1, at, [C2P])
        halves, at = carve(BIG1, at, [C2P])
        e_half = halves.bitcast(I32)
        assert at <= T * TAB
        hh, at = carve(BIG2, 0, [2, 4, J * P])
        merge_b = [BIG2[0:P, at + k * HALF:at + (k + 1) * HALF] for k in range(2)]
        gates_T = [place[0:8, first:first + N].rearrange("e (t p) -> e t p", p=P) for place, first in ((BIG1, CC), (RD, 0))]
        ranks = [(BIG1[0:P, 0:T * 64], BIG1[0:P, T * 64:2 * T * 64]), (RD[0:P, 0:T * 64], hh1_all[0:P, 0:T * 64])]
        hh1 = hh1_all[:, :].rearrange("p (u m n) -> p u m n", u=2, m=2)
        hidden = (hh, hh1)
        merge_a = [BIG1[0:P, k * HALF:(k + 1) * HALF] for k in range(2)]
        assert at + 2 * HALF <= KQ * KQ * CW and 2 * HALF <= CC
        zrow = RD[:, :]

        bank = [ctx.enter_context(nc.psum_tensor(f"bank{k}", [128, 512], FP32)) for k in range(8)]

        ld_x = sem("ld_x")
        ld_gat = sem("ld_gat")
        ld_edges = sem("ld_edges")
        ld_rt = sem("ld_rt")
        ld_gn = sem("ld_gn")
        ld_f0 = sem("ld_f0")
        ld_f1 = sem("ld_f1")
        z_mem = sem("z_mem")
        z_sums = sem("z_sums")
        z_counts = [sem(f"z_counts{k}") for k in range(2)]
        late_idx = sem("late_idx")
        consts = sem("consts")
        consts2 = sem("consts2")
        idx_mem = sem("idx_mem")
        idx_dve = sem("idx_dve")
        dve_chain = sem("dve_chain")
        ln_var = sem("ln_var")
        ln_std = sem("ln_std")
        NORM = [{k: sem(f"{k}_{i}") for k in ("xn", "tr", "xT", "h", "hev")} for i in range(4)]
        mx = sem("mx")
        mxr = sem("mxr")
        f_in = sem("f_in")
        f_out = sem("f_out")
        tab_rdy = sem("tab_rdy")
        tab_st = sem("tab_st")
        gidx = sem("gidx")
        gat_s = [sem(f"gathered{s}") for s in range(2)]
        diag_rdy = sem("diag_rdy")
        bc_rdy = sem("bc_rdy")
        prep = sem("prep")
        compared = sem("compared")
        edges_done = sem("edges_done")
        msg_rdy = sem("msg_rdy")
        agg_rdy = sem("agg_rdy")
        msum_rdy = sem("msum_rdy")
        row_sc = [sem(f"row_sc{k}") for k in range(2)]
        cell_sc = [sem(f"cell_sc{k}") for k in range(2)]
        own_rdy = sem("own_rdy")
        far_rdy = sem("far_rdy")
        pick_mm = sem("pick_mm")
        pick_done = sem("pick_done")
        diag2_rdy = sem("diag2_rdy")
        bc2_rdy = sem("bc2_rdy")
        own2_rdy = sem("own2_rdy")
        pick2_mm = sem("pick2_mm")
        pick2_done = sem("pick2_done")
        mg_ld = [sem(f"mg_ld{k}") for k in range(2)]
        mg_st = [sem(f"mg_st{k}") for k in range(2)]
        mg_sum = sem("mg_sum")
        mg_row = sem("mg_row")
        sc_done = sem("sc_done")
        ld_sums = [sem(f"ld_sums{g}") for g in range(G)]
        sums_free = sem("sums_free")
        rt_tab_rdy = sem("rt_tab_rdy")
        rt_tab_st = sem("rt_tab_st")
        gidx2 = sem("gidx2")
        gat2_s = [sem(f"gathered2_{s}") for s in range(2)]
        spread_rdy = sem("spread_rdy")
        spread_used = sem("spread_used")
        rt_agg = sem("rt_agg")
        pc_ld = [sem(f"pc_ld{k}") for k in range(KQ)]
        pc_free = sem("pc_free")
        deg_mm = sem("deg_mm")
        deg_ev = sem("deg_ev")
        rd_done = sem("rd_done")
        EX = [{k: sem(f"{k}_e{i}") for k in ("up", "act", "dn", "acc", "gates", "gates_T", "bias", "added")} for i in range(2)]
        gate_rdy = sem("gate_rdy")
        gate1_rdy = sem("gate1_rdy")
        f0_done = sem("f0_done")
        in_mm = sem("in_mm")
        in_ev = sem("in_ev")
        z_mm = sem("z_mm")
        z_ev = sem("z_ev")
        ld_win = sem("ld_win")
        ld_bout = sem("ld_bout")
        bout_in = sem("bout_in")
        w1_split = sem("w1_split")
        x_lo = sem("x_lo")
        ld_wout = sem("ld_wout")
        ld_wself = sem("ld_wself")
        z_hi = sem("z_hi")
        ag_mm = sem("ag_mm")
        ag_read = sem("ag_read")
        gn_mm = sem("gn_mm")
        gn_sum = sem("gn_sum")
        gn_rel = sem("gn_rel")
        o_mm = sem("o_mm")
        o_acc = sem("o_acc")
        all_done = sem("all_done")
        stored = sem("stored")
        pool_steps = sem("pool_steps")
        pe_steps = sem("pe_steps")
        sp_steps = sem("sp_steps")

        COUNTED = [16 * (1 + NOW * B1 + LATER // 2), 16 * (1 + LATER // 2)]
        LD_GN = 16 * (3 + 3)
        LD_F1 = 16 * (16 + 2)
        LD_F0 = 16 * 10

        block = ctx.enter_context(nc.Block())

        def free(n, j):
            return n + (2 if j == 0 else 1)

        @block.sync
        def _(sp):
            sp.dma_start(X[:, :, :], x.rearrange("(p t) d -> p t d", t=T)).then_inc(ld_x, 16)
            sp.wait_ge(idx_mem, 2)
            for e, a in ((e_src, src), (e_dst, dst)):
                sp.dma_start(e[0:127, 0:C1], a[0:127 * C1].rearrange("(p c) -> p c", c=C1)).then_inc(ld_edges, 16)
                sp.dma_start(e[127:128, 0:E1 - 127 * C1], a[127 * C1:E1].rearrange("(o c) -> o c", o=1)).then_inc(ld_edges, 16)
            wk = "(k p) n -> p k n"
            sp.dma_start(Wg[:, :, :], gat_W.rearrange(wk, p=128)).then_inc(ld_gat, 16)
            sp.dma_start(row_as[:, :], gat_as.rearrange("h c -> (h c)").partition_broadcast(P)).then_inc(ld_gat, 16)
            sp.dma_start(row_ad[:, :], gat_ad.rearrange("h c -> (h c)").partition_broadcast(P)).then_inc(ld_gat, 16)
            sp.dma_start(row_b[:, :], gat_b.partition_broadcast(P)).then_inc(ld_gat, 16)
            sp.wait_ge(z_mem, 1)
            for k in range(2):
                sv = sums[k][0:N, :].rearrange("(p t) c -> p (t c)", t=T)
                for a in range(0, T * MSG, CC):
                    b = min(a + CC, T * MSG)
                    sp.dma_start(sv[:, a:b], zrow[0:P, 0:b - a]).then_inc(z_sums, 16)
                sp.dma_start(sums[k][N:N + 129, :].rearrange("(a b) c -> a (b c)", b=3), zrow[0:43, 0:3 * MSG]).then_inc(z_sums, 16)
            sp.dma_start(tab_src[N:N + 1, :], zrow[0:1, 0:TAB]).then_inc(z_sums, 16)

            def clear_rest(k):
                sp.dma_start(counts[k][N * CC:N * CC + CC + 128, 0].rearrange("(o n) -> o n", n=149), zrow[0:22, 0:149]).then_inc(z_counts[k], 16)

            cv = counts[0][0:N * CC, 0].rearrange("(p t n) -> p t n", t=T, n=CC)
            for t in range(T):
                sp.dma_start(cv[:, t, :], zrow[0:P, :]).then_inc(z_counts[0], 16)
            clear_rest(0)
            sp.dma_start(e_src2[:, 0:C2], rt_edges[0, :].rearrange("(p c) -> p c", c=C2)).then_inc(ld_rt, 16)
            sp.dma_start(e_dst2[:, 0:C2], rt_edges[1, :].rearrange("(p c) -> p c", c=C2)).then_inc(ld_rt, 16)
            sp.dma_start(W16[:, :, :], rt_W.rearrange(wk, p=128)).then_inc(ld_rt, 16)
            for k, a in enumerate((rt_as, rt_ad)):
                sp.dma_start(row16[:, k, :], a.rearrange("h c -> (h c)").partition_broadcast(P)).then_inc(ld_rt, 16)
            for k, a in enumerate((rt_b, rt_gamma, rt_beta)):
                sp.dma_start(row16[:, 2 + k, :], a.partition_broadcast(P)).then_inc(ld_rt, 16)
            f0w1 = FW[:, 0:4096].rearrange("p (e k n) -> p e k n", e=4, k=2)
            f0w2 = FW[:, 4096:8192].rearrange("p (e k n) -> p e k n", e=4, k=4)
            sp.dma_start(Wr[:, :, :], f1_router.rearrange(wk, p=128)).then_inc(ld_gn, 16)
            with nc.allow_non_contiguous_dma(reason="biases, a few hundred elements"):
                sp.dma_start(b1_T[:, :].unsqueeze(2), f0_b1.rearrange("e (m p) -> p (e m)", p=128).unsqueeze(2)).then_inc(ld_f0, 16)
                sp.dma_start(bin_T[:, :].unsqueeze(2), gn_bin.rearrange("(m p) -> p m", p=128).unsqueeze(2)).then_inc(ld_gn, 16)
                sp.dma_start(bhid_T[:, :, :].rearrange("p l m -> p (l m)").unsqueeze(2), gn_bhid.rearrange("l (m p) -> p (l m)", p=128).unsqueeze(2)).then_inc(ld_gn, 16)
            sp.wait_ge(tab_rdy, 1)
            sp.dma_start(tab_src[0:N, :].rearrange("(p t) c -> p t c", t=T), tab).then_inc(tab_st, 16)
            halves_of = counts[1][0:N * CC, 0].rearrange("(p m n) -> p m n", m=2 * T, n=HALF)
            with sp.Fori(0, 2 * T) as i:
                sp.wait_ge(prep, i * 2 + 1)
                sp.dma_start(halves_of[:, bass.ds(i, 1), :].rearrange("p o n -> p (o n)"), zrow[0:P, 0:HALF]).then_inc(z_counts[1], 16)
            clear_rest(1)
            for k in range(2):
                sp.wait_ge(row_sc[k], 16 * (2 * B1 + k))
            for s in range(2):
                sp.wait_ge(gat_s[s], 64 * (B1 // 2 + 1))
            sp.wait_ge(edges_done, 1)
            sp.wait_ge(pick_mm, B1 + 1)
            for g in range(G):
                for k, to in enumerate((BIG2[0:P, 0:T * MSG], sums1_sb)):
                    sp.dma_start(to.rearrange("p (t c) -> p t c", c=MSG)[:, g * J:g * J + J, :],
                                 sums[k][0:N, :].rearrange("(p t) c -> p t c", t=T)[:, g * J:g * J + J, :]).then_inc(ld_sums[g], 16)
            sp.wait_ge(rt_tab_rdy, 1)
            sp.dma_start(rt_src.rearrange("(p t) c -> p t c", t=T), tab2[:, :, :]).then_inc(rt_tab_st, 16)
            cells = counts[0][0:N * CC, 0].rearrange("(p k n) -> p k n", k=T, n=CC)

            def stream(q, g):
                for k in range(KQ):
                    if k < KQ - 1:
                        sp.wait_ge(pc_free, q * (KQ - 1) + (k + 1))
                    else:
                        sp.wait_ge(ag_mm, q + 1)
                    sp.dma_start(piece[k][:, :, :].bitcast(FP32), cells[:, KQ * k:KQ * k + KQ, bass.ds(g * CW, CW)]).then_inc(pc_ld[k], 16)

            sp.wait_ge(rt_agg, 2)
            for e in range(4):
                sp.dma_start(f0w1[:, e, :, :], f0_W1[e, :, :].rearrange(wk, p=128)).then_inc(ld_f0, 16)
                sp.dma_start(f0w2[:, e, :, :], f0_W2[e, :, :].rearrange(wk, p=128)).then_inc(ld_f0, 16)
            sp.dma_start(b2_rows[0:4, :], f0_b2).then_inc(ld_f0, 16)
            for s in range(2):
                sp.wait_ge(gat2_s[s], 64 * (B2 // 2 + 2 - s))
            sp.wait_ge(gate_rdy, 1)
            for k in range(2):
                sp.wait_ge(cell_sc[k], COUNTED[k])
                sp.sem_inc(mg_st[k], 16)
            parts = [c[0:N * CC, 0].rearrange("(p m n) -> p m n", m=MERGES, n=HALF) for c in counts]
            per = MERGES // G
            with sp.Fori(0, G) as g:
                def fetch(i):
                    sp.wait_ge(mg_st[i % 2], g * (8 * per) + 16 * (i // 2 + 1))
                    sp.sem_inc(sp_steps, 1)
                    sp.wait_ge(mg_row, g * per + (i + 1))
                    for a, c in ((merge_a, 0), (merge_b, 1)):
                        sp.dma_start(a[i % 2], parts[c][:, bass.ds(g * per + i, 1), :].rearrange("p o n -> p (o n)")).then_inc(mg_ld[i % 2], 16)

                def put(i):
                    sp.wait_ge(mg_sum, g * per + (i + 1))
                    sp.dma_start(parts[0][:, bass.ds(g * per + i, 1), :].rearrange("p o n -> p (o n)"), merge_a[i % 2]).then_inc(mg_st[i % 2], 16)

                fetch(0)
                for i in range(1, per):
                    fetch(i)
                    put(i - 1)
                put(per - 1)
            sp.wait_ge(f0_done, 1)
            f1w1 = FW[:, 0:4096].rearrange("p (e k n) -> p e k n", e=8, k=2)
            f1w2 = FW[:, 4096:8192].rearrange("p (e k n) -> p e k n", e=8, k=2)
            sp.dma_start(row_b[:, :], gn_bout.partition_broadcast(P)).then_inc(ld_bout, 16)
            with nc.allow_non_contiguous_dma(reason="biases, a few hundred elements"):
                sp.dma_start(b1_T[:, :].unsqueeze(2), f1_b1.rearrange("e (m p) -> p (e m)", p=128).unsqueeze(2)).then_inc(ld_f1, 16)
            for k in range(2):
                sp.wait_ge(mg_st[k], 16 * (T + 1))
            sp.sem_inc(gn_mm, 1)
            with sp.Fori(0, 3) as l:
                sp.wait_ge(gn_mm, l * NG + 1)
                sp.dma_start(Wself[:, :, :], gn_Wself[bass.ds(l, 1), :, :].rearrange("o (k p) n -> p (o k) n", p=128)).then_inc(ld_wself, 16)
                with sp.Fori(0, NG) as g:
                    stream(l * NG + g, g)
            sp.dma_start(Wout[:, :, :], gn_Wout.rearrange(wk, p=128)).then_inc(ld_wout, 16)
            sp.wait_ge(gn_mm, 3 * NG + 1)
            for e in range(8):
                sp.dma_start(f1w1[:, e, :, :], f1_W1[e, :, :].rearrange(wk, p=128)).then_inc(ld_f1, 16)
                sp.dma_start(f1w2[:, e, :, :], f1_W2[e, :, :].rearrange(wk, p=128)).then_inc(ld_f1, 16)
            sp.dma_start(b2_rows[:, :], f1_b2).then_inc(ld_f1, 16)
            sp.wait_ge(all_done, 1)
            sp.dma_start(out.rearrange("(p t) d -> p t d", t=T), X[:, :, :]).then_inc(stored, 16)
            sp.wait_ge(stored, 16)

        @block.gpsimd
        def _(pool):
            pool.memset(e_src, PAD).then_inc(idx_mem, 1)
            pool.memset(e_dst, PAD).then_inc(idx_mem, 1)
            pool.memset(zrow, 0.0).then_inc(z_mem, 1)
            pool.memset(ident[:, :], 0.0).then_inc(consts, 1)
            pool.memset(ones[:, :], 1.0).then_inc(consts, 1)
            pool.memset(tie[:, :, :], 1.0).then_inc(consts, 1)
            pool.memset(e_src2[:, C2:C2P], 0).then_inc(consts, 1)
            pool.memset(e_dst2[:, C2:C2P], 0).then_inc(consts, 1)
            pool.memset(XT[:, :, N:CC], 0.0).then_inc(consts, 1)
            pool.wait_ge(consts, 6)
            pool.affine_select(out=ident[:, :], in_=ident[:, :], compare_op=ALU.not_equal, fill=1.0, base=0,
                               pattern=[[-1, 128]], channel_multiplier=1).then_inc(consts, 1)
            pool.affine_select(out=lower[:, :], in_=ones[:, :], compare_op=ALU.is_gt, fill=0.0, base=0,
                               pattern=[[-1, 128]], channel_multiplier=1).then_inc(consts, 1)
            pool.affine_select(out=tie[:, :, :], in_=tie[:, :, :], compare_op=ALU.is_gt, fill=0.0, base=0,
                               pattern=[[1, 8], [-1, 8]], channel_multiplier=0).then_inc(consts, 1)
            pool.iota(iota_i[:, :], pattern=[[1, P]], base=0, channel_multiplier=0).then_inc(consts, 1)
            pool.iota(pidx_i[:, 0:1], pattern=[[0, 1]], base=ROWS, channel_multiplier=1).then_inc(consts, 1)
            pool.iota(pidx_i[:, 1:2], pattern=[[0, 1]], base=CELLS, channel_multiplier=1).then_inc(consts, 1)

            pool.iota(pidx_i[:, 2:3], pattern=[[0, 1]], base=0, channel_multiplier=1).then_inc(consts, 1)

            pool.wait_ge(mx, 1)
            pool.partition_all_reduce(amax[:, 1, :], amax[:, 0, :], P, RMAX).then_inc(mxr, 1)

            def gather(s, j, table, buf, done):
                pool.indirect_dma_start(
                    out=buf[:, s, j, :], out_offset=None, in_=table,
                    in_offset=bass.IndirectOffsetOnAxis(ap=slot_i[:, s, 0, j:j + 1], axis=0)).then_inc(done[s], 16)

            first = (tab_src, gath, gat_s)
            pool.wait_ge(tab_st, 16)
            pool.wait_ge(z_sums, 16 * 9)
            for s in range(2):
                pool.wait_ge(gidx, s + 1)
                for j in range(Q):
                    gather(s, j, *first)
            pool.wait_ge(z_counts[0], 16 * (T + 1))

            def ahead(k, rows, cells):
                if rows:
                    pool.dma_start(sums[k][ROWS:ROWS + 1, :], zrow[0:1, 0:MSG]).then_inc(row_sc[k], 16)
                if cells:
                    pool.dma_start(counts[k][CELLS:CELLS + 128, 0].rearrange("(o n) -> o n", o=1), zrow[0:1, 0:128]).then_inc(cell_sc[k], 16)

            def count(k, cell, number):
                pool.indirect_dma_start(
                    out=counts[k], out_offset=bass.IndirectOffsetOnAxis(ap=cell, axis=0),
                    in_=number, in_offset=None, compute_op=ALU.add).then_inc(cell_sc[k], 16)

            pool.sem_inc(sc_done, 1)
            ahead(0, False, True)
            ahead(1, True, False)
            with pool.Fori(0, B1 // 2) as it:
                for s in range(2):
                    b = it * 2 + s
                    pool.wait_ge(gidx, b + 3)
                    pool.wait_ge(prep, b + 1)
                    pool.wait_ge(msum_rdy, b + 3)
                    pool.wait_ge(cell_sc[0], b * 32 + 16)
                    pool.sem_inc(pool_steps, 1)
                    for j in range(Q):
                        pool.indirect_dma_start(
                            out=sums[j % 2], out_offset=bass.IndirectOffsetOnAxis(ap=slot_i[:, s, 1, j:j + 1], axis=0),
                            in_=msum[:, s, j, :], in_offset=None, compute_op=ALU.add).then_inc(row_sc[j % 2], 16)
                        if j % 2 == 0:
                            count(0, slot_i[:, s, 2, j // 2:j // 2 + 1], slot_f[:, s, 0, j // 2:j // 2 + 1])
                        gather(s, j, *first)
                        pool.wait_ge(row_sc[(j + 1) % 2], b * 32 + 16 * (j // 2 + 1))
                        if j == 1:
                            pool.wait_ge(cell_sc[0], b * 32 + 32)
                        pool.sem_inc(pool_steps, 1)
                        if j == 0:
                            pool.sem_inc(sc_done, 1)
            for s in range(2):
                pool.wait_ge(gat_s[s], 64 * (B1 // 2 + 1))

            pool.wait_ge(z_counts[1], 16 * (2 * T + 1))
            ahead(1, False, True)
            pool.wait_ge(edges_done, 1)
            late_base = [16 * (1 + NOW * B1), 16]

            def fetch_late(s, m, n):
                pool.tensor_copy(late_i[:, s, 0:n], kept[:, 0, bass.ds(m, n)])
                pool.tensor_copy(late_f[:, s, 0:n], kept[:, 1, bass.ds(m, n)]).then_inc(late_idx, 1)

            def late_fetched(turn):
                pool.wait_ge(late_idx, turn + 1)

            def count_late(s, i, k, earlier):
                pool.wait_ge(cell_sc[k], earlier * 16 + late_base[k])
                pool.sem_inc(pool_steps, 1)
                count(k, late_i[:, s, i:i + 1], late_f[:, s, i:i + 1])

            def late_pairs(m, n):
                with pool.Fori(0, n // 4) as it:
                    for s in range(2):
                        fetch_late(s, it * 4 + (m + 2 * s), 2)
                        late_fetched(it * 2 + (m // 2 + s))
                        for i in range(2):
                            count_late(s, i, i, it * 2 + (m // 2 + s))

            late_pairs(0, BEFORE)

            pool.wait_ge(mx, 2)
            pool.partition_all_reduce(amax[:, 1, :], amax[:, 0, :], P, RMAX).then_inc(mxr, 1)
            second = (rt_src, gath2, gat2_s)
            pool.wait_ge(rt_tab_st, 16)
            for b in range(3):
                pool.wait_ge(gidx2, b + 1)
                for j in range(Q):
                    gather(b % 2, j, *second)
            with pool.Fori(0, B2 // 2) as it:
                for s in range(2):
                    pool.wait_ge(gidx2, it * 2 + s + 4)
                    pool.sem_inc(pool_steps, 1)
                    fetch_late(s, it * (2 * BESIDE) + (BEFORE + BESIDE * s), BESIDE)
                    for j in range(Q // 2):
                        gather(1 - s, j, *second)
                    turn = it * 2 + (s + BEFORE // 2)
                    late_fetched(turn)
                    count_late(s, 0, 0, turn)
                    count_late(s, 1, 1, turn)
                    for j in range(Q // 2, Q):
                        gather(1 - s, j, *second)
            for s in range(2):
                pool.wait_ge(gat2_s[s], 64 * (B2 // 2 + 2 - s))

            late_pairs(BEFORE + BESIDE * B2, AFTER)

            pool.sem_inc(mg_row, 2)
            with pool.Fori(0, MERGES // 2) as it:
                for i in range(2):
                    pool.wait_ge(mg_ld[i], it * 32 + 32)
                    part = RD[0:P, i * HALF:(i + 1) * HALF]
                    pool.tensor_tensor(merge_a[i], merge_a[i], merge_b[i], ALU.add).then_inc(mg_sum, 1)
                    pool.wait_ge(mg_sum, it * 2 + (i + 1))
                    pool.tensor_tensor(part, part, merge_a[i], ALU.add).then_inc(mg_row, 1)
            pool.wait_ge(ld_bout, 16)
            pool.wait_ge(rd_done, 1)
            pool.tensor_tensor(X[:, :, :], X[:, :, :], row_b[:, :].unsqueeze(1).to_broadcast([P, T, D]), ALU.add).then_inc(bout_in, 1)

            pool.sem_inc(x_lo, 2)
            tmajor_hi, tmajor_lo = (x[:, :, 0:N].rearrange("p k (t n) -> p k t n", n=P) for x in (XT_hi, XT_lo))
            pool.wait_ge(ld_f1, LD_F1)
            pool.tensor_copy(W1_hi[:, :], FW[:, 0:4096]).then_inc(w1_split, 1)
            pool.wait_ge(w1_split, 1)
            pool.tensor_tensor(W1_lo[:, :], FW[:, 0:4096], W1_hi[:, :].bitcast(FP32), ALU.subtract).then_inc(w1_split, 1)
            with pool.Fori(0, G) as g:
                for j in range(J):
                    n = g * J + j
                    pool.wait_ge(NORM[3]["xT"], n + 3)
                    pool.tensor_tensor(tmajor_lo[:, :, n, :], xT_s[:, j % 2, :, :], tmajor_hi[:, :, n, :].bitcast(FP32), ALU.subtract).then_inc(x_lo, 1)

        @block.tensor
        def _(pe):
            mm = pe.matmul
            pe.wait_ge(consts, 13)

            def tiles(i, product=None, done=None):
                s = NORM[i]
                pe.sem_inc(s["tr"], 5)
                if product:
                    pe.sem_inc(s["h"], 2)
                with pe.Fori(0, G) as g:
                    def turn(j):
                        n = g * J + j
                        pe.wait_ge(s["xn"], n + 1)
                        pe.wait_ge(s["xT"], free(n, j))
                        for k in range(2):
                            last = pe.transpose(bank[j % 2][:, k * P:(k + 1) * P], xn_s[:, j, k * 128:(k + 1) * 128], ident[0:P, 0:P])
                        last.then_inc(s["tr"], 1)

                    def multiply(j):
                        n = g * J + j
                        pe.wait_ge(s["xT"], n + 3)
                        pe.wait_ge(s["hev"], free(n, j))
                        product(j).then_inc(s["h"], 1)

                    for j in range(J):
                        turn(j)
                        if product and j:
                            multiply(j - 1)
                    if product:
                        multiply(J - 1)

            def with_weights(w, width):
                def product(j):
                    for k in range(2):
                        last = mm(bank[2 + j % 2][0:P, 0:width], xT_s[:, j % 2, k, :], w[:, k, :], start=k == 0, stop=k == 1)
                    return last
                return product

            pe.wait_ge(ld_gat, 64)
            tiles(0, with_weights(Wg, D))

            def spread_numbers(banks):
                for k, bk in banks:
                    last = mm(bank[bk][:, :], ones[:, :], diag[:, k, :, :].rearrange("p q n -> p (q n)"), start=True, stop=True)
                return last

            def pick(b0):
                for j in range(Q):
                    last = mm(bank[b0 + j // 2][:, (j % 2) * T * 8:(j % 2 + 1) * T * 8], owner[0:P, j, :],
                              uv[:, :, :].rearrange("p t c -> p (t c)"), start=True, stop=True)
                return last

            rows = ((0, 0), (1, 1))
            pe.sem_inc(agg_rdy, 1)
            pe.wait_ge(diag_rdy, 1)
            spread_numbers(rows).then_inc(bc_rdy, 1)
            pe.wait_ge(own_rdy, 1)
            pick(6).then_inc(pick_mm, 1)
            pe.wait_ge(diag_rdy, 2)
            pe.wait_ge(compared, 1)
            pe.wait_ge(far_rdy, 1)
            spread_numbers(rows).then_inc(bc_rdy, 1)
            with pe.Fori(0, B1 // 2) as it:
                for s in range(2):
                    b = it * 2 + s
                    pe.wait_ge(diag_rdy, b + 3)
                    pe.wait_ge(compared, b + 2)
                    pe.wait_ge(far_rdy, b + 2)
                    spread_numbers(rows).then_inc(bc_rdy, 1)
                    pe.wait_ge(own_rdy, b + 2)
                    pe.wait_ge(pick_done, b + 1)
                    pick(6).then_inc(pick_mm, 1)
                    pe.wait_ge(msg_rdy, b + 1)
                    pe.wait_ge(msum_rdy, b + 2)
                    for j in range(Q):
                        last = mm(bank[2 + j][:, 0:MSG], same[:, s, j, :], msg[:, s, j, :], start=True, stop=True)
                    last.then_inc(agg_rdy, 1)

            pe.wait_ge(ld_rt, 128)
            tiles(1, with_weights(W16, 16))

            for_router = bank[0]
            zero_l, zero_r = RD[:, 0:P], RD[:, 0:T * 20]
            pe.sem_inc(spread_used, 2)
            pe.wait_ge(rt_tab_rdy, 1)
            mm(for_router[0:P, 0:T * 20], zero_l, zero_r, start=True, stop=False, skip_group_check=True).then_inc(rt_agg, 1)
            rows2 = ((0, 1),)
            pe.wait_ge(diag2_rdy, 1)
            spread_numbers(rows2).then_inc(bc2_rdy, 1)
            pe.wait_ge(own2_rdy, 1)
            pick(2).then_inc(pick2_mm, 1)
            for b in (1, 2):
                pe.wait_ge(diag2_rdy, b + 1)
                pe.wait_ge(own2_rdy, b)
                spread_numbers(rows2).then_inc(bc2_rdy, 1)
            pe.wait_ge(pick2_done, 1)
            pick(2).then_inc(pick2_mm, 1)
            with pe.Fori(0, B2 // 2) as it:
                for s in range(2):
                    b = it * 2 + s
                    pe.wait_ge(diag2_rdy, b + 4)
                    pe.wait_ge(own2_rdy, b + 3)
                    spread_numbers(rows2).then_inc(bc2_rdy, 1)
                    pe.wait_ge(pick2_done, b + 2)
                    pick(2).then_inc(pick2_mm, 1)
                    pe.wait_ge(spread_rdy, b + 1)
                    for j in range(Q):
                        last = mm(for_router[0:P, 0:T * 20], onep[:, s, j, :],
                                  spread[:, s, j, :, :].rearrange("p t c -> p (t c)"), start=False, stop=False, skip_group_check=True)
                    last.then_inc(spread_used, 1)
            mm(for_router[0:P, 0:T * 20], zero_l, zero_r, start=False, stop=True, skip_group_check=True).then_inc(rt_agg, 1)

            def experts(i, n_e, n_m, products, w2):
                s = EX[i]
                for t in range(T):
                    last = pe.transpose(bank[t // 4][0:n_e, (t % 4) * P:(t % 4 + 1) * P], gates[:, t, 0:n_e], ident[0:P, 0:P])
                    if t % 4 == 3 or t == T - 1:
                        last.then_inc(s["gates"], 1)
                pe.wait_ge(s["gates_T"], -(-T // 4))
                for h in range(-(-T // 2)):
                    pe.wait_ge(s["added"], h + 1)
                    for t in range(2 * h, min(2 * h + 2, T)):
                        last = mm(bank[4 + h % 2][0:P, (t % 2) * D:(t % 2 + 1) * D], gates_T[i][0:n_e, t, :], b2_rows[0:n_e, :], start=True, stop=True)
                    last.then_inc(s["bias"], 1)
                pe.wait_ge(s["added"], -(-T // 2) + 2)
                with pe.Fori(0, G) as g:
                    def up(e):
                        for m in range(n_m):
                            c = e * n_m + m
                            a = 2 * (c % 2)
                            pe.wait_ge(s["act"], g * (n_e * n_m) + (c + 1))
                            for lo, width, bk in ((0, 3 * P, a), (3 * P, 2 * P, a + 1)):
                                width += width % 2
                                terms = [(w, x, k) for w, x in products for k in range(2)]
                                for n, (w, x, k) in enumerate(terms):
                                    last = mm(bank[bk][:, 0:width], w[:, e, k, m * 128:(m + 1) * 128],
                                              x[:, k, bass.ds(g * (J * P) + lo, width)], start=n == 0, stop=n == len(terms) - 1)
                            last.then_inc(s["up"], 1)

                    def down(e):
                        pe.wait_ge(s["act"], g * (n_e * n_m) + ((e + 1) * n_m + 2))
                        for j in range(J):
                            c = e * J + j
                            pe.wait_ge(s["acc"], g * (n_e * J) + (c + 1))
                            for m in range(n_m):
                                last = mm(bank[4 + c % 2][0:P, 0:D], hidden[i][:, e % 2, m, j * P:(j + 1) * P], w2[:, e, m, :],
                                          start=m == 0, stop=m == n_m - 1)
                            last.then_inc(s["dn"], 1)

                    up(0)
                    for e in range(n_e):
                        if e + 1 < n_e:
                            up(e + 1)
                        down(e)

            pe.wait_ge(ld_f0, LD_F0)
            pe.wait_ge(gate_rdy, 1)
            experts(0, 4, 4, [(FW[:, 0:4096].rearrange("p (e k n) -> p e k n", e=4, k=2), XT)],
                    FW[:, 4096:8192].rearrange("p (e k n) -> p e k n", e=4, k=4))

            pe.wait_ge(ld_gn, LD_GN)
            pe.wait_ge(ld_win, 16)
            tiles(2)
            pe.wait_ge(NORM[2]["xT"], T + 2)
            with pe.Fori(0, NG) as g:
                pe.wait_ge(in_ev, g + 1)
                for f in range(2):
                    for k in range(2):
                        last = mm(bank[2 + f][:, 0:CW], Win[:, k, f * 128:(f + 1) * 128], XT[:, k, bass.ds(g * CW, CW)], start=k == 0, stop=k == 1)
                last.then_inc(in_mm, 1)
            pe.wait_ge(in_ev, NG + 1)

            pe.sem_inc(pc_free, KQ - 1)
            pe.sem_inc(ag_mm, 1)
            pe.wait_ge(mg_row, MERGES + 2)
            with pe.Fori(0, NG) as g:
                pe.wait_ge(deg_ev, g + 1)
                mm(bank[7][:, 0:CW], ones[0:P, :], RD[0:P, bass.ds(g * CW, CW)], start=True, stop=True).then_inc(deg_mm, 1)

            def tile_cols(k, t):
                return XT[:, k, 0:N].rearrange("p (a t) -> p t a", t=T)[:, t, :]

            pe.wait_ge(rd_done, 1)
            largest = pe.value_load(flag[0:1, 0:1])
            with pe.Fori(0, 3) as l:
                pe.wait_ge(gn_rel, l * NG + 1)
                for t in range(T):
                    pe.wait_ge(z_ev, l * T + free(t, t))
                    for k in range(2):
                        last = mm(bank[t % 2][0:P, 0:D], tile_cols(k, t), Wagg[:, bass.ds(l, 1), k, :].rearrange("p o n -> p (o n)"), start=k == 0, stop=k == 1)
                    last.then_inc(z_mm, 1)
                pe.wait_ge(z_ev, l * T + (T + 2))
                pe.wait_ge(ld_wself, l * 16 + 16)
                pe.sem_inc(pe_steps, 1)
                with pe.Fori(0, NG) as g:
                    q = l * NG + g

                    def aggregate(dt):
                        for k in range(KQ):
                            pe.wait_ge(pc_ld[k], q * 16 + 16)
                            for r in range(KQ):
                                t = KQ * k + r
                                for f in range(2):
                                    for z in (Z_hi, Z_lo):
                                        last = mm(bank[4 + f][:, 0:CW], z[:, t, f * 128:(f + 1) * 128].bitcast(dt), piece[k][:, r, :].bitcast(dt),
                                                  start=t == 0 and z is Z_hi, stop=t == T - 1 and z is Z_lo)
                            last.then_inc(pc_free if k < KQ - 1 else ag_mm, 1)

                    pe.wait_ge(ag_read, q + 1)
                    pe.sem_inc(pe_steps, 1)
                    with pe.If(largest < EXACT):
                        aggregate(F32R)
                    with pe.If(largest >= EXACT):
                        aggregate(FP32)
                    pe.wait_ge(gn_sum, q + 1)
                    for f in range(2):
                        for k in range(2):
                            last = mm(bank[6 + f][:, 0:CW], Wself[:, k, f * 128:(f + 1) * 128], XT[:, k, bass.ds(g * CW, CW)], start=k == 0, stop=k == 1)
                    last.then_inc(gn_mm, 1)
            pe.wait_ge(gn_rel, 3 * NG + 1)
            pe.wait_ge(ld_wout, 16)
            for t in range(T):
                pe.wait_ge(o_acc, free(t, t))
                for k in range(2):
                    last = mm(bank[t % 2][0:P, 0:D], tile_cols(k, t), Wout[:, k, :], start=k == 0, stop=k == 1)
                last.then_inc(o_mm, 1)

            tiles(3, with_weights(Wr, 8))
            pe.wait_ge(ld_f1, LD_F1)
            pe.wait_ge(gate1_rdy, 1)
            pe.wait_ge(w1_split, 2)
            pe.wait_ge(x_lo, T + 2)
            w1_hi, w1_lo = (w[:, :].rearrange("p (e k n) -> p e k n", e=8, k=2) for w in (W1_hi, W1_lo))
            experts(1, 8, 2, [(w1_hi, XT_hi), (w1_hi, XT_lo), (w1_lo, XT_hi)],
                    FW[:, 4096:8192].rearrange("p (e k n) -> p e k n", e=8, k=2))

        @block.scalar
        def _(act):
            fn = act.activation

            def root(i):
                act.wait_ge(ln_var, i + 1)
                fn(ln[:, 3, :], ln[:, 2, :], ACT.Sqrt).then_inc(ln_std, 1)

            def tiles(i, wide=None, store=None, also=None):
                s = NORM[i]
                act.sem_inc(s["xT"], 2)
                if store:
                    act.sem_inc(s["hev"], 2)
                with act.Fori(0, G) as g:
                    def copy(j):
                        n = g * J + j
                        act.wait_ge(s["tr"], n + 6)
                        if store:
                            act.wait_ge(s["h"], free(n, j))
                        if also:
                            act.wait_ge(also, free(n, j))
                        got = bank[j % 2][:, 0:2 * P].rearrange("p (k n) -> p k n", k=2)
                        if wide:
                            last = fn(wide(n), got, ACT.Copy)
                        if store:
                            last = fn(xT_s[:, j % 2, :, :], got, ACT.Copy)
                        last.then_inc(s["xT"], 1)

                    def take(j):
                        n = g * J + j
                        act.wait_ge(s["h"], n + 3)
                        store(j, n).then_inc(s["hev"], 1)

                    for j in range(J):
                        copy(j)
                        if store and j:
                            take(j - 1)
                    if store:
                        take(J - 1)

            root(0)
            tiles(0, store=lambda j, n: fn(tab_h[:, n, :, 0:64], bank[2 + j % 2][0:P, 0:D].rearrange("p (h c) -> p h c", h=HEADS), ACT.Copy))

            def factors():
                for k, scale in ((4, 0.8), (5, 0.2), (6, 0.8), (7, -0.8)):
                    source = small[:, 2 if k < 6 else 3 if k == 6 else 8, :, :]
                    last = fn(small[:, k, :, :], source, ACT.Exp, scale=scale)
                last.then_inc(f_out, 1)

            act.wait_ge(f_in, 1)
            factors()

            act.sem_inc(msum_rdy, 2)

            def diagonals(b, numbers, ready):
                for k, a in enumerate(numbers):
                    for j in range(Q):
                        last = fn(diag[:, k, j, :], ident[:, :], ACT.Copy, scale=a[:, bass.ds(b * Q + j, 1)] if not isinstance(b, int) else a[:, b * Q + j:b * Q + j + 1])
                last.then_inc(ready, 1)

            act.wait_ge(idx_dve, 1)
            act.wait_ge(consts, 13)
            act.wait_ge(consts2, 1)
            numbers1 = (dst_f, key_f)

            def distances():
                fn(far[0:P, :, :].rearrange("p q n -> p (q n)"), bank[0][0:P, :], ACT.Abs, bias=middle[0:P, 0:1]).then_inc(far_rdy, 1)

            diagonals(0, numbers1, diag_rdy)
            act.wait_ge(bc_rdy, 1)
            distances()
            diagonals(1, numbers1, diag_rdy)
            act.wait_ge(bc_rdy, 2)
            act.wait_ge(own_rdy, 1)
            distances()
            with act.Fori(0, B1 // 2) as it:
                for s in range(2):
                    b = it * 2 + s
                    act.wait_ge(bc_rdy, b + 2)
                    diagonals(b + 2, numbers1, diag_rdy)
                    act.wait_ge(bc_rdy, b + 3)
                    act.wait_ge(own_rdy, b + 2)
                    distances()
                    act.wait_ge(agg_rdy, b + 2)
                    act.wait_ge(sc_done, b + 1)
                    for j in range(Q):
                        last = fn(msum[:, s, j, :], bank[2 + j][:, 0:MSG], ACT.Copy)
                    last.then_inc(msum_rdy, 1)

            root(1)
            tmajor = XT[:, :, 0:N].rearrange("p k (t n) -> p k t n", n=P)
            tiles(1, wide=lambda n: tmajor[:, :, n, :],
                  store=lambda j, n: fn(s16[:, 0, n, :], bank[2 + j % 2][0:P, 0:16], ACT.Copy))
            act.wait_ge(f_in, 2)
            factors()
            act.wait_ge(rt_tab_rdy, 1)
            diagonals(0, (pd,), diag2_rdy)
            for b in (1, 2):
                act.wait_ge(bc2_rdy, b)
                diagonals(b, (pd,), diag2_rdy)
            with act.Fori(0, B2 // 2) as it:
                for s in range(2):
                    act.wait_ge(bc2_rdy, it * 2 + s + 3)
                    diagonals(it * 2 + s + 3, (pd,), diag2_rdy)
            act.wait_ge(ln_var, 3)
            fn(ln[:, 3, :], ln[:, 2, :], ACT.Sqrt).then_inc(ln_std, 1)
            act.wait_ge(f_in, 3)
            fn(small[:, 1, :, :], small[:, 1, :, :], ACT.Exp).then_inc(f_out, 1)

            def experts(i, n_e, n_m):
                s = EX[i]
                for k in range(-(-T // 4)):
                    n = min(4, T - 4 * k)
                    act.wait_ge(s["gates"], k + 1)
                    fn(gates_T[i][0:n_e, 4 * k:4 * k + n, :].rearrange("e t p -> e (t p)"), bank[k][0:n_e, 0:n * P], ACT.Copy).then_inc(s["gates_T"], 1)
                act.sem_inc(s["act"], 2)
                with act.Fori(0, G) as g:
                    for e in range(n_e):
                        u = e % 2
                        for m in range(n_m):
                            c = e * n_m + m
                            a = 2 * (c % 2)
                            act.wait_ge(s["up"], g * (n_e * n_m) + (c + 1))
                            for lo, width, bk in ((0, 3 * P, a), (3 * P, 2 * P, a + 1)):
                                last = fn(hidden[i][:, u, m, lo:lo + width], bank[bk][:, 0:width], ACT.Gelu, bias=b1_T[:, c:c + 1])
                            last.then_inc(s["act"], 1)

            act.wait_ge(gate_rdy, 1)
            act.wait_ge(ld_f0, LD_F0)
            experts(0, 4, 4)

            act.wait_ge(f0_done, 1)
            act.dma_start(Win[:, :, :], gn_Win.rearrange("(k p) n -> p k n", p=128)).then_inc(ld_win, 16)
            for l in range(3):
                act.dma_start(Wagg[:, l, :, :], gn_Wagg[l, :, :].rearrange("(k p) n -> p k n", p=128)).then_inc(ld_gn, 16)
            root(3)
            natural = XT[:, :, 0:N].rearrange("p k (n t) -> p k t n", t=T)
            act.wait_ge(EX[0]["dn"], G * 4 * J)
            tiles(2, wide=lambda n: natural[:, :, n, :])
            act.wait_ge(ld_gn, LD_GN)
            act.sem_inc(in_ev, 1)
            with act.Fori(0, NG) as g:
                act.wait_ge(in_mm, g + 1)
                for f in range(2):
                    last = fn(XT[:, f, bass.ds(g * CW, CW)], bank[2 + f][:, 0:CW], ACT.Identity, bias=bin_T[:, f:f + 1])
                last.then_inc(in_ev, 1)
            act.sem_inc(gn_rel, 1)
            for k in range(2):
                act.wait_ge(mg_st[k], 16 * (T + 1))
            with act.Fori(0, 3) as l:
                for t in range(T):
                    act.wait_ge(z_mm, l * T + (t + 1))
                    fn(Z_hi[:, t, :], bank[t % 2][0:P, 0:D], ACT.Copy).then_inc(z_hi, 1)
                with act.Fori(0, NG) as g:
                    act.wait_ge(gn_sum, l * NG + g + 2)
                    for f in range(2):
                        last = fn(XT[:, f, bass.ds(g * CW, CW)], XT[:, f, bass.ds(g * CW, CW)], ACT.Relu, bias=bhid_T[:, bass.ds(l, 1), f])
                    last.then_inc(gn_rel, 1)

            root(4)
            tmajor_hi = XT_hi[:, :, 0:N].rearrange("p k (t n) -> p k t n", n=P)
            tiles(3, wide=lambda n: tmajor_hi[:, :, n, :], also=x_lo,
                  store=lambda j, n: fn(gates[:, n, :], bank[2 + j % 2][0:P, 0:8], ACT.Copy))
            act.wait_ge(f_in, 4)
            fn(gates[:, :, :], gates[:, :, :], ACT.Exp).then_inc(f_out, 1)
            act.wait_ge(ld_f1, LD_F1)
            experts(1, 8, 2)

        @block.vector
        def _(dve):
            step = Chain(dve, dve_chain)
            tt, ts, stt = dve.tensor_tensor, dve.tensor_scalar, dve.scalar_tensor_tensor

            def cast(shape, a, axis):
                return a.unsqueeze(axis).to_broadcast(shape)

            dve.wait_ge(consts, 13)
            dve.tensor_copy(iota_f[:, :], iota_i[:, :])
            step(dve.tensor_copy(pidx_f[:, :], pidx_i[:, :]))
            ts(middle[:, 0:1], lane, -float(T), -float(T // 2), ALU.mult, ALU.add)
            ts(dupw[:, :], lower[:, :], TRASH_MARK, 1.0, ALU.mult, ALU.add).then_inc(consts2, 1)
            dve.wait_ge(ld_edges, 64)
            dve.tensor_copy(src_f, e_src)
            step(dve.tensor_copy(dst_f, e_dst))
            step(stt(key_f, dst_f, float(CC), src_f, ALU.mult, ALU.add))
            ts(off_row, dst_f, -1.0, pidx_f[:, 0:1], ALU.mult, ALU.add)
            step(ts(off_cell, key_f, -1.0, pidx_f[:, 1:2], ALU.mult, ALU.add))
            def divide(n, p, t, tmp, whole):
                step(ts(tmp, n, 0.5, 1.0 / T, ALU.add, ALU.mult))
                step(ts(tmp, tmp, -0.5, None, ALU.add))
                step(dve.tensor_copy(whole, tmp))
                step(dve.tensor_copy(p, whole))
                step(stt(t, p, -float(T), n, ALU.mult, ALU.add))
                step(ts(tmp, t, float(T), None, ALU.is_ge))
                step(tt(p, p, tmp, ALU.add))
                step(stt(t, tmp, -float(T), t, ALU.mult, ALU.add))

            divide(dst_f, dst_p, dst_t, div_f, div_i)
            dve.sem_inc(idx_dve, 1)

            def norm_stats(i, ready=False):
                if not ready:
                    with step.loop(G, 1) as g:
                        for j in range(J):
                            n = bass.ds(g * J + j, 1)
                            last = dve.bn_stats(stats[:, n, :].rearrange("p o c -> p (o c)"), X[:, n, :].rearrange("p o c -> p (o c)"))
                        step(last)
                me, ve, mo, vo = stats[:, :, 1], stats[:, :, 2], stats[:, :, 4], stats[:, :, 5]
                tt(ln[:, 0, :], me, mo, ALU.add)
                tt(ln[:, 1, :], me, mo, ALU.subtract)
                step(tt(ln[:, 2, :], ve, vo, ALU.add))
                step(tt(ln[:, 1, :], ln[:, 1, :], ln[:, 1, :], ALU.mult))
                ts(ln[:, 0, :], ln[:, 0, :], 0.5, None, ALU.mult)
                ts(ln[:, 1, :], ln[:, 1, :], 0.25, 1e-5, ALU.mult, ALU.add)
                step(ts(ln[:, 2, :], ln[:, 2, :], 1.0 / D, None, ALU.mult))
                tt(ln[:, 2, :], ln[:, 2, :], ln[:, 1, :], ALU.add).then_inc(ln_var, 1)
                rsqrt(i)

            def rsqrt(i):
                dve.wait_ge(ln_std, i + 1)
                step(dve.reciprocal(ln[:, 4, :], ln[:, 3, :]))
                step(tt(ln[:, 4, :], ln[:, 4, :], ln[:, 2, :], ALU.mult))
                step(tt(ln[:, 4, :], ln[:, 4, :], ln[:, 3, :], ALU.add))
                step(dve.reciprocal(ln[:, 4, :], ln[:, 4, :]))
                step(ts(ln[:, 5, :], ln[:, 4, :], 2.0, None, ALU.mult))

            def normalised(i, g):
                for j in range(J):
                    n = g * J + j
                    dve.wait_ge(NORM[i]["tr"], n + 1)
                    ts(xn_s[:, j, :], X[:, n, :], ln[:, 0, bass.ds(n, 1)], ln[:, 5, bass.ds(n, 1)],
                       ALU.subtract, ALU.mult).then_inc(NORM[i]["xn"], 1)

            def heads(k):
                return small[:, k, :, :]

            def factors(turn):
                dve.tensor_reduce(amax[:, 0, :], heads(0).rearrange("p t h -> p h t"), AX, ALU.max).then_inc(mx, 1)
                dve.wait_ge(mxr, turn)
                top = cast([P, T, HEADS], amax[:, 1, :], 1)
                tt(heads(2), heads(0), top, ALU.subtract)
                step(tt(heads(3), heads(1), top, ALU.add))
                step(ts(heads(8), heads(3), 0.0, None, ALU.max))
                ts(heads(3), heads(3), 0.0, None, ALU.min).then_inc(f_in, 1)
                dve.wait_ge(f_out, turn)
                dve.tensor_copy(uv[:, :, 0:4], heads(6))
                dve.tensor_copy(uv[:, :, 4:8], heads(7))
                step(tt(heads(9), heads(4), heads(6), ALU.mult))
                step(tt(heads(9), heads(9), heads(7), ALU.max))

            dve.wait_ge(ld_x, 16)
            norm_stats(0)
            dve.wait_ge(ld_gat, 64)
            att_scr = BIG2[0:P, 0:2 * D].rearrange("p (k n) -> p k n", k=2)
            with step.loop(G, 2 * J) as g:
                normalised(0, g)
                for j in range(J):
                    n = g * J + j
                    dve.wait_ge(NORM[0]["hev"], n + 3)
                    for k, row in enumerate((row_as, row_ad)):
                        last = tt(att_scr[:, k, :].rearrange("p (h c) -> p h c", h=HEADS), tab_h[:, n, :, 0:64],
                                  row[:, :].rearrange("p (h c) -> p h c", h=HEADS), ALU.mult)
                    step(last)
                    step(dve.tensor_reduce(small[:, 0:2, n, :], att_scr.rearrange("p k (h c) -> p k h c", c=64), AX, ALU.add))
            factors(1)
            dve.wait_ge(NORM[0]["hev"], T + 2)
            dve.tensor_copy(tab[:, :, MSG:TAB], heads(4))
            dve.tensor_copy(tab_h[:, :, :, 64], heads(5))
            part = tab_h[:, :, :, 0:64]
            step(tt(part, part, cast([P, T, HEADS, 64], heads(5), 3), ALU.mult))
            dve.sem_inc(tab_rdy, 1)

            def numbers(s, b, e, ready):
                cols = bass.ds(b * Q, Q) if not isinstance(b, int) else slice(b * Q, b * Q + Q)
                dve.tensor_copy(slot_i[:, s, 0, :], e[:, cols]).then_inc(ready, 1)

            def pick_product(b0, s):
                for h in range(2):
                    last = tt(picked[:, 2 * h:2 * h + 2, :, :], bank[b0 + h][:, 0:2 * T * 8].rearrange("p (q t c) -> p q t c", q=2, t=T),
                              cast([128, 2, T, 8], onet[:, s, 2 * h:2 * h + 2, :], 3), ALU.mult)
                return step.mark(last)

            def pick_sum():
                return step.mark(dve.tensor_reduce(uve[:, :, :], picked.rearrange("p q t c -> p q c t"), AX, ALU.add))

            def columns(b):
                return bass.ds(b * Q, Q) if not isinstance(b, int) else slice(b * Q, b * Q + Q)

            shape1 = [128, Q, 128]

            def compare_cells(b):
                dve.wait_ge(bc_rdy, b + 1)
                tt(same_cell, bank[1][:, :].rearrange("p (q n) -> p q n", q=Q), cast(shape1, key_f[:, columns(b)], 2), ALU.is_equal)

            def compare_rows(s, b):
                dve.wait_ge(far_rdy, b + 1)
                return step.mark(tt(same[:, s, :, :], bank[0][:, :].rearrange("p (q n) -> p q n", q=Q), cast(shape1, dst_f[:, columns(b)], 2), ALU.is_equal))

            def weigh(s):
                tt(earlier, same[:, s, :, :], cast(shape1, lower[:, :], 1), ALU.mult)
                return step.mark(tt(same_cell, same_cell, cast(shape1, dupw[:, :], 1), ALU.mult))

            def number(s):
                dve.tensor_reduce(slot_f[:, s, 1, :], earlier, AX, ALU.add)
                return step.mark(dve.tensor_reduce(slot_f[:, s, 4, :], same_cell, AX, ALU.add))

            def speak(s, b):
                stt(slot_f[:, s, 2, :], slot_f[:, s, 1, :], 0.0, off_row[:, columns(b)], ALU.is_gt, ALU.mult)
                return step.mark(stt(slot_f[:, s, 3, :], slot_f[:, s, 4, :], TRASH_MARK, off_cell[:, columns(b)], ALU.is_ge, ALU.mult))

            def own(s, b):
                ts(owner[0:P, :, :], far[0:P, :, :], float(T // 2) + 0.5, None, ALU.is_lt).then_inc(own_rdy, 1)
                tt(onet[:, s, :, :], cast([128, Q, T], iota_f[:, 0:T], 1), cast([128, Q, T], dst_t[:, columns(b)], 2), ALU.is_equal)

            def post(s, b):
                f = lambda k: slot_f[:, s, k, :]
                dve.wait_ge(sc_done, b + 1)
                dve.tensor_copy(f(0)[:, 0:NOW], f(4)[:, 0:NOW])
                dve.tensor_copy(kept[:, 1, bass.ds(b * NOW, NOW)], f(4)[:, NOW:Q])
                tt(kept[:, 0, bass.ds(b * NOW, NOW)], f(3)[:, NOW:Q], key_f[:, bass.ds(b * Q + NOW, NOW)], ALU.add)
                tt(slot_i[:, s, 1, :], f(2), dst_f[:, bass.ds(b * Q, Q)], ALU.add)
                tt(slot_i[:, s, 2, 0:NOW], f(3)[:, 0:NOW], key_f[:, bass.ds(b * Q, NOW)], ALU.add).then_inc(prep, 1)

            numbers(0, 0, e_src, gidx)
            numbers(1, 1, e_src, gidx)
            dve.wait_ge(consts2, 1)
            compare_cells(0)
            step.need(compare_rows(0, 0))
            dve.sem_inc(compared, 1)
            step.need(weigh(0))
            step.need(number(0))
            own(0, 0)
            step.need(speak(0, 0))
            dve.wait_ge(tab_st, 16)
            step(tt(tab_h, tab_h, cast([P, T, HEADS, 65], heads(9), 3), ALU.mult))
            with step.loop(B1 // 2, 16) as it:
                for s in range(2):
                    b = it * 2 + s
                    dve.wait_ge(pick_mm, b + 1)
                    got = pick_product(6, s)
                    compare_cells(b + 1)
                    step.need(got)
                    dve.sem_inc(pick_done, 1)
                    got = pick_sum()
                    dve.wait_ge(agg_rdy, b + 1)
                    cmp = compare_rows(1 - s, b + 1)
                    step.need(cmp)
                    dve.sem_inc(compared, 1)
                    cmp = weigh(1 - s)
                    step.need(got)
                    dve.wait_ge(gat_s[s], it * 64 + 64)
                    numbers(s, b + 2, e_src, gidx)
                    got = step.mark(tt(wgt[:, s, :, :], gath[:, s, :, MSG:TAB], uve[:, :, 0:4], ALU.mult))
                    step.need(cmp)
                    cmp = number(1 - s)
                    step.need(got)
                    got = step.mark(tt(wgt[:, s, :, :], wgt[:, s, :, :], uve[:, :, 4:8], ALU.max))
                    own(1 - s, b + 1)
                    step.need(got)
                    dve.wait_ge(msum_rdy, b + 1)
                    tt(msg[:, s, :, :].rearrange("p q (h c) -> p q h c", c=65),
                       gath[:, s, :, 0:MSG].rearrange("p q (h c) -> p q h c", c=65),
                       cast([128, Q, HEADS, 65], wgt[:, s, :, :], 3), ALU.mult).then_inc(msg_rdy, 1)
                    step.need(cmp)
                    cmp = speak(1 - s, b + 1)
                    post(s, b)
                    step.need(cmp)
            dve.sem_inc(edges_done, 1)
            for g in range(G):
                tiles = slice(g * J, g * J + J)
                cols = slice(g * J * MSG, (g + 1) * J * MSG)
                tot, scale = BIG2[0:P, cols], heads(5)[:, tiles, :]
                dve.wait_ge(ld_sums[g], 32)
                step(tt(tot, tot, sums1_sb[:, cols], ALU.add))
                step(tt(sums_sb[:, tiles], sums_sb[:, tiles], tab_h[:, tiles], ALU.add))
                step(ts(heads(4)[:, tiles, :], sums_sb[:, tiles, :, 64], 1e-30, None, ALU.max))
                step(dve.reciprocal(scale, heads(4)[:, tiles, :]))
                part = sums_sb[:, tiles, :, 0:64]
                step(tt(part, part, cast([P, J, HEADS, 64], scale, 3), ALU.mult))
                step(tt(part, part, cast([P, J, HEADS, 64], row_b[:, :].rearrange("p (h c) -> p h c", c=64), 1), ALU.add))
                res = X[:, tiles, :].rearrange("p t (h c) -> p t h c", c=64)
                step(stt(res, part, 0.0, res, ALU.max, ALU.add))
                for t in range(g * J, g * J + J):
                    last = dve.bn_stats(stats[:, t, :], X[:, t, :])
            step(last)
            dve.sem_inc(sums_free, 1)

            norm_stats(1, ready=True)
            with step.loop(G, 0) as g:
                normalised(1, g)
            dve.wait_ge(NORM[1]["hev"], T + 2)
            dve.wait_ge(ld_rt, 128)
            for k in range(2):
                step(tt(s16[:, 1, :, :], s16[:, 0, :, :], cast([P, T, 16], row16[:, k, :], 1), ALU.mult))
                step(dve.tensor_reduce(heads(k), s16[:, 1, :, :].rearrange("p t (h c) -> p t h c", c=4), AX, ALU.add))
            factors(2)
            own2 = tab2[:, :, 0:20].rearrange("p t (h c) -> p t h c", c=5)
            dve.tensor_copy(tab2[:, :, 20:24], heads(4))
            dve.tensor_copy(own2[:, :, :, 4], heads(5))
            step(tt(own2[:, :, :, 0:4], s16[:, 0, :, :].rearrange("p t (h c) -> p t h c", c=4), cast([P, T, HEADS, 4], heads(5), 3), ALU.mult))
            step(dve.tensor_copy(dd, e_dst2[:, :]))
            divide(dd, pd, td, halves, e_half)
            dve.sem_inc(rt_tab_rdy, 1)

            numbers(0, 0, e_src2, gidx2)
            numbers(1, 1, e_src2, gidx2)

            def own2_part(b):
                dve.wait_ge(bc2_rdy, b + 1)
                ts(owner[0:P, :, :], bank[1][0:P, :].rearrange("p (q n) -> p q n", q=Q), lane[0:P, 0:1], None, ALU.is_equal).then_inc(own2_rdy, 1)

            def own2_tile(s, b):
                return step.mark(tt(onet[:, s, :, :], cast([128, Q, T], iota_f[:, 0:T], 1), cast([128, Q, T], td[:, columns(b)], 2), ALU.is_equal))

            def message2(s):
                return step.mark(tt(msg2[:, s, :, :].rearrange("p q (h c) -> p q h c", c=5), gath2[:, s, :, 0:20].rearrange("p q (h c) -> p q h c", c=5),
                                    cast([128, Q, HEADS, 5], wgt[:, s, :, :], 3), ALU.mult))

            def weight_u(s):
                return step.mark(tt(wgt[:, s, :, :], gath2[:, s, :, 20:24], uve[:, :, 0:4], ALU.mult))

            def weight_v(s):
                return step.mark(tt(wgt[:, s, :, :], wgt[:, s, :, :], uve[:, :, 4:8], ALU.max))

            def spread_out(s, j):
                return tt(spread[:, s, j, :, :], cast([128, T, 20], onet[:, s, j, :], 2), cast([128, T, 20], msg2[:, s, j, :], 1), ALU.mult)

            own2_part(0)
            step.need(own2_tile(0, 0))
            dve.wait_ge(pick2_mm, 1)
            got = pick_product(2, 0)
            own2_part(1)
            step.need(got)
            dve.sem_inc(pick2_done, 1)
            step.need(pick_sum())
            dve.wait_ge(gat2_s[0], 64)
            step.need(weight_u(0))
            step.need(weight_v(0))
            step.need(message2(0))
            numbers(0, 2, e_src2, gidx2)
            step.need(own2_tile(1, 1))
            with step.loop(B2 // 2, 14) as it:
                for s in range(2):
                    b, o = it * 2 + s, 1 - s
                    dve.wait_ge(pick2_mm, b + 2)
                    got = pick_product(2, o)
                    own2_part(b + 2)
                    dve.wait_ge(spread_used, b + 1)
                    tt(onep[:, s, :, :], cast([128, Q, P], iota_f[:, :], 1), cast([128, Q, P], pd[:, columns(b)], 2), ALU.is_equal)
                    step.need(got)
                    dve.sem_inc(pick2_done, 1)
                    got = pick_sum()
                    spread_out(s, 0)
                    step.need(got)
                    dve.wait_ge(gat2_s[o], it * 64 + 64 * (1 + s))
                    got = weight_u(o)
                    spread_out(s, 1)
                    step.need(got)
                    got = weight_v(o)
                    spread_out(s, 2)
                    step.need(got)
                    message2(o)
                    numbers(o, b + 3, e_src2, gidx2)
                    step.need(step.mark(spread_out(s, 3)))
                    dve.sem_inc(spread_rdy, 1)
                    step.need(own2_tile(s, b + 2))
            dve.wait_ge(pick2_mm, B2 + 2)
            dve.wait_ge(rt_agg, 2)
            for s in range(2):
                dve.wait_ge(gat2_s[s], 64 * (B2 // 2 + 2 - s))
            got = bank[0][0:P, 0:T * 20].rearrange("p (t h c) -> p t h c", h=HEADS, c=5)
            step(tt(own2, own2, cast([P, T, HEADS, 5], heads(9), 3), ALU.mult))
            step(tt(own2, own2, got, ALU.add))
            step(ts(heads(4), own2[:, :, :, 4], 1e-30, None, ALU.max))
            step(dve.reciprocal(heads(5), heads(4)))
            agg, dev, sq = (s16[:, k, :, :] for k in range(3))
            step(tt(agg.rearrange("p t (h c) -> p t h c", c=4), own2[:, :, :, 0:4], cast([P, T, HEADS, 4], heads(5), 3), ALU.mult))
            step(tt(agg, agg, cast([P, T, 16], row16[:, 2, :], 1), ALU.add))
            step(dve.tensor_reduce(ln[:, 0, :], agg, AX, ALU.add))
            step(ts(ln[:, 0, :], ln[:, 0, :], 1.0 / 16, None, ALU.mult))
            step(tt(dev, agg, cast([P, T, 16], ln[:, 0, :], 2), ALU.subtract))
            step(tt(sq, dev, dev, ALU.mult))
            step(dve.tensor_reduce(ln[:, 1, :], sq, AX, ALU.add))
            ts(ln[:, 2, :], ln[:, 1, :], 1.0 / 16, 1e-5, ALU.mult, ALU.add).then_inc(ln_var, 1)
            rsqrt(2)
            step(tt(dev, dev, cast([P, T, 16], ln[:, 5, :], 2), ALU.mult))
            step(tt(dev, dev, cast([P, T, 16], row16[:, 3, :], 1), ALU.mult))
            step(tt(dev, dev, cast([P, T, 16], row16[:, 4, :], 1), ALU.add))
            step(dve.tensor_reduce(heads(0), dev.rearrange("p t (h e) -> p t e h", h=HEADS), AX, ALU.add))
            step(ts(heads(0), heads(0), 1.0 / HEADS, None, ALU.mult))

            def top_two(i, scores, n_e, sel):
                shape = [P, T, n_e, n_e]
                a = ranks[i][0][:, 0:T * n_e * n_e].rearrange("p (t e f) -> p t e f", e=n_e, f=n_e)
                b = ranks[i][1][:, 0:T * n_e * n_e].rearrange("p (t e f) -> p t e f", e=n_e, f=n_e)
                mine, other = cast(shape, scores, 3), cast(shape, scores, 2)
                tt(a, other, mine, ALU.is_gt)
                step(tt(b, other, mine, ALU.is_equal))
                for e in range(n_e):
                    last = tt(b[:, :, e, :], b[:, :, e, :], cast([P, T, n_e], tie[0:P, e, 0:n_e], 1), ALU.mult)
                step(last)
                step(tt(a, a, b, ALU.add))
                step(dve.tensor_reduce(sel, a, AX, ALU.add))
                step(ts(sel, sel, 2.0, None, ALU.is_lt))

            top_two(0, heads(0), 4, heads(2))
            step(dve.tensor_reduce(ln[:, 0, :], heads(0), AX, ALU.max))
            tt(heads(1), heads(0), cast([P, T, 4], ln[:, 0, :], 2), ALU.subtract).then_inc(f_in, 1)
            dve.wait_ge(f_out, 3)
            step(tt(heads(1), heads(1), heads(2), ALU.mult))
            step(dve.tensor_reduce(ln[:, 0, :], heads(1), AX, ALU.add))
            step(dve.reciprocal(ln[:, 0, :], ln[:, 0, :]))
            step(tt(gates[:, :, 0:4], heads(1), cast([P, T, 4], ln[:, 0, :], 2), ALU.mult))
            dve.sem_inc(gate_rdy, 1)

            def experts(i, n_e):
                s = EX[i]
                dve.sem_inc(s["acc"], 2)
                dve.sem_inc(s["added"], 2)
                for h in range(-(-T // 2)):
                    dve.wait_ge(s["bias"], h + 1)
                    n = min(2, T - 2 * h)
                    part = X[:, 2 * h:2 * h + n, :].rearrange("p t c -> p (t c)")
                    tt(part, part, bank[4 + h % 2][0:P, 0:n * D], ALU.add).then_inc(s["added"], 1)
                dve.wait_ge(s["added"], -(-T // 2) + 2)
                with step.loop(G, 0) as g:
                    for e in range(n_e):
                        for j in range(J):
                            c = e * J + j
                            n = g * J + j
                            dve.wait_ge(s["dn"], g * (n_e * J) + (c + 1))
                            if e:
                                dve.wait_ge(s["acc"], g * (n_e * J) + (c - J + 3))
                            stt(X[:, n, :], bank[4 + c % 2][0:P, 0:D], gates[:, n, e:e + 1], X[:, n, :], ALU.mult, ALU.add).then_inc(s["acc"], 1)
                dve.wait_ge(s["acc"], G * n_e * J + 2)

            dve.wait_ge(ld_f0, LD_F0)
            experts(0, 4)
            dve.sem_inc(f0_done, 1)
            norm_stats(3)
            with step.loop(G, 0) as g:
                normalised(2, g)
            dve.sem_inc(deg_ev, 1)
            with step.loop(NG, 1) as g:
                cols = RD[:, bass.ds(g * CW, CW)]
                dve.wait_ge(deg_mm, g + 1)
                step(ts(cols, bank[7][:, 0:CW], 1.0, None, ALU.max))
                dve.sem_inc(deg_ev, 1)
            step(dve.tensor_reduce(flag[:, 0:1], RD[:, :], AX, ALU.max))
            step(dve.reciprocal(RD[:, :], RD[:, :]))
            dve.sem_inc(rd_done, 1)

            dve.sem_inc(gn_sum, 1)
            dve.sem_inc(ag_read, 1)
            dve.sem_inc(z_ev, 2)
            with step.loop(3, NG) as l:
                for t in range(T):
                    dve.wait_ge(z_hi, l * T + (t + 1))
                    tt(Z_lo[:, t, :], bank[t % 2][0:P, 0:D], Z_hi[:, t, :].bitcast(FP32), ALU.subtract).then_inc(z_ev, 1)
                with step.loop(NG, 1) as g:
                    q = l * NG + g
                    cols = bass.ds(g * CW, CW)
                    dve.wait_ge(ag_mm, q + 2)
                    dve.wait_ge(gn_sum, q + 1)
                    for f in range(2):
                        last = tt(scaled[:, f, :], bank[4 + f][:, 0:CW], RD[:, cols], ALU.mult)
                    step(last)
                    dve.sem_inc(ag_read, 1)
                    dve.wait_ge(gn_mm, q + 2)
                    for f in range(2):
                        last = tt(XT[:, f, cols], scaled[:, f, :], bank[6 + f][:, 0:CW], ALU.add)
                    last.then_inc(gn_sum, 1)
            dve.sem_inc(o_acc, 2)
            dve.wait_ge(bout_in, 1)
            for t in range(T):
                dve.wait_ge(o_mm, t + 1)
                tt(X[:, t, :], bank[t % 2][0:P, 0:D], X[:, t, :], ALU.add).then_inc(o_acc, 1)
                if t:
                    dve.wait_ge(o_acc, t + 2)
                    dve.bn_stats(stats[:, t - 1, :], X[:, t - 1, :])
            dve.wait_ge(o_acc, T + 2)
            step(dve.bn_stats(stats[:, T - 1, :], X[:, T - 1, :]))

            norm_stats(4, ready=True)
            with step.loop(G, 1) as g:
                normalised(3, g)
                dve.wait_ge(NORM[3]["xn"], g * J + J)
                for j in range(J):
                    n = g * J + j
                    last = tt(X[:, n, :], X[:, n, :], xn_s[:, j, :], ALU.add)
                step(last)
            dve.wait_ge(NORM[3]["hev"], T + 2)
            g8 = gates[:, :, :]
            step(dve.tensor_reduce(ln[:, 0, :], g8, AX, ALU.max))
            tt(g8, g8, cast([P, T, 8], ln[:, 0, :], 2), ALU.subtract).then_inc(f_in, 1)
            dve.wait_ge(f_out, 4)
            step(dve.tensor_reduce(ln[:, 0, :], g8, AX, ALU.add))
            step(dve.reciprocal(ln[:, 0, :], ln[:, 0, :]))
            step(tt(g8, g8, cast([P, T, 8], ln[:, 0, :], 2), ALU.mult))
            top_two(1, g8, 8, uv[:, :, :])
            step(tt(g8, g8, uv[:, :, :], ALU.mult))
            step(dve.tensor_reduce(ln[:, 0, :], g8, AX, ALU.add))
            step(ts(ln[:, 0, :], ln[:, 0, :], 1e-12, None, ALU.max))
            step(dve.reciprocal(ln[:, 0, :], ln[:, 0, :]))
            step(tt(g8, g8, cast([P, T, 8], ln[:, 0, :], 2), ALU.mult))
            dve.sem_inc(gate1_rdy, 1)
            experts(1, 8)
            dve.sem_inc(all_done, 1)


_INS = ["x", "src", "dst", "L0_gnn_W", "L0_gnn_att_src", "L0_gnn_att_dst", "L0_gnn_bias", "L0_ffn_W_gat",
        "L0_ffn_att_src", "L0_ffn_att_dst", "L0_ffn_b_gat", "L0_ffn_ln_gamma", "L0_ffn_ln_beta", "L0_ffn_W1",
        "L0_ffn_b1", "L0_ffn_W2", "L0_ffn_b2", "L0_ffn_edge_index", "L1_gnn_W_in", "L1_gnn_b_in", "L1_gnn_W_agg",
        "L1_gnn_W_self", "L1_gnn_b_hid", "L1_gnn_W_out", "L1_gnn_b_out", "L1_ffn_router_w", "L1_ffn_w1",
        "L1_ffn_b1", "L1_ffn_w2", "L1_ffn_b2"]


def kernel(**inputs):
    import numpy as _np
    import concourse.bacc as _bacc
    from concourse import mybir as _mybir
    from concourse.bass_utils import run_bass_kernel_spmd as _run

    nc = _bacc.Bacc("TRN2", target_bir_lowering=False, num_devices=1)
    arrays, args = {}, []
    for name in _INS:
        a = _np.asarray(inputs[name])
        if name == "L1_ffn_router_w":
            a = a.T
        a = _np.ascontiguousarray(a)
        arrays[f"in_{name}"] = a
        args.append(nc.dram_tensor(f"in_{name}", a.shape, _mybir.dt.from_np(a.dtype), kind="ExternalInput").ap())
    out = nc.dram_tensor("out_0", (N, D), _mybir.dt.float32, kind="ExternalOutput").ap()
    build_model(nc, *args, out)
    r = _run(nc, [arrays], core_ids=[0])
    return r.results[0]["out_0"]
```
